# Optimizing a Trainium2 kernel written in Bass

```python
import numpy as np
import jax
import jax.numpy as jnp

def _softmax(x, axis=-1):
    return jax.nn.softmax(x, axis=axis)

def _gelu(x):
    return jax.nn.gelu(x, approximate=True)

def _silu(x):
    return jax.nn.silu(x)

def _sigmoid(x):
    return jax.nn.sigmoid(x)

def _layernorm(x, axis=-1, eps=1e-05):
    m = jnp.mean(x, axis=axis, keepdims=True)
    v = jnp.var(x, axis=axis, keepdims=True)
    return (x - m) / jnp.sqrt(v + eps)

def _scatter_add(tgt, idx, src, axis=0):
    return tgt.at[idx].add(src)

def _segment_sum(src, seg, n):
    return jax.ops.segment_sum(src, seg, n)
kernel_name = 'mk_xattn_seq_d2_seqx_r8_a7e1fd'

def setup_inputs(seed: int=0):
    np.random.seed(seed)
    _w = jnp.asarray

    def _rec_inputs():
        import jax
        import jax.numpy as jnp
        _rk = jax.random.key(seed)
        x = -0.0005146 + 1 * jax.random.normal(jax.random.fold_in(_rk, 1), (8, 256, 256), jnp.float32)
        _lenS = 256 - jax.random.randint(jax.random.fold_in(_rk, 7), (8,), 0, max(1, 256 // 4) + 1, jnp.int32)
        _lenS2 = 1601 - jax.random.randint(jax.random.fold_in(_rk, 8), (8,), 0, max(1, 1601 // 4) + 1, jnp.int32)
        _ctx_2048P = jax.random.normal(jax.random.fold_in(_rk, 11), (8, 16, 256), jnp.float32)
        _ctx_2048c = jax.random.dirichlet(jax.random.fold_in(_rk, 511), 0.3 * jnp.ones((16,), jnp.float32), (8, 1601))
        _ctx_2048t = jnp.einsum('bsk,bkd->bsd', _ctx_2048c, _ctx_2048P)
        _ctx_2048t = _ctx_2048t * jax.lax.rsqrt(jnp.mean(jnp.square(_ctx_2048t)) + 1e-12) * 0.953939
        ctx_2048 = -0.000392918 + 0.999932 * (_ctx_2048t + 0.3 * jax.random.normal(jax.random.fold_in(_rk, 611), (8, 1601, 256), jnp.float32))
        _validS = jnp.arange(256)[None, :] < _lenS[:, None]
        _validS2 = jnp.arange(1601)[None, :] < _lenS2[:, None]
        _causal = jnp.tril(jnp.ones((256, 256), dtype=bool))
        mask_BxS2_ik0 = jnp.where(jnp.broadcast_to(_validS2[:, :], (8, 1601)), 0, 1).astype(jnp.int32)
        mask_Bx1xSxS2_ff0 = jnp.where(jnp.ones((8, 1, 256, 1601), dtype=bool), 0.0, -1000000000.0).astype(jnp.float32)
        return (x, ctx_2048, mask_BxS2_ik0, mask_Bx1xSxS2_ff0)
    x, ctx_2048, mask_BxS2_ik0, mask_Bx1xSxS2_ff0 = _rec_inputs()

    def _L0_xattn_setup():
        import jax, jax.numpy as jnp
        import numpy as np
        B, P, K, H, NH = (4, 256, 32, 256, 16)
        DH = H // NH
        EPS = 1e-06

        def rmsnorm(x, w):
            var = jnp.mean(jnp.square(x), axis=-1, keepdims=True)
            return x * jax.lax.rsqrt(var + EPS) * w
        key = jax.random.key(seed)
        ks = jax.random.split(key, 12)
        s = 0.02
        return {'x': jax.random.normal(ks[0], (B, P, H), jnp.float32), 'latents': jax.random.normal(ks[1], (B, K, H), jnp.float32), 'attention_mask': jax.random.randint(ks[2], (B, P), 0, 2, jnp.int32), 'q_w': s * jax.random.normal(ks[3], (H, H), jnp.float32), 'q_b': jnp.zeros((H,), jnp.float32), 'kv_w': s * jax.random.normal(ks[4], (H, 2 * H), jnp.float32), 'kv_b': jnp.zeros((2 * H,), jnp.float32), 'out_w': s * jax.random.normal(ks[5], (H, H), jnp.float32), 'out_b': jnp.zeros((H,), jnp.float32), 'postnorm_w': jnp.ones((H,), jnp.float32), 'mlp_w1': s * jax.random.normal(ks[6], (H, 4 * H), jnp.float32), 'mlp_b1': jnp.zeros((4 * H,), jnp.float32), 'mlp_w2': s * jax.random.normal(ks[7], (4 * H, H), jnp.float32), 'mlp_b2': jnp.zeros((H,), jnp.float32)}
    _L0_xattn_all = _L0_xattn_setup()
    _L0_xattn_in = {k: v for k, v in _L0_xattn_all.items() if k in ('q_w', 'q_b', 'kv_w', 'kv_b', 'out_w', 'out_b', 'postnorm_w', 'mlp_w1', 'mlp_b1', 'mlp_w2', 'mlp_b2')}
    del _L0_xattn_all

    def _L1_xattn_setup():
        import jax, jax.numpy as jnp
        import numpy as np
        H = 256
        NH = 32
        KVH = 8
        HD = H // NH
        GROUPS = NH // KVH
        EPS = 1e-06
        B, L, S = (4, 128, 128)

        def _gqa_forward(hidden_state, encoder_hidden_state, encoder_attention_mask, Wq, bq, Wk, bk, Wv, bv, Wo, bo, gamma, beta):
            b, l, _ = hidden_state.shape
            s = encoder_hidden_state.shape[1]
            q = hidden_state @ Wq + bq
            k = encoder_hidden_state @ Wk + bk
            v = encoder_hidden_state @ Wv + bv
            q = q.reshape(b, l, KVH, GROUPS, HD).transpose(0, 2, 3, 1, 4)
            k = k.reshape(b, s, KVH, HD).transpose(0, 2, 1, 3)
            v = v.reshape(b, s, KVH, HD).transpose(0, 2, 1, 3)
            scale = 1.0 / jnp.sqrt(jnp.asarray(HD, q.dtype))
            scores = jnp.einsum('bkgld,bksd->bkgls', q, k) * scale
            scores = scores + encoder_attention_mask[:, :, None, :, :]
            attn = jax.nn.softmax(scores, axis=-1)
            out = jnp.einsum('bkgls,bksd->bkgld', attn, v)
            out = out.transpose(0, 3, 1, 2, 4).reshape(b, l, H)
            out = out @ Wo + bo
            x = out + hidden_state
            mu = jnp.mean(x, axis=-1, keepdims=True)
            var = jnp.var(x, axis=-1, keepdims=True)
            return (x - mu) * jax.lax.rsqrt(var + EPS) * gamma + beta
        key = jax.random.key(seed)
        ks = jax.random.split(key, 12)
        sd = 0.02
        return {'hidden_state': jax.random.normal(ks[0], (B, L, H), jnp.float32), 'encoder_hidden_state': jax.random.normal(ks[1], (B, S, H), jnp.float32), 'encoder_attention_mask': jnp.zeros((B, 1, L, S), jnp.float32), 'Wq': jax.random.normal(ks[2], (H, H), jnp.float32) * sd, 'bq': jnp.zeros((H,), jnp.float32), 'Wk': jax.random.normal(ks[3], (H, KVH * HD), jnp.float32) * sd, 'bk': jnp.zeros((KVH * HD,), jnp.float32), 'Wv': jax.random.normal(ks[4], (H, KVH * HD), jnp.float32) * sd, 'bv': jnp.zeros((KVH * HD,), jnp.float32), 'Wo': jax.random.normal(ks[5], (H, H), jnp.float32) * sd, 'bo': jnp.zeros((H,), jnp.float32), 'gamma': jnp.ones((H,), jnp.float32), 'beta': jnp.zeros((H,), jnp.float32)}
    _L1_xattn_all = _L1_xattn_setup()
    _L1_xattn_in = {k: v for k, v in _L1_xattn_all.items() if k in ('Wq', 'bq', 'Wk', 'bk', 'Wv', 'bv', 'Wo', 'bo', 'gamma', 'beta')}
    del _L1_xattn_all
    return {'x': x, 'ctx_2048': ctx_2048, 'mask_BxS2_ik0': mask_BxS2_ik0, 'mask_Bx1xSxS2_ff0': mask_Bx1xSxS2_ff0, 'L0_xattn_q_w': _L0_xattn_in['q_w'], 'L0_xattn_q_b': _L0_xattn_in['q_b'], 'L0_xattn_kv_w': _L0_xattn_in['kv_w'], 'L0_xattn_kv_b': _L0_xattn_in['kv_b'], 'L0_xattn_out_w': _L0_xattn_in['out_w'], 'L0_xattn_out_b': _L0_xattn_in['out_b'], 'L0_xattn_postnorm_w': _L0_xattn_in['postnorm_w'], 'L0_xattn_mlp_w1': _L0_xattn_in['mlp_w1'], 'L0_xattn_mlp_b1': _L0_xattn_in['mlp_b1'], 'L0_xattn_mlp_w2': _L0_xattn_in['mlp_w2'], 'L0_xattn_mlp_b2': _L0_xattn_in['mlp_b2'], 'L1_xattn_Wq': _L1_xattn_in['Wq'], 'L1_xattn_bq': _L1_xattn_in['bq'], 'L1_xattn_Wk': _L1_xattn_in['Wk'], 'L1_xattn_bk': _L1_xattn_in['bk'], 'L1_xattn_Wv': _L1_xattn_in['Wv'], 'L1_xattn_bv': _L1_xattn_in['bv'], 'L1_xattn_Wo': _L1_xattn_in['Wo'], 'L1_xattn_bo': _L1_xattn_in['bo'], 'L1_xattn_gamma': _L1_xattn_in['gamma'], 'L1_xattn_beta': _L1_xattn_in['beta']}

def reference(x, ctx_2048, mask_BxS2_ik0, mask_Bx1xSxS2_ff0, L0_xattn_q_w, L0_xattn_q_b, L0_xattn_kv_w, L0_xattn_kv_b, L0_xattn_out_w, L0_xattn_out_b, L0_xattn_postnorm_w, L0_xattn_mlp_w1, L0_xattn_mlp_b1, L0_xattn_mlp_w2, L0_xattn_mlp_b2, L1_xattn_Wq, L1_xattn_bq, L1_xattn_Wk, L1_xattn_bk, L1_xattn_Wv, L1_xattn_bv, L1_xattn_Wo, L1_xattn_bo, L1_xattn_gamma, L1_xattn_beta):
    import jax
    import jax.numpy as jnp

    def _L0_xattn_ref(x, latents, attention_mask, q_w, q_b, kv_w, kv_b, out_w, out_b, postnorm_w, mlp_w1, mlp_b1, mlp_w2, mlp_b2):
        import jax, jax.numpy as jnp
        import numpy as np
        B, P, K, H, NH = (4, 256, 32, 256, 16)
        DH = H // NH
        EPS = 1e-06

        def rmsnorm(x, w):
            var = jnp.mean(jnp.square(x), axis=-1, keepdims=True)
            return x * jax.lax.rsqrt(var + EPS) * w
        b, p, _ = x.shape
        k_len = latents.shape[1]
        residual = latents
        h = jnp.concatenate([x, latents], axis=1)
        q = (latents @ q_w + q_b).reshape(b, k_len, NH, DH)
        kv = (h @ kv_w + kv_b).reshape(b, p + k_len, NH, DH, 2)
        kmat, v = (kv[..., 0], kv[..., 1])
        attn = jnp.einsum('bkhd,bnhd->bhkn', q, kmat) / DH
        full_mask = jnp.concatenate([attention_mask.astype(bool), jnp.ones((b, k_len), bool)], axis=-1)
        attn = jnp.where(full_mask[:, None, None, :], attn, -jnp.inf)
        attn = jax.nn.softmax(attn.astype(jnp.float32), axis=-1).astype(q.dtype)
        attn_out = jnp.einsum('bhkn,bnhd->bkhd', attn, v).reshape(b, k_len, H)
        attn_out = attn_out @ out_w + out_b + residual
        out = rmsnorm(attn_out, postnorm_w)
        out = jax.nn.gelu(out @ mlp_w1 + mlp_b1) @ mlp_w2 + mlp_b2
        return out + residual

    def _L1_xattn_ref(hidden_state, encoder_hidden_state, encoder_attention_mask, Wq, bq, Wk, bk, Wv, bv, Wo, bo, gamma, beta):
        import jax, jax.numpy as jnp
        import numpy as np
        H = 256
        NH = 32
        KVH = 8
        HD = H // NH
        GROUPS = NH // KVH
        EPS = 1e-06
        B, L, S = (4, 128, 128)

        def _gqa_forward(hidden_state, encoder_hidden_state, encoder_attention_mask, Wq, bq, Wk, bk, Wv, bv, Wo, bo, gamma, beta):
            b, l, _ = hidden_state.shape
            s = encoder_hidden_state.shape[1]
            q = hidden_state @ Wq + bq
            k = encoder_hidden_state @ Wk + bk
            v = encoder_hidden_state @ Wv + bv
            q = q.reshape(b, l, KVH, GROUPS, HD).transpose(0, 2, 3, 1, 4)
            k = k.reshape(b, s, KVH, HD).transpose(0, 2, 1, 3)
            v = v.reshape(b, s, KVH, HD).transpose(0, 2, 1, 3)
            scale = 1.0 / jnp.sqrt(jnp.asarray(HD, q.dtype))
            scores = jnp.einsum('bkgld,bksd->bkgls', q, k) * scale
            scores = scores + encoder_attention_mask[:, :, None, :, :]
            attn = jax.nn.softmax(scores, axis=-1)
            out = jnp.einsum('bkgls,bksd->bkgld', attn, v)
            out = out.transpose(0, 3, 1, 2, 4).reshape(b, l, H)
            out = out @ Wo + bo
            x = out + hidden_state
            mu = jnp.mean(x, axis=-1, keepdims=True)
            var = jnp.var(x, axis=-1, keepdims=True)
            return (x - mu) * jax.lax.rsqrt(var + EPS) * gamma + beta
        return _gqa_forward(hidden_state, encoder_hidden_state, encoder_attention_mask, Wq, bq, Wk, bk, Wv, bv, Wo, bo, gamma, beta)
    x = _L0_xattn_ref(ctx_2048, x, mask_BxS2_ik0, L0_xattn_q_w, L0_xattn_q_b, L0_xattn_kv_w, L0_xattn_kv_b, L0_xattn_out_w, L0_xattn_out_b, L0_xattn_postnorm_w, L0_xattn_mlp_w1, L0_xattn_mlp_b1, L0_xattn_mlp_w2, L0_xattn_mlp_b2)
    x = _L1_xattn_ref(x, ctx_2048, mask_Bx1xSxS2_ff0, L1_xattn_Wq, L1_xattn_bq, L1_xattn_Wk, L1_xattn_bk, L1_xattn_Wv, L1_xattn_bv, L1_xattn_Wo, L1_xattn_bo, L1_xattn_gamma, L1_xattn_beta)
    return x

_drawn_inputs = setup_inputs


def setup_inputs(seed=0):
    import zlib

    import numpy as np

    out = dict(_drawn_inputs(seed))
    spreads = {'L0_xattn_q_b': (0.0, 0.8),
     'L0_xattn_kv_b': (0.0, 0.8),
     'L0_xattn_out_b': (0.0, 0.656),
     'L0_xattn_postnorm_w': (1.0, 0.6),
     'L0_xattn_mlp_b1': (0.0, 0.1),
     'L0_xattn_mlp_b2': (0.0, 0.1),
     'L1_xattn_bq': (0.0, 0.8),
     'L1_xattn_bk': (0.0, 0.8),
     'L1_xattn_bv': (0.0, 0.1),
     'L1_xattn_bo': (0.0, 0.1),
     'L1_xattn_gamma': (1.0, 0.2),
     'L1_xattn_beta': (0.0, 0.1)}
    factors = {'L0_xattn_q_w': 8.0,
     'L0_xattn_kv_w': 8.0,
     'L0_xattn_out_w': 8.0,
     'L1_xattn_Wq': 8.0,
     'L1_xattn_Wk': 8.0}
    for name, (base, spread) in spreads.items():
        noise = np.random.default_rng([zlib.crc32(name.encode()), seed]).standard_normal(out[name].shape)
        drawn = base * np.exp(spread * noise) if base else spread * noise
        out[name] = jnp.asarray(drawn.astype(out[name].dtype))
    for name, factor in factors.items():
        out[name] = (out[name] * factor).astype(out[name].dtype)
    return out
```

```python
from contextlib import ExitStack

import concourse.bass as bass
from concourse import mybir

F32 = mybir.dt.float32
BF16 = mybir.dt.bfloat16
I32 = mybir.dt.int32
ALU = mybir.AluOpType
ACT = mybir.ActivationFunctionType
AX = mybir.AxisListType

P = 128
B, SQ, H, SC = 8, 256, 256, 1601
HALVES = H // P
QB = SQ // P
F = 4 * H
EPS = 1e-6

NKB0 = -(-(SC + SQ) // P)
NKB1 = -(-SC // P)
K0, K1 = NKB0 * P, NKB1 * P
G0, G1 = 4, 8
D0, D1 = 16, 8
KV1 = H // 4
VW = H + KV1
NEG = -1.0e30

COMBOS = [(0, 0), (0, 1), (1, 0), (1, 1), (0, 2), (2, 0)]
EXTRA = 96
KROWS = 100


def each_batch(eng, body):
    body(0, True, False)
    with eng.Fori(1, B - 1) as b:
        body(b, False, False)
    body(B - 1, False, True)


def wait_at_least(eng, sem, b, per_batch, count):
    if isinstance(b, int):
        if b * per_batch + count > 0:
            eng.wait_ge(sem, b * per_batch + count)
    else:
        eng.wait_ge(sem, b * per_batch + count)


def project_inputs(nc, t, scratch):
    def items():
        out = []
        for o in range(HALVES):
            for c in range(0, K0, 512):
                out.append(("k0", o, c, min(512, K0 - c)))
        for c in range(0, K1, 512):
            out.append(("k1", 0, c, min(512, K1 - c)))
        for o in range(HALVES):
            out.append(("q0", o, SC, SQ))
        return out
    ITEMS = items()
    NI = len(ITEMS)
    PB = 4

    with ExitStack() as ctx:
        sb = lambda name, shape, dt: ctx.enter_context(nc.sbuf_tensor(name, shape, dt))
        sem = lambda name: ctx.enter_context(nc.semaphore(name))
        psum = ctx.enter_context(nc.psum_tensor("proj_psum", [P, 8, 512], F32))
        w_k0 = sb("w_k0", [P, HALVES, H], F32)
        w_q0 = sb("w_q0", [P, HALVES, H], F32)
        w_k1 = sb("w_k1", [P, HALVES, KV1], F32)
        w_v = sb("w_v", [P, HALVES, VW], F32)
        b_k0 = sb("b_k0", [P, HALVES], F32)
        b_q0 = sb("b_q0", [P, HALVES], F32)
        b_q0s = sb("b_q0s", [P, HALVES], F32)
        b_k1 = sb("b_k1", [KV1, 1], F32)
        b_v = sb("b_v", [P, VW], F32)
        hT = [sb(f"hT{i}", [P, HALVES, K0], F32) for i in range(2)]
        pc_k0 = [sb(f"pc_k0_{i}", [P, HALVES, 3, K0], BF16) for i in range(2)]
        pc_k1 = [sb(f"pc_k1_{i}", [KV1, 3, K1], BF16) for i in range(2)]
        pc_q0 = [sb(f"pc_q0_{i}", [P, HALVES, 3, SQ], BF16) for i in range(2)]
        vals = [sb(f"vals{i}", [P, NKB0, VW], F32) for i in range(2)]
        xf = sb("xf", [P, 4, 512], F32)
        r1 = sb("r1", [P, 2, 512], F32)
        mask_i = sb("mask_i", [B, SC], I32)
        mask_f = sb("mask_f", [B, SC], F32)
        bias0 = sb("bias0", [B, K0], BF16)
        bias1 = sb("bias1", [1, K1], BF16)

        weights_in = sem("proj_weights_in")
        hT_in = [sem(f"proj_hT_in{i}") for i in range(2)]
        pads_zero = sem("proj_pads_zero")
        item_psum = sem("proj_item_psum")
        item_read = sem("proj_item_read")
        val_psum = sem("proj_val_psum")
        val_read = sem("proj_val_read")
        piece_step = sem("proj_piece_step")
        bias_done = sem("proj_bias_done")
        qbias = sem("proj_qbias")
        stored = [sem(f"proj_stored{i}") for i in range(2)]
        bias_stored = sem("proj_bias_stored")
        STEPS = 4
        STORES = 5

        def rows(kind):
            return KV1 if kind == "k1" else P

        def piece(b, kind, o, pc, c, n):
            if kind == "k0":
                return pc_k0[b % 2][:, o, pc, c:c + n]
            if kind == "k1":
                return pc_k1[b % 2][:, pc, c:c + n]
            return pc_q0[b % 2][:, o, pc, :]

        with nc.Block() as block:
            @block.sync
            def _(sp):
                for dst, src in ((w_k0, t["kw0"]), (w_q0, t["qw0"]), (w_k1, t["kw1"])):
                    sp.dma_start(dst[:], src.rearrange("(i p) n -> p i n", p=P)).then_inc(weights_in, 16)
                sp.dma_start(w_v[:, :, 0:H], t["vw0"].rearrange("(i p) n -> p i n", p=P)).then_inc(weights_in, 16)
                sp.dma_start(w_v[:, :, H:VW], t["vw1"].rearrange("(i p) n -> p i n", p=P)).then_inc(weights_in, 16)
                sp.dma_start(b_k0[:], t["kb0"]).then_inc(weights_in, 16)
                sp.dma_start(b_q0[:], t["qb0"]).then_inc(weights_in, 16)
                sp.dma_start(b_k1[:], t["kb1"]).then_inc(weights_in, 16)
                sp.dma_start(b_v[:, 0:H], t["vb0"].rearrange("(a n) -> a n", a=1).to_broadcast([P, H])).then_inc(weights_in, 16)
                sp.dma_start(b_v[:, H:VW], t["vb1"].rearrange("(a n) -> a n", a=1).to_broadcast([P, KV1])).then_inc(weights_in, 16)
                sp.dma_start(mask_i[:], t["mask0"]).then_inc(weights_in, 16)

                def load(b):
                    if b >= 2:
                        sp.wait_ge(val_psum, (b - 1) * NKB0)
                        sp.wait_ge(item_psum, (b - 1) * NI)
                    for i in range(HALVES):
                        sp.dma_start(hT[b % 2][:, i, 0:SC], t["ctxT"][b, i * P:(i + 1) * P, :]).then_inc(hT_in[b % 2], 16)
                        sp.dma_start(hT[b % 2][:, i, SC:SC + SQ], t["xT"][b, i * P:(i + 1) * P, :]).then_inc(hT_in[b % 2], 16)
                load(0)
                load(1)
                for b in range(B):
                    sp.wait_ge(piece_step, (b + 1) * NI * STEPS)
                    sp.wait_ge(item_read, 2 * (b + 1) * NI)
                    sp.wait_ge(val_read, (b + 1) * NKB0)
                    sp.dma_start(scratch["kp0"][b], pc_k0[b % 2][:]).then_inc(stored[b % 2], 16)
                    sp.dma_start(scratch["kp1"][b], pc_k1[b % 2][:]).then_inc(stored[b % 2], 16)
                    sp.dma_start(scratch["qp0"][b], pc_q0[b % 2][:]).then_inc(stored[b % 2], 16)
                    sp.dma_start(scratch["v0"][b], vals[b % 2][:, :, 0:H]).then_inc(stored[b % 2], 16)
                    sp.dma_start(scratch["v1"][b], vals[b % 2][:, 0:NKB1, H:VW]).then_inc(stored[b % 2], 16)
                    if b + 2 < B:
                        load(b + 2)
                sp.wait_ge(bias_done, 5)
                sp.dma_start(scratch["bias0"], bias0[:]).then_inc(bias_stored, 16)
                sp.dma_start(scratch["bias1"], bias1[:]).then_inc(bias_stored, 16)
                for i in range(2):
                    sp.wait_ge(stored[i], 16 * STORES * B // 2)
                sp.wait_ge(bias_stored, 32)

            @block.gpsimd
            def _(pool):
                for i in range(2):
                    pool.memset(hT[i][:, :, SC + SQ:K0], 0.0).then_inc(pads_zero, 1)
                pool.memset(bias0[:], NEG).then_inc(bias_done, 1)
                pool.memset(bias1[:], 0.0).then_inc(bias_done, 1)
                pool.wait_ge(bias_done, 2)
                pool.memset(bias0[:, SC:SC + SQ], 0.0).then_inc(bias_done, 1)
                pool.memset(bias1[:, SC:K1], NEG).then_inc(bias_done, 1)

            @block.tensor
            def _(pe):
                w = {"k0": w_k0, "k1": w_k1, "q0": w_q0}
                pe.wait_ge(weights_in, 16 * 11)
                pe.wait_ge(pads_zero, 2)

                def item(b, n):
                    kind, o, c, cols = ITEMS[n]
                    count = b * NI + n
                    if count >= PB:
                        pe.wait_ge(item_read, 2 * (count - PB + 1))
                    for i in range(HALVES):
                        mm = nc.tensor.matmul(psum[0:rows(kind), count % PB, 0:cols],
                                              w[kind][:, i, o * P:o * P + rows(kind)], hT[b % 2][:, i, c:c + cols],
                                              start=(i == 0), stop=(i == HALVES - 1))
                    mm.then_inc(item_psum, 1)

                def values(b, kb):
                    count = b * NKB0 + kb
                    if count >= PB:
                        pe.wait_ge(val_read, count - PB + 1)
                    for i in range(HALVES):
                        mm = nc.tensor.matmul(psum[:, PB + count % PB, 0:VW], hT[b % 2][:, i, kb * P:(kb + 1) * P],
                                              w_v[:, i, :], start=(i == 0), stop=(i == HALVES - 1))
                    mm.then_inc(val_psum, 1)

                for b in range(B):
                    pe.wait_ge(hT_in[b % 2], 64 * (b // 2 + 1))
                    for n in range(max(NI, NKB0)):
                        if n < NI:
                            item(b, n)
                        if n < NKB0:
                            values(b, n)

            @block.scalar
            def _(act):
                act.wait_ge(weights_in, 16 * 11)
                act.wait_ge(qbias, 1)
                bias = {"k0": b_k0, "q0": b_q0s, "k1": b_k1}
                for b in range(B):
                    for n, (kind, o, c, cols) in enumerate(ITEMS):
                        count = b * NI + n
                        r = rows(kind)
                        scale = 1.0 / D0 if kind == "q0" else 1.0
                        act.wait_ge(item_psum, count + 1)
                        if b >= 2 and n == 0:
                            act.wait_ge(stored[b % 2], 16 * STORES * (b // 2))
                        if count >= 4:
                            act.wait_ge(piece_step, (count - 3) * STEPS)
                        src = psum[0:r, count % PB, 0:cols]
                        nc.scalar.activation(xf[0:r, count % 4, 0:cols], src, ACT.Identity,
                                             bias=bias[kind][0:r, o:o + 1], scale=scale).then_inc(item_read, 1)
                        nc.scalar.activation(piece(b, kind, o, 0, c, cols), src, ACT.Identity,
                                             bias=bias[kind][0:r, o:o + 1], scale=scale).then_inc(item_read, 1)

            @block.vector
            def _(dve):
                dve.wait_ge(weights_in, 16 * 11)
                dve.tensor_scalar(b_q0s[:], b_q0[:], 1.0 / D0, None, ALU.mult).then_inc(qbias, 1)
                dve.tensor_copy(mask_f[:], mask_i[:]).then_inc(qbias, 1)
                dve.wait_ge(qbias, 2)
                dve.wait_ge(bias_done, 4)
                dve.tensor_scalar(bias0[:, 0:SC], mask_f[:], 0.0, NEG, ALU.is_equal, ALU.mult).then_inc(bias_done, 1)

                def split(b, n):
                    kind, o, c, cols = ITEMS[n]
                    count = b * NI + n
                    r = rows(kind)
                    x, rest = xf[0:r, count % 4, 0:cols], r1[0:r, count % 2, 0:cols]
                    dve.wait_ge(item_read, 2 * (count + 1))
                    if count >= 2:
                        dve.wait_ge(piece_step, (count - 1) * STEPS)
                    dve.tensor_tensor(rest, x, piece(b, kind, o, 0, c, cols), ALU.subtract).then_inc(piece_step, 1)
                    dve.wait_ge(piece_step, count * STEPS + 1)
                    dve.tensor_copy(piece(b, kind, o, 1, c, cols), rest).then_inc(piece_step, 1)
                    dve.wait_ge(piece_step, count * STEPS + 2)
                    dve.tensor_tensor(piece(b, kind, o, 2, c, cols), rest, piece(b, kind, o, 1, c, cols),
                                      ALU.subtract).then_inc(piece_step, 2)

                def values(b, kb):
                    count = b * NKB0 + kb
                    dve.wait_ge(val_psum, count + 1)
                    if b >= 2 and kb == 0:
                        dve.wait_ge(stored[b % 2], 16 * STORES * (b // 2))
                    dve.tensor_tensor(vals[b % 2][:, kb, :], psum[:, PB + count % PB, 0:VW], b_v[:], ALU.add)\
                       .then_inc(val_read, 1)

                for b in range(B):
                    for n in range(max(NI, NKB0)):
                        if n < NKB0:
                            values(b, n)
                        if n < NI:
                            split(b, n)


def attention(nc, t, scratch, layer):
    L0 = layer == 0
    NG, NKB, D = (G0, NKB0, D0) if L0 else (G1, NKB1, D1)
    KEYS = NKB * P
    NKEYS = SC + SQ if L0 else SC
    KH = 4 if L0 else 1
    SLOTS = 4
    CH = 4
    cuts = [0]
    for i in range(CH):
        cuts.append(cuts[-1] + -(-(NKEYS - cuts[-1]) // (CH - i)))
    NJ = 4 * QB
    UNIT = 4
    if L0:
        STEPS = [[(kb, j) for kb in range(u, min(u + UNIT, NKB))] for u in range(0, NKB, UNIT) for j in range(4)]
        LAG = 4
    else:
        STEPS = [[(kb, j) for j in range(4)] for kb in range(NKB)]
        LAG = 2
    NS = len(STEPS)
    NP = 8
    assert NG * NS % NP == 0 and NG * NS % 2 == 0
    HALF = NJ * CH // 2
    ITEMS = [("s", i) for i in range(HALF)] + [("s", HALF + i) for i in range(5)] + [("m", 0)]
    ITEMS += [("s", HALF + i) for i in range(5, HALF)] + [("m", 1)]
    NI = len(ITEMS)
    NSI = 2 * HALF
    assert NI % 2 == 0
    when = [[] for _ in range(NS)]
    for n in range(NI - 1):
        when[min(n * (NS - 2) // (NI - 1), NS - 3)].append(n)
    when[NS - 1].append(NI - 1)
    def products():
        out = []
        if L0:
            for kb in range(NKB):
                u, k = divmod(kb, UNIT)
                out.append((4 * u + LAG + k, kb, [(4 * u + j, k, j) for j in range(4)]))
        else:
            for kb in range(NKB):
                out.append((kb + LAG, kb, [(kb, j, j) for j in range(4)]))
        return out
    PRODUCTS = products()
    END = max(p[0] for p in PRODUCTS) - NS
    LOADS = 2 * len(COMBOS) + 2

    with ExitStack() as ctx:
        nm = f"a{layer}_"
        sb = lambda name, shape, dt: ctx.enter_context(nc.sbuf_tensor(nm + name, shape, dt))
        sem = lambda name: ctx.enter_context(nc.semaphore(nm + name))
        first_psum = ctx.enter_context(nc.psum_tensor(nm + "first", [P, 2, 512], F32))
        second_psum = ctx.enter_context(nc.psum_tensor(nm + "second", [P, 2, 1024], F32))
        out_psum = ctx.enter_context(nc.psum_tensor(nm + "out", [P, 512], F32))
        turn_psum = ctx.enter_context(nc.psum_tensor(nm + "turn", [P, QB, 256], F32))

        keys = [sb(f"keys{i}", [P, KH, KEYS], BF16) for i in range(SLOTS)]
        queries = [sb(f"queries{i}", [P, 4, SQ], BF16) for i in range(SLOTS)]
        values_in = [sb(f"values_in{i}", [P, NKB, KH * D], F32) for i in range(2)]
        values = [sb(f"values{i}", [P, NKB, KH, 32], F32) for i in range(2)]
        probs = sb("probs", [P, NP, 1024], F32)
        maxima = sb("maxima", [P, NJ, CH], F32)
        m_all = sb("m_all", [P, NJ], F32)
        m_rest = sb("m_rest", [P, NJ], F32)
        m_cols = sb("m_cols", [P, NJ, 4], BF16)
        ident = sb("ident", [P, P], F32)
        ident_b = sb("ident_b", [P, P], BF16)
        out_T = sb("out_T", [P, SQ], F32)
        recip = sb("recip", [P, QB, 4], F32)
        out_n = sb("out_n", [P, 2, QB, 4 * D], F32)
        if not L0:
            mask_q = sb("mask_q", [P, QB, SC], F32)
            mask_k = sb("mask_k", [P, NKB, SQ], F32)
            mask_p = sb("mask_p", [P, 3, NKB, SQ], BF16)

        constants = sem("constants")
        loaded = [sem(f"loaded{i}") for i in range(SLOTS)]
        v_loaded = [sem(f"v_loaded{i}") for i in range(2)]
        v_placed = sem("v_placed")
        first_full = sem("first_full")
        first_free = sem("first_free")
        m_step = sem("m_step")
        m_rows = sem("m_rows")
        second_full = sem("second_full")
        probs_ready = sem("probs_ready")
        product = sem("product")
        out_read = sem("out_read")
        turned = sem("turned")
        recip_done = sem("recip_done")
        normed = sem("normed")
        stored = [sem(f"stored{i}") for i in range(2)]
        mask_in = sem("mask_in")
        mask_k_in = sem("mask_k_in")
        mask_step = sem("mask_step")
        MSTEPS = 4
        MS = 6
        dst = scratch["attn0" if L0 else "attn1"]

        CONSTS = 10 + 2 * SLOTS if L0 else 11 + 4 * SLOTS

        block = ctx.enter_context(nc.Block())

        @block.sync
        def _(sp):
            def load(b, first, G):
                n = G % SLOTS
                wait_at_least(sp, second_full, b, NG * NS, (G - SLOTS + 1) * NS)
                if L0:
                    lo, o = 64 * (G % 2), G // 2
                    kp = scratch["kp0"][b, lo:lo + 64, o, :, :].rearrange("(j d) c k -> d c j k", d=D)
                    qp = scratch["qp0"][b, lo:lo + 64, o, :, :].rearrange("(j d) c q -> d c j q", d=D)
                else:
                    lo, o = 32 * (G % 4), G // 4
                    kp = scratch["kp1"][b, D * G:D * G + D, :, :].rearrange("d c (a k) -> d c a k", a=1)
                    qp = scratch["qp1"][o, lo:lo + 32, :, bass.ds(b * SQ, SQ)].rearrange("(j d) c q -> d c j q", d=D)
                for c, (qc, kc) in enumerate(COMBOS):
                    sp.dma_start(queries[n][D * c:D * c + D, :, :], qp[:, qc]).then_inc(loaded[n], 16)
                    sp.dma_start(keys[n][D * c:D * c + D, :, :], kp[:, kc]).then_inc(loaded[n], 16)
                row = scratch["bias0"][bass.ds(b, 1), :] if L0 else scratch["bias1"]
                for h in range(KH):
                    sp.dma_start(keys[n][EXTRA:EXTRA + 1, h, :], row).then_inc(loaded[n], 16)
                wait_at_least(sp, v_placed, b, NG, G - 1)
                v = scratch["v0"][b, :, :, 64 * G:64 * G + 64] if L0 else scratch["v1"][b, :, :, D * G:D * G + D]
                sp.dma_start(values_in[G % 2][:], v).then_inc(v_loaded[G % 2], 16)

            def load_mask(b):
                wait_at_least(sp, first_free, b, NG * NSI, 0)
                sp.dma_start(mask_q[:], t["mask1"][b].rearrange("(a p) k -> p a k", p=P)).then_inc(mask_in, 16)

            def load_mask_k(b):
                wait_at_least(sp, mask_step, b, MSTEPS, 0)
                sp.dma_start(mask_k[:, 0:NKB - 1, :],
                             t["mask1T"][b, 0:(NKB - 1) * P, :].rearrange("(a p) q -> p a q", p=P)).then_inc(mask_k_in, 16)
                sp.dma_start(mask_k[0:SC - (NKB - 1) * P, NKB - 1, :], t["mask1T"][b, (NKB - 1) * P:SC, :]).then_inc(mask_k_in, 16)

            def store(b, G):
                sp.wait_ge(normed, b * NG + G + 1)
                sp.dma_start(dst[b, :, :, 4 * D * G:4 * D * G + 4 * D], out_n[:, G % 2, :, :]).then_inc(stored[G % 2], 16)

            sp.wait_ge(constants, CONSTS)
            if not L0:
                load_mask(0)
                load_mask_k(0)
            for G in range(SLOTS - 1):
                load(0, True, G)

            def body(b, first, last):
                for G in range(NG):
                    ahead = G + SLOTS - 1
                    if not L0 and G == NG - 1 and not last:
                        load_mask(b + 1)
                    if not L0 and G == 1 and not last:
                        load_mask_k(b + 1)
                    if ahead < NG:
                        load(b, first, ahead)
                    elif not last:
                        load(b + 1, False, ahead - NG)
                    if G:
                        store(b, G - 1)
                    elif not first:
                        store(b - 1, NG - 1)
            each_batch(sp, body)
            store(B - 1, NG - 1)
            for i in range(2):
                sp.wait_ge(stored[i], 16 * B * NG // 2)

        @block.gpsimd
        def _(pool):
            made = 0

            def constant(ins):
                nonlocal made
                made += 1
                ins.then_inc(constants, 1)
                pool.wait_ge(constants, made)

            for m in [m_cols, ident, ident_b] + values + ([] if L0 else keys + queries + [mask_k]):
                constant(pool.memset(m[:], 0.0))
            for n in range(SLOTS):
                constant(pool.memset(keys[n][EXTRA:KROWS, :, :], 1.0))
                constant(pool.memset(queries[n][EXTRA:EXTRA + 1, :, :], 1.0))
            for i in range(2):
                constant(pool.memset(values[i][:, :, :, D:D + 1], 1.0))
            constant(pool.memset(m_cols[:, :, 0:1], 1.0))
            for m in (ident, ident_b):
                constant(pool.affine_select(out=m[:], in_=m[:], compare_op=ALU.not_equal, fill=1.0, base=0,
                                            pattern=[[-1, P]], channel_multiplier=1))
            assert made == CONSTS

            def place(b, G):
                uses = NG // 2
                pool.wait_ge(v_loaded[G % 2], 16 * (b * uses + G // 2 + 1))
                wait_at_least(pool, product, b, NG * NKB, (G - 1) * NKB)
                pool.nop(nofuse=True)
                pool.tensor_copy(values[G % 2][:, :, :, 0:D],
                                 values_in[G % 2][:].rearrange("p k (h d) -> p k h d", h=KH)).then_inc(v_placed, 1)

            def split_mask(b):
                pool.wait_ge(mask_k_in, 32 * (b + 1))
                wait_at_least(pool, second_full, b, NG * NS, 0)
                at = lambda pc: mask_p[:, pc]
                pool.nop(nofuse=True)
                pool.tensor_copy(at(0), mask_k[:]).then_inc(mask_step, 1)
                pool.wait_ge(mask_step, b * MSTEPS + 1)
                pool.nop(nofuse=True)
                pool.tensor_tensor(mask_k[:], mask_k[:], at(0), ALU.subtract).then_inc(mask_step, 1)
                pool.wait_ge(mask_step, b * MSTEPS + 2)
                pool.nop(nofuse=True)
                pool.tensor_copy(at(1), mask_k[:]).then_inc(mask_step, 1)
                pool.wait_ge(mask_step, b * MSTEPS + 3)
                pool.nop(nofuse=True)
                pool.tensor_tensor(at(2), mask_k[:], at(1), ALU.subtract).then_inc(mask_step, 1)

            def body(b, first, last):
                for G in range(NG):
                    place(b, G)
                    if G == 0 and not L0:
                        split_mask(b)
            each_batch(pool, body)

        @block.tensor
        def _(pe):
            def item(b, G, n):
                kind, i = ITEMS[n]
                slot = G % SLOTS
                if n == 0:
                    pe.wait_ge(loaded[slot], 16 * (12 + KH) * (b * (NG // SLOTS) + G // SLOTS + 1))
                bank = n % 2
                pg, pn = (G, n - 2) if n >= 2 else (G - 1, NI + n - 2)
                if ITEMS[pn][0] == "s":
                    wait_at_least(pe, first_free, b, NG * NSI, pg * NSI + ITEMS[pn][1] + 1)
                else:
                    wait_at_least(pe, m_rows, b, 2 * NG, 2 * pg + ITEMS[pn][1] + 1)
                if kind == "s":
                    j, rest = divmod(i, QB * CH)
                    qb, c = divmod(rest, CH)
                    nc.tensor.matmul(first_psum[:, bank, 0:cuts[c + 1] - cuts[c]],
                                     queries[slot][0:EXTRA + 1, j, qb * P:(qb + 1) * P],
                                     keys[slot][0:EXTRA + 1, j % KH, cuts[c]:cuts[c + 1]],
                                     start=True, stop=True).then_inc(first_full, 1)
                else:
                    pe.wait_ge(m_step, (b * NG + G) * 2 * MS + (i + 1) * MS)
                    for k in range(NJ // 2):
                        mm = nc.tensor.matmul(first_psum[EXTRA:KROWS, bank, k * P:(k + 1) * P],
                                              m_cols[:, i * NJ // 2 + k, :], ident_b[:], start=True, stop=True)
                    mm.then_inc(first_full, 1)

            def scores(b, G, s):
                slot = G % SLOTS
                if s == 0 or (L0 and s == 2):
                    half = 2 if not L0 or s else 1
                    pe.wait_ge(m_rows, (b * NG + G) * 2 + half)
                wait_at_least(pe, probs_ready, b, NG * NS, G * NS + s - 1)
                unit = (G * NS + s) % 2
                if L0:
                    for k, (kb, j) in enumerate(STEPS[s]):
                        mm = nc.tensor.matmul(second_psum[:, unit, k * SQ:(k + 1) * SQ],
                                              keys[slot][0:KROWS, j, kb * P:(kb + 1) * P],
                                              queries[slot][0:KROWS, j, :], start=True, stop=True)
                    mm.then_inc(second_full, 1)
                else:
                    if G == 0 and s == 0:
                        pe.wait_ge(mask_step, (b + 1) * MSTEPS)
                    for h in range(2):
                        bank = second_psum[:, unit, 512 * h:512 * h + 512]
                        nc.tensor.matmul(bank, keys[slot][0:KROWS, 0, s * P:(s + 1) * P],
                                         queries[slot][0:KROWS, 2 * h:2 * h + 2, :].rearrange("p a q -> p (a q)"),
                                         start=True, stop=False)
                        for pc in range(3):
                            mm = nc.tensor.matmul(bank.rearrange("p (a q) -> p a q", a=2), ident_b[:],
                                                  mask_p[:, pc, s, :].unsqueeze(1).to_broadcast([P, 2, SQ]),
                                                  start=False, stop=(pc == 2))
                    mm.then_inc(second_full, 1)

            def products(b, G, kb, parts):
                if kb == 0:
                    pe.wait_ge(v_placed, b * NG + G + 1)
                    wait_at_least(pe, out_read, b, NG, G)
                pe.wait_ge(probs_ready, (b * NG + G) * NS + max(s for s, _, _ in parts) + 1)
                for s, col, j in parts:
                    mm = nc.tensor.matmul(out_psum[32 * j:32 * j + 32, 0:SQ], values[G % 2][:, kb, j % KH, :],
                                          probs[:, (G * NS + s) % NP, col * SQ:(col + 1) * SQ],
                                          start=(kb == 0), stop=(kb == NKB - 1))
                mm.then_inc(product, 1)

            def turn(b, G):
                pe.wait_ge(out_read, b * NG + G + 1)
                wait_at_least(pe, normed, b, NG, G)
                for qb in range(QB):
                    mm = nc.tensor.transpose(turn_psum[:, qb, 0:P], out_T[:, qb * P:(qb + 1) * P], ident[:])
                mm.then_inc(turned, 1)

            def after(b, G, s):
                for at, kb, parts in PRODUCTS:
                    if at == s:
                        products(b, G, kb, parts)

            pe.wait_ge(constants, CONSTS)
            for n in range(NI):
                item(0, 0, n)

            def body(b, first, last):
                for G in range(NG):
                    before = (b, G - 1) if G else (b - 1, NG - 1)
                    nxt = (b, G + 1) if G + 1 < NG else (b + 1, 0)
                    for s in range(NS):
                        scores(b, G, s)
                        if not (last and G == NG - 1):
                            for n in when[s]:
                                item(*nxt, n)
                        if G or not first:
                            if s <= END:
                                after(*before, NS + s)
                            if s == END + 2:
                                turn(*before)
                        after(b, G, s)
            each_batch(pe, body)
            for s in range(END + 1):
                after(B - 1, NG - 1, NS + s)
            turn(B - 1, NG - 1)

        @block.scalar
        def _(act):
            def rows(b, G, n):
                half = ITEMS[n][1]
                act.wait_ge(first_full, (b * NG + G) * NI + n + 1)
                nc.scalar.copy(queries[G % SLOTS][EXTRA:KROWS, 2 * half:2 * half + 2, :].rearrange("p a q -> p (a q)"),
                               first_psum[EXTRA:KROWS, n % 2, :]).then_inc(m_rows, 1)

            def exps(b, G, s):
                act.wait_ge(second_full, (b * NG + G) * NS + s + 1)
                prev = G * NS + s - NP
                pg, ps = divmod(prev, NS)
                kb = max(kb for at, kb, parts in PRODUCTS if any(p[0] == ps for p in parts))
                wait_at_least(act, product, b, NG * NKB, pg * NKB + kb + 1)
                cols = len(STEPS[s]) * SQ
                nc.scalar.activation(probs[:, (G * NS + s) % NP, 0:cols], second_psum[:, (G * NS + s) % 2, 0:cols],
                                     ACT.Exp).then_inc(probs_ready, 1)

            def read_out(b, G):
                act.wait_ge(product, (b * NG + G + 1) * NKB)
                wait_at_least(act, turned, b, NG, G)
                nc.scalar.copy(out_T[:], out_psum[:, 0:SQ]).then_inc(out_read, 1)

            act.wait_ge(constants, CONSTS)
            M_ITEMS = [n for n, (kind, _) in enumerate(ITEMS) if kind == "m"]
            for n in M_ITEMS:
                rows(0, 0, n)

            def body(b, first, last):
                for G in range(NG):
                    before = (b, G - 1) if G else (b - 1, NG - 1)
                    nxt = (b, G + 1) if G + 1 < NG else (b + 1, 0)
                    for s in range(NS):
                        if (G or not first) and s == END + 1:
                            read_out(*before)
                        exps(b, G, s)
                        if not (last and G == NG - 1):
                            for n in when[s]:
                                if n in M_ITEMS:
                                    rows(*nxt, n)
            each_batch(act, body)
            read_out(B - 1, NG - 1)

        @block.vector
        def _(dve):
            def item(b, G, n):
                kind, i = ITEMS[n]
                if kind == "m":
                    return
                j, rest = divmod(i, QB * CH)
                qb, c = divmod(rest, CH)
                jq = j * QB + qb
                w = cuts[c + 1] - cuts[c]
                if i == 0 and not L0 and G == 0:
                    dve.wait_ge(mask_in, 16 * (b + 1))
                dve.wait_ge(first_full, (b * NG + G) * NI + n + 1)
                if i % HALF == 0:
                    wait_at_least(dve, m_step, b, NG * 2 * MS, (2 * (G - 1) + i // HALF) * MS + 1)
                dve.nop(nofuse=True)
                bank = first_psum[:, n % 2, 0:w]
                if L0:
                    dve.tensor_reduce(maxima[:, jq, c:c + 1], bank, AX.X, ALU.max).then_inc(first_free, 1)
                else:
                    dve.tensor_tensor_reduce(bank, bank, mask_q[:, qb, cuts[c]:cuts[c + 1]], 1.0, -3.0e38,
                                             ALU.add, ALU.max, maxima[:, jq, c:c + 1]).then_inc(first_free, 1)
                if i % HALF == HALF - 1:
                    pieces(b, G, i // HALF, n)

            def pieces(b, G, half, n):
                a = slice(half * NJ // 2, (half + 1) * NJ // 2)
                base = (b * NG + G) * 2 * MS + half * MS
                step = 0

                def done(ins):
                    nonlocal step
                    step += 1
                    ins.then_inc(m_step, 1)
                    if step < MS:
                        dve.wait_ge(m_step, base + step)
                dve.wait_ge(first_free, (b * NG + G) * NSI + (half + 1) * HALF)
                wait_at_least(dve, m_step, b, NG * 2 * MS, (G * 2 + half) * MS)
                done(dve.tensor_reduce(m_all[:, a].unsqueeze(2), maxima[:, a, :], AX.X, ALU.max))
                done(dve.tensor_scalar(m_cols[:, a, 1:2], m_all[:, a].unsqueeze(2), -1.0, None, ALU.mult))
                done(dve.tensor_tensor(m_rest[:, a].unsqueeze(2), m_all[:, a].unsqueeze(2), m_cols[:, a, 1:2], ALU.add))
                done(dve.tensor_scalar(m_cols[:, a, 2:3], m_rest[:, a].unsqueeze(2), -1.0, None, ALU.mult))
                done(dve.tensor_tensor(m_all[:, a].unsqueeze(2), m_rest[:, a].unsqueeze(2), m_cols[:, a, 2:3], ALU.add))
                done(dve.tensor_scalar(m_cols[:, a, 3:4], m_all[:, a].unsqueeze(2), -1.0, None, ALU.mult))

            def norm(b, G):
                dve.wait_ge(turned, b * NG + G + 1)
                wait_at_least(dve, normed, b, NG, G)
                out4 = turn_psum[:, :, 0:P].rearrange("p a (j w) -> p a j w", w=32)
                dve.reciprocal(recip[:].unsqueeze(3), out4[:, :, :, D:D + 1]).then_inc(recip_done, 1)
                dve.wait_ge(recip_done, b * NG + G + 1)
                wait_at_least(dve, stored[G % 2], b, 16 * (NG // 2), 16 * (G // 2))
                dve.tensor_tensor(out_n[:, G % 2, :, :].rearrange("p a (j d) -> p a j d", d=D), out4[:, :, :, 0:D],
                                  recip[:].unsqueeze(3).to_broadcast([P, QB, 4, D]), ALU.mult).then_inc(normed, 1)

            dve.wait_ge(constants, CONSTS)
            for n in range(NI):
                item(0, 0, n)

            def body(b, first, last):
                for G in range(NG):
                    before = (b, G - 1) if G else (b - 1, NG - 1)
                    nxt = (b, G + 1) if G + 1 < NG else (b + 1, 0)
                    for s in range(NS):
                        if not (last and G == NG - 1):
                            for n in when[s]:
                                item(*nxt, n)
                        if (G or not first) and s == END + 2:
                            norm(*before)
            each_batch(dve, body)
            norm(B - 1, NG - 1)


CT = 4
NT = B * QB
NCH = NT // CT
NF = F // P


def identity(pool, tile, sem):
    pool.memset(tile[:], 0.0).then_inc(sem, 1)
    pool.wait_ge(sem, 1)
    pool.affine_select(out=tile[:], in_=tile[:], compare_op=ALU.not_equal, fill=1.0, base=0,
                       pattern=[[-1, P]], channel_multiplier=1).then_inc(sem, 1)


def middle(nc, t, scratch):
    ORDER = [("T", 0), ("O", 0), ("T", 1), ("O", 1), ("Y", 0), ("U", 0), ("T", 2), ("O", 2), ("Y", 1), ("D", 0),
             ("U", 1), ("X", 0), ("T", 3), ("O", 3), ("Y", 2), ("D", 1), ("Q", 0), ("U", 2), ("X", 1), ("Y", 3),
             ("D", 2), ("Q", 1), ("U", 3), ("X", 2), ("D", 3), ("Q", 2), ("X", 3), ("Q", 3)]
    TURNS = [x for x in ORDER if x[0] in "TYX"]
    turn_no = {x: i for i, x in enumerate(TURNS)}
    GELU_A, GELU_B = 0.7978845608028654, 0.044715
    SCALE = float(D1) ** -0.5

    def gelu_at(step, n):
        c, f = divmod(n, NF)
        if step == "inner":
            return c * 3 * NF + (3 * f + 1 if f else 2)
        return c * 3 * NF + min(3 * (f + 1) + 2, 3 * NF)

    with ExitStack() as ctx:
        sb = lambda name, shape, dt: ctx.enter_context(nc.sbuf_tensor("mid_" + name, shape, dt))
        sem = lambda name: ctx.enter_context(nc.semaphore("mid_" + name))
        psum = ctx.enter_context(nc.psum_tensor("mid_psum", [P, 8, 512], F32))
        turn_ps, proj_ps, up_ps, down_ps, q_ps = (psum[:, 0:2], psum[:, 2:4], psum[:, 4:6], psum[:, 6], psum[:, 7])
        w_o = sb("w_o", [P, HALVES, H], F32)
        w_1 = sb("w_1", [P, HALVES, F], F32)
        w_2 = sb("w_2", [P, NF, H], F32)
        w_q = sb("w_q", [P, HALVES, H], F32)
        b_o = sb("b_o", [P, H], F32)
        b_2 = sb("b_2", [P, H], F32)
        w_n = sb("w_n", [P, H], F32)
        b_1 = sb("b_1", [P, NF], F32)
        b_q = sb("b_q", [P, HALVES], F32)
        b_qs = sb("b_qs", [P, HALVES], F32)
        ident = sb("ident", [P, P], F32)
        attn = sb("attn", [P, NT, H], F32)
        x_o = sb("x_o", [P, NT, H], F32)
        x_2 = sb("x_2", [P, NT, H], F32)
        x_1 = sb("x_1", [P, NT, H], F32)
        turned = {"T": sb("attn_T", [P, 2, HALVES, 512], F32), "Y": sb("norm_T", [P, 2, HALVES, 512], F32),
                  "X": sb("x_1_T", [P, 2, HALVES, 512], F32)}
        hidden = sb("hidden", [P, 2, NF, 512], F32)
        up = sb("up", [P, 2, 512], F32)
        cubic = sb("cubic", [P, 2, 512], F32)
        sumsq = sb("sumsq", [P, NT], F32)
        square = sb("square", [P, H], F32)
        rms = sb("rms", [P, NT], F32)
        qf = sb("qf", [P, 512], F32)
        q_pc = sb("q_pc", [P, 2, HALVES, 3, 512], BF16)

        weights_in, x_in, attn_in = sem("weights_in"), sem("x_in"), sem("attn_in")
        ident_done, bias_step = sem("ident_done"), sem("bias_step")
        x_step = sem("x_step")
        turn_full, turn_read = sem("turn_full"), sem("turn_read")
        proj_full, proj_read = sem("proj_full"), sem("proj_read")
        up_full, up_read = sem("up_full"), sem("up_read")
        down_full, down_read = sem("down_full"), sem("down_read")
        q_full, q_read = sem("q_full"), sem("q_read")
        norm_step, root, gelu_step, tanh_done = sem("norm_step"), sem("root"), sem("gelu_step"), sem("tanh_done")
        q_step, x_stored = sem("q_step"), sem("x_stored")
        q_stored = [sem(f"q_stored{i}") for i in range(2)]
        NSTEPS = 2 * CT + 2 + CT
        W = 9

        with nc.Block() as block:
            @block.sync
            def _(sp):
                row = lambda name: t[name].rearrange("(a n) -> a n", a=1).to_broadcast([P, H])
                sp.dma_start(attn[:].rearrange("p (b a) h -> p b (a h)", a=QB), scratch["attn0"].rearrange("b p a h -> p b (a h)")).then_inc(attn_in, 16)
                sp.dma_start(x_2[:], t["x"].rearrange("b (a p) h -> p (b a) h", p=P)).then_inc(x_in, 16)
                for dst, src in ((w_o, t["ow0"]), (w_1, t["w1"]), (w_2, t["w2"]), (w_q, t["qw1"])):
                    sp.dma_start(dst[:], src.rearrange("(i p) n -> p i n", p=P)).then_inc(weights_in, 16)
                sp.dma_start(b_o[:], row("ob0")).then_inc(weights_in, 16)
                sp.dma_start(b_2[:], row("b2")).then_inc(weights_in, 16)
                sp.dma_start(w_n[:], row("nw")).then_inc(weights_in, 16)
                sp.dma_start(b_1[:], t["b1"]).then_inc(weights_in, 16)
                sp.dma_start(b_q[:], t["qb1"]).then_inc(weights_in, 16)
                for c in range(NCH):
                    sp.wait_ge(q_step, (c + 1) * HALVES * 3)
                    sp.wait_ge(q_read, (c + 1) * HALVES * 2)
                    for o in range(HALVES):
                        sp.dma_start(scratch["qp1"][o, :, :, c * 512:(c + 1) * 512], q_pc[:, c % 2, o]).then_inc(q_stored[c % 2], 16)
                sp.wait_ge(down_read, NT)
                sp.dma_start(scratch["x1"].rearrange("b p a h -> p b (a h)"), x_1[:].rearrange("p (b a) h -> p b (a h)", a=QB)).then_inc(x_stored, 16)
                for i in range(2):
                    sp.wait_ge(q_stored[i], 16 * HALVES * NCH // 2)
                sp.wait_ge(x_stored, 16)

            @block.gpsimd
            def _(pool):
                identity(pool, ident, ident_done)
                pool.wait_ge(weights_in, 16 * W)
                pool.wait_ge(x_in, 16)
                for T in range(NT):
                    pool.tensor_tensor(x_o[:, T], x_2[:, T], b_o[:], ALU.add).then_inc(x_step, 1)
                pool.wait_ge(x_step, NT)
                for T in range(NT):
                    pool.tensor_tensor(x_2[:, T], x_2[:, T], b_2[:], ALU.add).then_inc(x_step, 1)

            @block.tensor
            def _(pe):
                pe.wait_ge(ident_done, 2)
                pe.wait_ge(attn_in, 16)
                pe.wait_ge(weights_in, 16 * W)
                src = {"T": attn, "Y": attn, "X": x_1}
                for kind, c in ORDER:
                    if kind in "TYX":
                        if kind == "Y":
                            pe.wait_ge(norm_step, (c + 1) * NSTEPS)
                        if kind == "X":
                            pe.wait_ge(down_read, (c + 1) * CT)
                        for k in range(CT):
                            n = turn_no[kind, c] * CT + k
                            if n >= 2:
                                pe.wait_ge(turn_read, n - 1)
                            for i in range(HALVES):
                                mm = nc.tensor.transpose(turn_ps[:, n % 2, i * P:(i + 1) * P],
                                                         src[kind][:, c * CT + k, i * P:(i + 1) * P], ident[:])
                            mm.then_inc(turn_full, 1)
                    if kind == "O":
                        pe.wait_ge(turn_read, (turn_no["T", c] + 1) * CT)
                        for k in range(CT):
                            n = c * CT + k
                            if n >= 2:
                                pe.wait_ge(proj_read, n - 1)
                            for i in range(HALVES):
                                mm = nc.tensor.matmul(proj_ps[:, n % 2, 0:H], turned["T"][:, c % 2, i, k * P:(k + 1) * P],
                                                      w_o[:, i, :], start=(i == 0), stop=(i == HALVES - 1))
                            mm.then_inc(proj_full, 1)
                    if kind == "U":
                        pe.wait_ge(turn_read, (turn_no["Y", c] + 1) * CT)
                        for f in range(NF):
                            n = c * NF + f
                            if n >= 2:
                                pe.wait_ge(up_read, 2 * (n - 1))
                            for i in range(HALVES):
                                mm = nc.tensor.matmul(up_ps[:, n % 2, :], w_1[:, i, f * P:(f + 1) * P],
                                                      turned["Y"][:, c % 2, i, :], start=(i == 0), stop=(i == HALVES - 1))
                            mm.then_inc(up_full, 1)
                    if kind == "D":
                        pe.wait_ge(gelu_step, (c + 1) * NF * 3)
                        for k in range(CT):
                            n = c * CT + k
                            if n >= 1:
                                pe.wait_ge(down_read, n)
                            for f in range(NF):
                                mm = nc.tensor.matmul(down_ps[:, 0:H], hidden[:, c % 2, f, k * P:(k + 1) * P], w_2[:, f, :],
                                                      start=(f == 0), stop=(f == NF - 1))
                            mm.then_inc(down_full, 1)
                    if kind == "Q":
                        pe.wait_ge(turn_read, (turn_no["X", c] + 1) * CT)
                        for o in range(HALVES):
                            n = c * HALVES + o
                            if n >= 1:
                                pe.wait_ge(q_read, 2 * n)
                            for i in range(HALVES):
                                mm = nc.tensor.matmul(q_ps[:, :], w_q[:, i, o * P:(o + 1) * P], turned["X"][:, c % 2, i, :],
                                                      start=(i == 0), stop=(i == HALVES - 1))
                            mm.then_inc(q_full, 1)

            @block.scalar
            def _(act):
                act.wait_ge(weights_in, 16 * W)
                act.wait_ge(bias_step, 1)
                for kind, c in ORDER:
                    if kind == "O":
                        act.wait_ge(norm_step, c * NSTEPS + 2 * CT + 1)
                        nc.scalar.activation(rms[:, c * CT:(c + 1) * CT], rms[:, c * CT:(c + 1) * CT], ACT.Sqrt).then_inc(root, 1)
                    if kind == "U":
                        for f in range(NF + 1):
                            n = c * NF + f
                            if f < NF:
                                act.wait_ge(up_full, n + 1)
                                if n >= 2:
                                    act.wait_ge(gelu_step, gelu_at("last", n - 2))
                                nc.scalar.activation(up[:, n % 2], up_ps[:, n % 2], ACT.Identity,
                                                     bias=b_1[:, f:f + 1]).then_inc(up_read, 1)
                                nc.scalar.activation(cubic[:, n % 2], up_ps[:, n % 2], ACT.Square,
                                                     bias=b_1[:, f:f + 1]).then_inc(up_read, 1)
                            if f:
                                act.wait_ge(gelu_step, gelu_at("inner", n - 1))
                                nc.scalar.activation(cubic[:, (n - 1) % 2], cubic[:, (n - 1) % 2], ACT.Tanh,
                                                     scale=GELU_A).then_inc(tanh_done, 1)
                    if kind == "Q":
                        for o in range(HALVES):
                            n = c * HALVES + o
                            act.wait_ge(q_full, n + 1)
                            if n >= 1:
                                act.wait_ge(q_step, 3 * n)
                            if c >= 2 and o == 0:
                                act.wait_ge(q_stored[c % 2], 16 * HALVES * (c // 2))
                            nc.scalar.activation(qf[:], q_ps[:, :], ACT.Identity, bias=b_qs[:, o:o + 1],
                                                 scale=SCALE).then_inc(q_read, 1)
                            nc.scalar.activation(q_pc[:, c % 2, o, 0], q_ps[:, :], ACT.Identity, bias=b_qs[:, o:o + 1],
                                                 scale=SCALE).then_inc(q_read, 1)

            @block.vector
            def _(dve):
                dve.wait_ge(weights_in, 16 * W)
                dve.tensor_scalar(b_qs[:], b_q[:], SCALE, None, ALU.mult).then_inc(bias_step, 1)

                def norm(c):
                    a, base = slice(c * CT, (c + 1) * CT), c * NSTEPS
                    for k in range(CT):
                        T = c * CT + k
                        dve.wait_ge(proj_full, T + 1)
                        dve.wait_ge(x_step, T + 1)
                        dve.wait_ge(turn_full, (turn_no["T", c] + 1) * CT)
                        dve.tensor_tensor(attn[:, T], proj_ps[:, T % 2, 0:H], x_o[:, T], ALU.add).then_inc(proj_read, 1)
                        dve.wait_ge(proj_read, T + 1)
                        if T:
                            dve.wait_ge(norm_step, base + 2 * k if k else base)
                        dve.tensor_tensor_reduce(square[:], attn[:, T], attn[:, T], 1.0, 0.0, ALU.mult, ALU.add,
                                                 sumsq[:, T:T + 1]).then_inc(norm_step, 2)
                    dve.wait_ge(norm_step, base + 2 * CT)
                    dve.tensor_scalar(rms[:, a], sumsq[:, a], 1.0 / H, EPS, ALU.mult, ALU.add).then_inc(norm_step, 1)
                    dve.wait_ge(root, c + 1)
                    dve.reciprocal(sumsq[:, a], rms[:, a]).then_inc(norm_step, 1)
                    dve.wait_ge(norm_step, base + 2 * CT + 2)
                    for k in range(CT):
                        T = c * CT + k
                        dve.scalar_tensor_tensor(out=attn[:, T], in0=attn[:, T], scalar=sumsq[:, T:T + 1], in1=w_n[:],
                                                 op0=ALU.mult, op1=ALU.mult).then_inc(norm_step, 1)

                for kind, c in ORDER:
                    if kind in "TYX":
                        for k in range(CT):
                            n = turn_no[kind, c] * CT + k
                            dve.wait_ge(turn_full, n + 1)
                            dve.tensor_copy(turned[kind][:, c % 2, :, k * P:(k + 1) * P],
                                            turn_ps[:, n % 2, 0:H].rearrange("p (i q) -> p i q", i=HALVES)).then_inc(turn_read, 1)
                    if kind == "O":
                        norm(c)
                    if kind == "U":
                        for f in range(NF + 1):
                            n = c * NF + f
                            if f < NF:
                                buf = n % 2
                                dve.wait_ge(up_read, 2 * (n + 1))
                                dve.tensor_scalar(cubic[:, buf], cubic[:, buf], GELU_B, 1.0, ALU.mult, ALU.add).then_inc(gelu_step, 1)
                                dve.wait_ge(gelu_step, gelu_at("inner", n) - 1)
                                dve.tensor_tensor(cubic[:, buf], cubic[:, buf], up[:, buf], ALU.mult).then_inc(gelu_step, 1)
                            if f:
                                m = n - 1
                                dve.wait_ge(tanh_done, m + 1)
                                dve.scalar_tensor_tensor(out=hidden[:, c % 2, f - 1], in0=cubic[:, m % 2], scalar=1.0,
                                                         in1=up[:, m % 2], op0=ALU.add, op1=ALU.mult).then_inc(gelu_step, 1)
                    if kind == "D":
                        for k in range(CT):
                            T = c * CT + k
                            dve.wait_ge(down_full, T + 1)
                            dve.wait_ge(x_step, NT + T + 1)
                            dve.scalar_tensor_tensor(out=x_1[:, T], in0=down_ps[:, 0:H], scalar=0.5, in1=x_2[:, T],
                                                     op0=ALU.mult, op1=ALU.add).then_inc(down_read, 1)
                    if kind == "Q":
                        for o in range(HALVES):
                            n = c * HALVES + o
                            pc = lambda i: q_pc[:, c % 2, o, i]
                            dve.wait_ge(q_read, 2 * (n + 1))
                            dve.tensor_tensor(qf[:], qf[:], pc(0), ALU.subtract).then_inc(q_step, 1)
                            dve.wait_ge(q_step, 3 * n + 1)
                            dve.tensor_copy(pc(1), qf[:]).then_inc(q_step, 1)
                            dve.wait_ge(q_step, 3 * n + 2)
                            dve.tensor_tensor(pc(2), qf[:], pc(1), ALU.subtract).then_inc(q_step, 1)


def finish(nc, t, scratch, out):
    with ExitStack() as ctx:
        sb = lambda name, shape, dt: ctx.enter_context(nc.sbuf_tensor("fin_" + name, shape, dt))
        sem = lambda name: ctx.enter_context(nc.semaphore("fin_" + name))
        psum = ctx.enter_context(nc.psum_tensor("fin_psum", [P, 8, 512], F32))
        w_o = sb("w_o", [P, HALVES, H], F32)
        b_o, gamma, beta = sb("b_o", [P, H], F32), sb("gamma", [P, H], F32), sb("beta", [P, H], F32)
        ident = sb("ident", [P, P], F32)
        attn = sb("attn", [P, NT, H], F32)
        x_1 = sb("x_1", [P, NT, H], F32)
        y = sb("y", [P, NT, H], F32)
        attn_T = sb("attn_T", [P, 4, HALVES, P], F32)
        stats = sb("stats", [P, NT, 6], F32)
        mean_var = sb("mean_var", [P, NT, 2], F32)
        std = sb("std", [P, NT], F32)
        weights_in, attn_in, x_in, ident_done = sem("weights_in"), sem("attn_in"), sem("x_in"), sem("ident_done")
        x_step, turn_full, turn_read = sem("x_step"), sem("turn_full"), sem("turn_read")
        proj_full, proj_read, stat_step, root = sem("proj_full"), sem("proj_read"), sem("stat_step"), sem("root")
        norm_step, scaled, stored = sem("norm_step"), sem("scaled"), sem("stored")

        with nc.Block() as block:
            @block.sync
            def _(sp):
                sp.dma_start(attn[:].rearrange("p (b a) h -> p b (a h)", a=QB), scratch["attn1"].rearrange("b p a h -> p b (a h)")).then_inc(attn_in, 16)
                sp.dma_start(w_o[:], t["ow1"].rearrange("(i p) n -> p i n", p=P)).then_inc(weights_in, 16)
                for dst, name in ((b_o, "ob1"), (gamma, "gamma"), (beta, "beta")):
                    sp.dma_start(dst[:], t[name].rearrange("(a n) -> a n", a=1).to_broadcast([P, H])).then_inc(weights_in, 16)
                sp.dma_start(x_1[:].rearrange("p (b a) h -> p b (a h)", a=QB), scratch["x1"].rearrange("b p a h -> p b (a h)")).then_inc(x_in, 16)
                for b in range(B):
                    sp.wait_ge(scaled, 2 * QB * (b + 1))
                    sp.dma_start(out[b].rearrange("(a p) h -> p a h", p=P), y[:, b * QB:(b + 1) * QB]).then_inc(stored, 16)
                sp.wait_ge(stored, 16 * B)

            @block.gpsimd
            def _(pool):
                identity(pool, ident, ident_done)
                pool.wait_ge(weights_in, 64)
                pool.wait_ge(x_in, 16)
                for T in range(NT):
                    pool.tensor_tensor(x_1[:, T], x_1[:, T], b_o[:], ALU.add).then_inc(x_step, 1)

            @block.tensor
            def _(pe):
                pe.wait_ge(ident_done, 2)
                pe.wait_ge(attn_in, 16)
                pe.wait_ge(weights_in, 64)
                for T in range(NT + 1):
                    if T < NT:
                        if T >= 4:
                            pe.wait_ge(turn_read, T - 3)
                        for i in range(HALVES):
                            mm = nc.tensor.transpose(psum[:, T % 4, i * P:(i + 1) * P], attn[:, T, i * P:(i + 1) * P], ident[:])
                        mm.then_inc(turn_full, 1)
                    if T:
                        n = T - 1
                        pe.wait_ge(turn_read, n + 1)
                        if n >= 4:
                            pe.wait_ge(proj_read, n - 3)
                        for i in range(HALVES):
                            mm = nc.tensor.matmul(psum[:, 4 + n % 4, 0:H], attn_T[:, n % 4, i, :], w_o[:, i, :],
                                                  start=(i == 0), stop=(i == HALVES - 1))
                        mm.then_inc(proj_full, 1)

            @block.scalar
            def _(act):
                for T in range(NT):
                    act.wait_ge(turn_full, T + 1)
                    if T >= 4:
                        act.wait_ge(proj_full, T - 3)
                    nc.scalar.copy(attn_T[:, T % 4].rearrange("p i q -> p (i q)"), psum[:, T % 4, 0:H]).then_inc(turn_read, 1)
                act.wait_ge(stat_step, 2 * NT + 1)
                nc.scalar.activation(std[:], std[:], ACT.Sqrt).then_inc(root, 1)

            @block.vector
            def _(dve):
                for T in range(NT):
                    dve.wait_ge(proj_full, T + 1)
                    dve.wait_ge(x_step, T + 1)
                    dve.tensor_tensor(y[:, T], psum[:, 4 + T % 4, 0:H], x_1[:, T], ALU.add).then_inc(proj_read, 1)
                    dve.wait_ge(proj_read, T + 1)
                    dve.bn_stats(stats[:, T], y[:, T]).then_inc(stat_step, 1)
                    dve.wait_ge(stat_step, 2 * T + 1)
                    dve.bn_aggr(mean_var[:, T], stats[:, T]).then_inc(stat_step, 1)
                dve.wait_ge(stat_step, 2 * NT)
                dve.tensor_scalar(std[:].unsqueeze(2), mean_var[:, :, 1:2], EPS, None, ALU.add).then_inc(stat_step, 1)
                dve.wait_ge(root, 1)
                dve.reciprocal(std[:], std[:]).then_inc(norm_step, 1)
                dve.wait_ge(norm_step, 1)
                for T in range(NT):
                    dve.tensor_scalar(y[:, T], y[:, T], mean_var[:, T, 0:1], std[:, T:T + 1], ALU.subtract, ALU.mult)\
                       .then_inc(norm_step, 1)
                    dve.wait_ge(norm_step, T + 2)
                    dve.tensor_tensor(y[:, T], y[:, T], gamma[:], ALU.mult).then_inc(scaled, 1)
                    dve.wait_ge(scaled, 2 * T + 1)
                    dve.tensor_tensor(y[:, T], y[:, T], beta[:], ALU.add).then_inc(scaled, 1)


def build(nc, t, out):
    dram = lambda name, shape, dt: nc.dram_tensor(name, shape, dt, kind="Internal").ap()
    scratch = {
        "kp0": dram("kp0", (B, P, HALVES, 3, K0), BF16),
        "qp0": dram("qp0", (B, P, HALVES, 3, SQ), BF16),
        "kp1": dram("kp1", (B, KV1, 3, K1), BF16),
        "qp1": dram("qp1", (HALVES, P, 3, B * SQ), BF16),
        "v0": dram("v0", (B, P, NKB0, H), F32),
        "v1": dram("v1", (B, P, NKB1, KV1), F32),
        "bias0": dram("bias0_rows", (B, K0), BF16),
        "bias1": dram("bias1_row", (1, K1), BF16),
        "attn0": dram("attn0", (B, P, QB, H), F32),
        "attn1": dram("attn1", (B, P, QB, H), F32),
        "x1": dram("x1", (B, P, QB, H), F32),
    }
    project_inputs(nc, t, scratch)
    attention(nc, t, scratch, 0)
    middle(nc, t, scratch)
    attention(nc, t, scratch, 1)
    finish(nc, t, scratch, out)


def kernel(**inputs):
    import numpy as np
    import concourse.bacc as bacc
    from concourse.bass_utils import run_bass_kernel_spmd

    a = {name: np.asarray(v) for name, v in inputs.items()}
    kw = a["L0_xattn_kv_w"].reshape(H, H, 2)
    kb = a["L0_xattn_kv_b"].reshape(H, 2)
    column = lambda v: v.reshape(-1, P).T
    laid = {
        "x": a["x"], "xT": a["x"].transpose(0, 2, 1), "ctxT": a["ctx_2048"].transpose(0, 2, 1),
        "mask0": a["mask_BxS2_ik0"], "mask1": a["mask_Bx1xSxS2_ff0"][:, 0], "mask1T": a["mask_Bx1xSxS2_ff0"][:, 0].transpose(0, 2, 1),
        "qw0": a["L0_xattn_q_w"], "qb0": column(a["L0_xattn_q_b"]), "kw0": kw[:, :, 0], "vw0": kw[:, :, 1],
        "kb0": column(kb[:, 0]), "vb0": kb[:, 1], "ow0": a["L0_xattn_out_w"], "ob0": a["L0_xattn_out_b"],
        "nw": a["L0_xattn_postnorm_w"], "w1": a["L0_xattn_mlp_w1"], "b1": column(a["L0_xattn_mlp_b1"]),
        "w2": a["L0_xattn_mlp_w2"], "b2": a["L0_xattn_mlp_b2"],
        "qw1": a["L1_xattn_Wq"], "qb1": column(a["L1_xattn_bq"]), "kw1": a["L1_xattn_Wk"], "kb1": a["L1_xattn_bk"][:, None],
        "vw1": a["L1_xattn_Wv"], "vb1": a["L1_xattn_bv"], "ow1": a["L1_xattn_Wo"], "ob1": a["L1_xattn_bo"],
        "gamma": a["L1_xattn_gamma"], "beta": a["L1_xattn_beta"],
    }
    nc = bacc.Bacc("TRN2", target_bir_lowering=False, num_devices=1)
    arrays, t = {}, {}
    for name, v in laid.items():
        arrays[f"in_{name}"] = np.ascontiguousarray(v)
        t[name] = nc.dram_tensor(f"in_{name}", v.shape, mybir.dt.from_np(v.dtype), kind="ExternalInput").ap()
    out = nc.dram_tensor("out_0", (B, SQ, H), F32, kind="ExternalOutput").ap()
    build(nc, t, out)
    r = run_bass_kernel_spmd(nc, [arrays], core_ids=[0])
    return r.results[0]["out_0"]
```

```python
from contextlib import ExitStack

import concourse.bass as bass
from concourse import mybir

F32 = mybir.dt.float32
BF16 = mybir.dt.bfloat16
I32 = mybir.dt.int32
ALU = mybir.AluOpType
ACT = mybir.ActivationFunctionType
AX = mybir.AxisListType

P = 128
B, SQ, H, SC = 8, 256, 256, 1601
HALVES = H // P
QB = SQ // P
F = 4 * H
EPS = 1e-6

NKB0 = -(-(SC + SQ) // P)
NKB1 = -(-SC // P)
K0, K1 = NKB0 * P, NKB1 * P
SKIP0 = 9
G0, G1 = 4, 8
D0, D1 = 16, 8
KV1 = H // 4
VW = H + KV1
NEG = -1.0e30

COMBOS = [(0, 0), (0, 1), (1, 0), (1, 1), (0, 2), (2, 0)]
EXTRA = 96
KROWS = 100


def each_batch(eng, body):
    body(0, True, False)
    with eng.Fori(1, B - 1) as b:
        body(b, False, False)
    body(B - 1, False, True)


def wait_at_least(eng, sem, b, per_batch, count):
    if isinstance(b, int):
        if b * per_batch + count > 0:
            eng.wait_ge(sem, b * per_batch + count)
    else:
        eng.wait_ge(sem, b * per_batch + count)


def project_inputs(nc, t, scratch):
    def items():
        out = []
        for o in range(HALVES):
            for c in range(0, K0, 512):
                out.append(("k0", o, c, min(512, K0 - c)))
        for c in range(0, K1, 512):
            out.append(("k1", 0, c, min(512, K1 - c)))
        for o in range(HALVES):
            out.append(("q0", o, SC, SQ))
        return out
    ITEMS = items()
    NI = len(ITEMS)
    PB = 4

    with ExitStack() as ctx:
        sb = lambda name, shape, dt: ctx.enter_context(nc.sbuf_tensor(name, shape, dt))
        sem = lambda name: ctx.enter_context(nc.semaphore(name))
        psum = ctx.enter_context(nc.psum_tensor("proj_psum", [P, 8, 512], F32))
        w_k0 = sb("w_k0", [P, HALVES, H], F32)
        w_q0 = sb("w_q0", [P, HALVES, H], F32)
        w_k1 = sb("w_k1", [P, HALVES, KV1], F32)
        w_v = sb("w_v", [P, HALVES, VW], F32)
        b_k0 = sb("b_k0", [P, HALVES], F32)
        b_q0 = sb("b_q0", [P, HALVES], F32)
        b_q0s = sb("b_q0s", [P, HALVES], F32)
        b_k1 = sb("b_k1", [KV1, 1], F32)
        b_v = sb("b_v", [P, VW], F32)
        hT = [sb(f"hT{i}", [P, HALVES, K0], F32) for i in range(2)]
        pc_k0 = [sb(f"pc_k0_{i}", [P, HALVES, 3, K0], BF16) for i in range(2)]
        pc_k1 = [sb(f"pc_k1_{i}", [KV1, 3, K1], BF16) for i in range(2)]
        pc_q0 = [sb(f"pc_q0_{i}", [P, HALVES, 3, SQ], BF16) for i in range(2)]
        vals = [sb(f"vals{i}", [P, NKB0, VW], F32) for i in range(2)]
        xf = sb("xf", [P, 4, 512], F32)
        r1 = sb("r1", [P, 2, 512], F32)
        mask_i = sb("mask_i", [B, SC], I32)
        mask_f = sb("mask_f", [B, SC], F32)
        bias0 = sb("bias0", [B, K0], BF16)
        bias1 = sb("bias1", [1, K1], BF16)
        attended = sb("attended", [B, SKIP0 * P], BF16)
        any_row = sb("any_row", [B, 1], F32)
        ones = sb("ones", [B, 1], F32)
        flag = sb("flag", [1, 1], I32)

        weights_in = sem("proj_weights_in")
        hT_in = [sem(f"proj_hT_in{i}") for i in range(2)]
        pads_zero = sem("proj_pads_zero")
        item_psum = sem("proj_item_psum")
        item_read = sem("proj_item_read")
        val_psum = sem("proj_val_psum")
        val_read = sem("proj_val_read")
        piece_step = sem("proj_piece_step")
        bias_done = sem("proj_bias_done")
        qbias = sem("proj_qbias")
        stored = [sem(f"proj_stored{i}") for i in range(2)]
        bias_stored = sem("proj_bias_stored")
        flag_rows, flag_sum, flag_done = sem("proj_flag_rows"), sem("proj_flag_sum"), sem("proj_flag_done")
        STEPS = 4
        STORES = 5

        def rows(kind):
            return KV1 if kind == "k1" else P

        def piece(b, kind, o, pc, c, n):
            if kind == "k0":
                return pc_k0[b % 2][:, o, pc, c:c + n]
            if kind == "k1":
                return pc_k1[b % 2][:, pc, c:c + n]
            return pc_q0[b % 2][:, o, pc, :]

        with nc.Block() as block:
            @block.sync
            def _(sp):
                for dst, src in ((w_k0, t["kw0"]), (w_q0, t["qw0"]), (w_k1, t["kw1"])):
                    sp.dma_start(dst[:], src.rearrange("(i p) n -> p i n", p=P)).then_inc(weights_in, 16)
                sp.dma_start(w_v[:, :, 0:H], t["vw0"].rearrange("(i p) n -> p i n", p=P)).then_inc(weights_in, 16)
                sp.dma_start(w_v[:, :, H:VW], t["vw1"].rearrange("(i p) n -> p i n", p=P)).then_inc(weights_in, 16)
                sp.dma_start(b_k0[:], t["kb0"]).then_inc(weights_in, 16)
                sp.dma_start(b_q0[:], t["qb0"]).then_inc(weights_in, 16)
                sp.dma_start(b_k1[:], t["kb1"]).then_inc(weights_in, 16)
                sp.dma_start(b_v[:, 0:H], t["vb0"].rearrange("(a n) -> a n", a=1).to_broadcast([P, H])).then_inc(weights_in, 16)
                sp.dma_start(b_v[:, H:VW], t["vb1"].rearrange("(a n) -> a n", a=1).to_broadcast([P, KV1])).then_inc(weights_in, 16)
                sp.dma_start(mask_i[:], t["mask0"]).then_inc(weights_in, 16)

                def load(b):
                    if b >= 2:
                        sp.wait_ge(val_psum, (b - 1) * NKB0)
                        sp.wait_ge(item_psum, (b - 1) * NI)
                    for i in range(HALVES):
                        sp.dma_start(hT[b % 2][:, i, 0:SC], t["ctxT"][b, i * P:(i + 1) * P, :]).then_inc(hT_in[b % 2], 16)
                        sp.dma_start(hT[b % 2][:, i, SC:SC + SQ], t["xT"][b, i * P:(i + 1) * P, :]).then_inc(hT_in[b % 2], 16)
                load(0)
                load(1)
                for b in range(B):
                    sp.wait_ge(piece_step, (b + 1) * NI * STEPS)
                    sp.wait_ge(item_read, 2 * (b + 1) * NI)
                    sp.wait_ge(val_read, (b + 1) * NKB0)
                    sp.dma_start(scratch["kp0"][b], pc_k0[b % 2][:]).then_inc(stored[b % 2], 16)
                    sp.dma_start(scratch["kp1"][b], pc_k1[b % 2][:]).then_inc(stored[b % 2], 16)
                    sp.dma_start(scratch["qp0"][b], pc_q0[b % 2][:]).then_inc(stored[b % 2], 16)
                    sp.dma_start(scratch["v0"][b], vals[b % 2][:, :, 0:H]).then_inc(stored[b % 2], 16)
                    sp.dma_start(scratch["v1"][b], vals[b % 2][:, 0:NKB1, H:VW]).then_inc(stored[b % 2], 16)
                    if b + 2 < B:
                        load(b + 2)
                sp.wait_ge(bias_done, 5)
                sp.dma_start(scratch["bias0"], bias0[:]).then_inc(bias_stored, 16)
                sp.dma_start(scratch["bias1"], bias1[:]).then_inc(bias_stored, 16)
                sp.wait_ge(flag_done, 1)
                sp.dma_start(scratch["flag0"], flag[:]).then_inc(bias_stored, 16)
                for i in range(2):
                    sp.wait_ge(stored[i], 16 * STORES * B // 2)
                sp.wait_ge(bias_stored, 48)

            @block.gpsimd
            def _(pool):
                for i in range(2):
                    pool.memset(hT[i][:, :, SC + SQ:K0], 0.0).then_inc(pads_zero, 1)
                pool.memset(bias0[:], NEG).then_inc(bias_done, 1)
                pool.memset(bias1[:], 0.0).then_inc(bias_done, 1)
                pool.wait_ge(bias_done, 2)
                pool.memset(bias0[:, SC:SC + SQ], 0.0).then_inc(bias_done, 1)
                pool.memset(bias1[:, SC:K1], NEG).then_inc(bias_done, 1)

            @block.tensor
            def _(pe):
                w = {"k0": w_k0, "k1": w_k1, "q0": w_q0}
                pe.wait_ge(weights_in, 16 * 11)
                pe.wait_ge(pads_zero, 2)

                def item(b, n):
                    kind, o, c, cols = ITEMS[n]
                    count = b * NI + n
                    if count >= PB:
                        pe.wait_ge(item_read, 2 * (count - PB + 1))
                    for i in range(HALVES):
                        mm = nc.tensor.matmul(psum[0:rows(kind), count % PB, 0:cols],
                                              w[kind][:, i, o * P:o * P + rows(kind)], hT[b % 2][:, i, c:c + cols],
                                              start=(i == 0), stop=(i == HALVES - 1))
                    mm.then_inc(item_psum, 1)

                def values(b, kb):
                    count = b * NKB0 + kb
                    if count >= PB:
                        pe.wait_ge(val_read, count - PB + 1)
                    for i in range(HALVES):
                        mm = nc.tensor.matmul(psum[:, PB + count % PB, 0:VW], hT[b % 2][:, i, kb * P:(kb + 1) * P],
                                              w_v[:, i, :], start=(i == 0), stop=(i == HALVES - 1))
                    mm.then_inc(val_psum, 1)

                for b in range(B):
                    pe.wait_ge(hT_in[b % 2], 64 * (b // 2 + 1))
                    for n in range(max(NI, NKB0)):
                        if n < NI:
                            item(b, n)
                        if n < NKB0:
                            values(b, n)
                pe.wait_ge(flag_rows, 2)
                pe.wait_ge(item_read, 2 * B * NI)
                nc.tensor.matmul(psum[0:1, 0, 0:1], any_row[:], ones[:], start=True, stop=True).then_inc(flag_sum, 1)

            @block.scalar
            def _(act):
                act.wait_ge(weights_in, 16 * 11)
                act.wait_ge(qbias, 1)
                bias = {"k0": b_k0, "q0": b_q0s, "k1": b_k1}
                for b in range(B):
                    for n, (kind, o, c, cols) in enumerate(ITEMS):
                        count = b * NI + n
                        r = rows(kind)
                        scale = 1.0 / D0 if kind == "q0" else 1.0
                        act.wait_ge(item_psum, count + 1)
                        if b >= 2 and n == 0:
                            act.wait_ge(stored[b % 2], 16 * STORES * (b // 2))
                        if count >= 4:
                            act.wait_ge(piece_step, (count - 3) * STEPS)
                        src = psum[0:r, count % PB, 0:cols]
                        nc.scalar.activation(xf[0:r, count % 4, 0:cols], src, ACT.Identity,
                                             bias=bias[kind][0:r, o:o + 1], scale=scale).then_inc(item_read, 1)
                        nc.scalar.activation(piece(b, kind, o, 0, c, cols), src, ACT.Identity,
                                             bias=bias[kind][0:r, o:o + 1], scale=scale).then_inc(item_read, 1)

            @block.vector
            def _(dve):
                dve.wait_ge(weights_in, 16 * 11)
                dve.tensor_scalar(b_q0s[:], b_q0[:], 1.0 / D0, None, ALU.mult).then_inc(qbias, 1)
                dve.tensor_copy(mask_f[:], mask_i[:]).then_inc(qbias, 1)
                dve.wait_ge(qbias, 2)
                dve.wait_ge(bias_done, 4)
                dve.tensor_scalar(bias0[:, 0:SC], mask_f[:], 0.0, NEG, ALU.is_equal, ALU.mult).then_inc(bias_done, 1)
                dve.memset(ones[:], 1.0).then_inc(flag_rows, 1)
                dve.tensor_scalar(attended[:], mask_f[:, 0:SKIP0 * P], 0.0, None, ALU.not_equal, ALU.max,
                                  accum_out=any_row[:]).then_inc(flag_rows, 1)

                def split(b, n):
                    kind, o, c, cols = ITEMS[n]
                    count = b * NI + n
                    r = rows(kind)
                    x, rest = xf[0:r, count % 4, 0:cols], r1[0:r, count % 2, 0:cols]
                    dve.wait_ge(item_read, 2 * (count + 1))
                    if count >= 2:
                        dve.wait_ge(piece_step, (count - 1) * STEPS)
                    dve.tensor_tensor(rest, x, piece(b, kind, o, 0, c, cols), ALU.subtract).then_inc(piece_step, 1)
                    dve.wait_ge(piece_step, count * STEPS + 1)
                    dve.tensor_copy(piece(b, kind, o, 1, c, cols), rest).then_inc(piece_step, 1)
                    dve.wait_ge(piece_step, count * STEPS + 2)
                    dve.tensor_tensor(piece(b, kind, o, 2, c, cols), rest, piece(b, kind, o, 1, c, cols),
                                      ALU.subtract).then_inc(piece_step, 2)

                def values(b, kb):
                    count = b * NKB0 + kb
                    dve.wait_ge(val_psum, count + 1)
                    if b >= 2 and kb == 0:
                        dve.wait_ge(stored[b % 2], 16 * STORES * (b // 2))
                    dve.tensor_tensor(vals[b % 2][:, kb, :], psum[:, PB + count % PB, 0:VW], b_v[:], ALU.add)\
                       .then_inc(val_read, 1)

                for b in range(B):
                    for n in range(max(NI, NKB0)):
                        if n < NKB0:
                            values(b, n)
                        if n < NI:
                            split(b, n)
                dve.wait_ge(flag_sum, 1)
                dve.tensor_copy(flag[:], psum[0:1, 0, 0:1]).then_inc(flag_done, 1)


class Plan:

    def __init__(self, layer, first_kb, masked):
        L0 = self.L0 = layer == 0
        self.masked = masked
        self.first_kb = first_kb
        self.NG, nkb, self.D = (G0, NKB0, D0) if L0 else (G1, NKB1, D1)
        self.NKB = nkb - first_kb
        self.KH = 4 if L0 else 1
        last_key = SC + SQ if L0 else SC
        n = last_key - first_kb * P
        self.CH = -(-n // 512)
        self.cuts = [first_kb * P]
        for i in range(self.CH):
            self.cuts.append(self.cuts[-1] + -(-(last_key - self.cuts[-1]) // (self.CH - i)))
        self.HALF = HALF = 4 * QB * self.CH // 2
        self.MS = 6 if masked else 4
        late = self.MS + 1
        self.ITEMS = [("s", i) for i in range(HALF + late)] + [("m", 0)]
        self.ITEMS += [("s", HALF + i) for i in range(late, HALF)] + [("m", 1)]
        self.NI, self.NSI = len(self.ITEMS), 2 * HALF
        if L0:
            units = -(-self.NKB // 4)
            edge = [self.NKB * u // units for u in range(units + 1)]
            self.STEPS = [[(kb, j) for kb in range(edge[u], edge[u + 1])] for u in range(units) for j in range(4)]
        else:
            self.STEPS = [[(kb, j) for j in range(4)] for kb in range(self.NKB)]
        self.NS = NS = len(self.STEPS)
        assert self.NG * NS % NPROB == 0 and self.NG * NS % 2 == 0
        self.PARTS = [[(s, step.index((kb, j)), j) for j in range(4) for s, step in enumerate(self.STEPS) if (kb, j) in step]
                      for kb in range(self.NKB)]
        lag = 4 if L0 else 2
        self.AFTER = []
        for kb in range(self.NKB):
            if L0:
                u = max(i for i, e in enumerate(edge[:-1]) if e <= kb)
                self.AFTER.append(4 * u + lag + min(3, 4 * (kb - edge[u]) // (edge[u + 1] - edge[u])))
            else:
                self.AFTER.append(kb + lag)
        self.END = self.AFTER[-1] - NS
        self.AFTER = [max(at, self.END + 4 + kb // 3) for kb, at in enumerate(self.AFTER)]
        base = []
        for s in range(NS):
            work = [("prev", kb, 0) for kb in range(self.NKB) if self.AFTER[kb] == NS + s]
            work += [("own", kb, 0) for kb in range(self.NKB) if self.AFTER[kb] == s]
            work = [(w, kb, part) for w, kb, _ in work for part in (0, 1)]
            if s == 0:
                base += work + [("scores", s, 0), ("scores", s, 1)]
            else:
                base += [("scores", s, 0)] + work[:2] + [("scores", s, 1)] + work[2:]
            if s == self.END + 2:
                base[-1:-1] = [("turn", 0, 0)]
            if s == self.END + 3:
                base[-4:-4] = [("norm", 0, 0)]
                base[-2:-2] = [("norm", 0, 1)]
        place = lambda n: n * (len(base) - TAIL) / (self.NI - 1) if n < self.NI - 1 else len(base) - 1
        self.ORDER, n = [], 0
        for i, x in enumerate(base):
            while n < self.NI and place(n) <= i:
                self.ORDER.append(("item", n, 0))
                n += 1
            self.ORDER.append(x)
        assert n == self.NI

        assert late <= HALF

        shifts = -self.NI % NFIRST
        self.BANK = [(n + shifts * n // (self.NI - NFIRST) if n < self.NI - NFIRST else n - self.NI) % NFIRST
                     for n in range(self.NI)]

    def bank_before(self, n):
        earlier = [i for i in range(n) if self.BANK[i] == self.BANK[n]]
        if earlier:
            return 0, earlier[-1]
        return 1, max(i for i in range(self.NI) if self.BANK[i] == self.BANK[n])


NPROB = 8
NFIRST = 3
SLOTS = 4
TAIL = 8


def choose(eng, flag, general, short):
    value = eng.value_load(flag[0:1, 0:1], min_val=0, max_val=B * P)
    with eng.If(value > 0):
        general()
    with eng.Else():
        short()


def attention(nc, t, scratch, layer):
    L0 = layer == 0
    general = Plan(layer, 0, not L0)
    short = Plan(layer, SKIP0 if L0 else 0, False)
    NG, NKB, D, KH = general.NG, general.NKB, general.D, general.KH
    KEYS = NKB * P
    NJ = 4 * QB
    LOADS = 2 * len(COMBOS) + KH

    with ExitStack() as ctx:
        nm = f"a{layer}_"
        sb = lambda name, shape, dt: ctx.enter_context(nc.sbuf_tensor(nm + name, shape, dt))
        sem = lambda name: ctx.enter_context(nc.semaphore(nm + name))
        first_psum = ctx.enter_context(nc.psum_tensor(nm + "first", [P, NFIRST, 512], F32))
        second_psum = ctx.enter_context(nc.psum_tensor(nm + "second", [P, 2, 1024], F32))
        out_bank = ctx.enter_context(nc.psum_tensor(nm + "out", [P, 512], F32))
        out_psum, turn_psum = out_bank[:, 0:SQ], out_bank[:, SQ:].rearrange("p (a w) -> p a w", a=QB)

        keys = [sb(f"keys{i}", [P, KH, KEYS], BF16) for i in range(SLOTS)]
        queries = [sb(f"queries{i}", [P, 4, SQ], BF16) for i in range(SLOTS)]
        values_in = [sb(f"values_in{i}", [P, NKB, KH * D], F32) for i in range(2)]
        values = [sb(f"values{i}", [P, NKB, KH, 32], F32) for i in range(2)]
        probs = sb("probs", [P, NPROB, 1024], F32)
        maxima = sb("maxima", [P, NJ, general.CH], F32)
        m_all = sb("m_all", [P, NJ], F32)
        m_rest = sb("m_rest", [P, NJ], F32)
        m_cols = sb("m_cols", [P, NJ, 4], BF16)
        ident = sb("ident", [P, P], F32)
        ident_b = sb("ident_b", [P, P], BF16)
        out_T = sb("out_T", [P, SQ], F32)
        recip = sb("recip", [P, QB, 4], F32)
        out_n = sb("out_n", [P, 2, QB, 4 * D], F32)
        if not L0:
            mask_q = sb("mask_q", [P, QB, SC], F32)
            mask_k = sb("mask_k", [P, NKB, SQ], F32)
            mask_p = sb("mask_p", [P, 3, NKB, SQ], BF16)

        constants = sem("constants")
        loaded = [sem(f"loaded{i}") for i in range(SLOTS)]
        v_loaded = [sem(f"v_loaded{i}") for i in range(2)]
        v_placed = sem("v_placed")
        first_full = sem("first_full")
        first_free = sem("first_free")
        m_step = sem("m_step")
        m_rows = sem("m_rows")
        second_full = sem("second_full")
        probs_ready = sem("probs_ready")
        product = sem("product")
        out_read = sem("out_read")
        turned = sem("turned")
        recip_done = sem("recip_done")
        normed = sem("normed")
        stored = [sem(f"stored{i}") for i in range(2)]
        mask_in = sem("mask_in")
        mask_k_in = sem("mask_k_in")
        mask_step = sem("mask_step")
        MSTEPS = 4
        CONSTS = 10 + 2 * SLOTS if L0 else 11 + 4 * SLOTS
        flag = scratch[f"flag{layer}"]
        dst = scratch["attn0" if L0 else "attn1"]

        block = ctx.enter_context(nc.Block())

        @block.sync
        def _(sp):
            def program(p):
                def load(b, G):
                    n, k0 = G % SLOTS, p.first_kb * P
                    wait_at_least(sp, second_full, b, NG * p.NS, (G - SLOTS + 1) * p.NS)
                    if L0:
                        lo, o = 64 * (G % 2), G // 2
                        kp = scratch["kp0"][b, lo:lo + 64, o, :, k0:].rearrange("(j d) c k -> d c j k", d=D)
                        qp = scratch["qp0"][b, lo:lo + 64, o, :, :].rearrange("(j d) c q -> d c j q", d=D)
                    else:
                        lo, o = 32 * (G % 4), G // 4
                        kp = scratch["kp1"][b, D * G:D * G + D, :, :].rearrange("d c (a k) -> d c a k", a=1)
                        qp = scratch["qp1"][o, lo:lo + 32, :, bass.ds(b * SQ, SQ)].rearrange("(j d) c q -> d c j q", d=D)
                    for c, (qc, kc) in enumerate(COMBOS):
                        sp.dma_start(queries[n][D * c:D * c + D, :, :], qp[:, qc]).then_inc(loaded[n], 16)
                        sp.dma_start(keys[n][D * c:D * c + D, :, k0:], kp[:, kc]).then_inc(loaded[n], 16)
                    row = scratch["bias0"][bass.ds(b, 1), k0:] if L0 else scratch["bias1"]
                    for h in range(KH):
                        sp.dma_start(keys[n][EXTRA:EXTRA + 1, h, k0:], row).then_inc(loaded[n], 16)
                    wait_at_least(sp, v_placed, b, NG, G - 1)
                    v = scratch["v0"][b, :, p.first_kb:, 64 * G:64 * G + 64] if L0 else scratch["v1"][b, :, :, D * G:D * G + D]
                    sp.dma_start(values_in[G % 2][:, p.first_kb:, :], v).then_inc(v_loaded[G % 2], 16)

                def load_mask(b):
                    wait_at_least(sp, first_free, b, NG * p.NSI, 0)
                    sp.dma_start(mask_q[:], t["mask1"][b].rearrange("(a p) k -> p a k", p=P)).then_inc(mask_in, 16)

                def load_mask_k(b):
                    wait_at_least(sp, mask_step, b, MSTEPS, 0)
                    sp.dma_start(mask_k[:, 0:NKB - 1, :],
                                 t["mask1T"][b, 0:(NKB - 1) * P, :].rearrange("(a p) q -> p a q", p=P)).then_inc(mask_k_in, 16)
                    sp.dma_start(mask_k[0:SC - (NKB - 1) * P, NKB - 1, :], t["mask1T"][b, (NKB - 1) * P:SC, :]).then_inc(mask_k_in, 16)

                def store(b, G):
                    sp.wait_ge(normed, b * NG + G + 1)
                    sp.dma_start(dst[b, :, :, 4 * D * G:4 * D * G + 4 * D], out_n[:, G % 2, :, :]).then_inc(stored[G % 2], 16)

                if p.masked:
                    load_mask(0)
                    load_mask_k(0)
                for G in range(SLOTS - 1):
                    load(0, G)

                def body(b, first, last):
                    for G in range(NG):
                        ahead = G + SLOTS - 1
                        if p.masked and G == NG - 1 and not last:
                            load_mask(b + 1)
                        if p.masked and G == 1 and not last:
                            load_mask_k(b + 1)
                        if ahead < NG:
                            load(b, ahead)
                        elif not last:
                            load(b + 1, ahead - NG)
                        if G:
                            store(b, G - 1)
                        elif not first:
                            store(b - 1, NG - 1)
                each_batch(sp, body)
                store(B - 1, NG - 1)

            sp.wait_ge(constants, CONSTS)
            choose(sp, flag, lambda: program(general), lambda: program(short))
            for i in range(2):
                sp.wait_ge(stored[i], 16 * B * NG // 2)

        @block.gpsimd
        def _(pool):
            made = 0

            def constant(ins):
                nonlocal made
                made += 1
                ins.then_inc(constants, 1)
                pool.wait_ge(constants, made)

            for m in [m_cols, ident, ident_b] + values + ([] if L0 else keys + queries + [mask_k]):
                constant(pool.memset(m[:], 0.0))
            for n in range(SLOTS):
                constant(pool.memset(keys[n][EXTRA:KROWS, :, :], 1.0))
                constant(pool.memset(queries[n][EXTRA:EXTRA + 1, :, :], 1.0))
            for i in range(2):
                constant(pool.memset(values[i][:, :, :, D:D + 1], 1.0))
            constant(pool.memset(m_cols[:, :, 0:1], 1.0))
            for m in (ident, ident_b):
                constant(pool.affine_select(out=m[:], in_=m[:], compare_op=ALU.not_equal, fill=1.0, base=0,
                                            pattern=[[-1, P]], channel_multiplier=1))
            assert made == CONSTS

            def program(p):
                def place(b, G):
                    uses = NG // 2
                    pool.wait_ge(v_loaded[G % 2], 16 * (b * uses + G // 2 + 1))
                    wait_at_least(pool, product, b, NG * p.NKB, (G - 1) * p.NKB)
                    pool.nop(nofuse=True)
                    pool.tensor_copy(values[G % 2][:, p.first_kb:, :, 0:D],
                                     values_in[G % 2][:, p.first_kb:, :].rearrange("p k (h d) -> p k h d", h=KH)).then_inc(v_placed, 1)

                def split_mask(b):
                    pool.wait_ge(mask_k_in, 32 * (b + 1))
                    wait_at_least(pool, second_full, b, NG * p.NS, 0)
                    pool.nop(nofuse=True)
                    pool.tensor_copy(mask_p[:, 0], mask_k[:]).then_inc(mask_step, 1)
                    pool.wait_ge(mask_step, b * MSTEPS + 1)
                    pool.nop(nofuse=True)
                    pool.tensor_tensor(mask_k[:], mask_k[:], mask_p[:, 0], ALU.subtract).then_inc(mask_step, 1)
                    pool.wait_ge(mask_step, b * MSTEPS + 2)
                    pool.nop(nofuse=True)
                    pool.tensor_copy(mask_p[:, 1], mask_k[:]).then_inc(mask_step, 1)
                    pool.wait_ge(mask_step, b * MSTEPS + 3)
                    pool.nop(nofuse=True)
                    pool.tensor_tensor(mask_p[:, 2], mask_k[:], mask_p[:, 1], ALU.subtract).then_inc(mask_step, 1)

                def body(b, first, last):
                    for G in range(NG):
                        place(b, G)
                        if G == 0 and p.masked:
                            split_mask(b)
                each_batch(pool, body)

            choose(pool, flag, lambda: program(general), lambda: program(short))

        @block.tensor
        def _(pe):
            def program(p):
                def item(b, G, n):
                    kind, i = p.ITEMS[n]
                    slot, bank = G % SLOTS, p.BANK[n]
                    if n == 0:
                        pe.wait_ge(loaded[slot], 16 * LOADS * (b * (NG // SLOTS) + G // SLOTS + 1))
                    back, n0 = p.bank_before(n)
                    what, i0 = p.ITEMS[n0]
                    if what == "s":
                        wait_at_least(pe, first_free, b, NG * p.NSI, (G - back) * p.NSI + i0 + 1)
                    else:
                        wait_at_least(pe, m_rows, b, 2 * NG, 2 * (G - back) + i0 + 1)
                    if kind == "s":
                        j, rest = divmod(i, QB * p.CH)
                        qb, c = divmod(rest, p.CH)
                        nc.tensor.matmul(first_psum[:, bank, 0:p.cuts[c + 1] - p.cuts[c]],
                                         queries[slot][0:EXTRA + 1, j, qb * P:(qb + 1) * P],
                                         keys[slot][0:EXTRA + 1, j % KH, p.cuts[c]:p.cuts[c + 1]],
                                         start=True, stop=True).then_inc(first_full, 1)
                    else:
                        pe.wait_ge(m_step, (b * NG + G) * 2 * p.MS + (i + 1) * p.MS)
                        for k in range(NJ // 2):
                            mm = nc.tensor.matmul(first_psum[EXTRA:KROWS, bank, k * P:(k + 1) * P],
                                                  m_cols[:, i * NJ // 2 + k, :], ident_b[:], start=True, stop=True)
                        mm.then_inc(first_full, 1)

                def scores(b, G, s, part):
                    slot, step = G % SLOTS, p.STEPS[s]
                    if part == 0:
                        if s == 0 or (L0 and s == 2):
                            half = 2 if not L0 or s else 1
                            pe.wait_ge(m_rows, (b * NG + G) * 2 + half)
                        wait_at_least(pe, probs_ready, b, NG * p.NS, G * p.NS + s - 1)
                    unit = (G * p.NS + s) % 2
                    if L0:
                        half = -(-len(step) // 2)
                        for k in range(half) if part == 0 else range(half, len(step)):
                            kb, j = step[k]
                            k0 = (p.first_kb + kb) * P
                            mm = nc.tensor.matmul(second_psum[:, unit, k * SQ:(k + 1) * SQ], keys[slot][0:KROWS, j, k0:k0 + P],
                                                  queries[slot][0:KROWS, j, :], start=True, stop=True)
                    else:
                        if p.masked and G == 0 and s == 0 and part == 0:
                            pe.wait_ge(mask_step, (b + 1) * MSTEPS)
                        bank = second_psum[:, unit, 512 * part:512 * part + 512]
                        mm = nc.tensor.matmul(bank, keys[slot][0:KROWS, 0, s * P:(s + 1) * P],
                                              queries[slot][0:KROWS, 2 * part:2 * part + 2, :].rearrange("p a q -> p (a q)"),
                                              start=True, stop=not p.masked)
                        for pc in range(3 if p.masked else 0):
                            mm = nc.tensor.matmul(bank.rearrange("p (a q) -> p a q", a=2), ident_b[:],
                                                  mask_p[:, pc, s, :].unsqueeze(1).to_broadcast([P, 2, SQ]),
                                                  start=False, stop=(pc == 2))
                    if part == 1:
                        mm.then_inc(second_full, 1)

                def products(b, G, kb, part):
                    parts = p.PARTS[kb]
                    if part == 0:
                        if kb == 0:
                            pe.wait_ge(v_placed, b * NG + G + 1)
                            wait_at_least(pe, out_read, b, NG, G)
                            wait_at_least(pe, normed, b, NG, G)
                        pe.wait_ge(probs_ready, (b * NG + G) * p.NS + max(s for s, _, _ in parts) + 1)
                    for s, col, j in parts[2 * part:2 * part + 2]:
                        mm = nc.tensor.matmul(out_psum[32 * j:32 * j + 32, 0:SQ], values[G % 2][:, p.first_kb + kb, j % KH, :],
                                              probs[:, (G * p.NS + s) % NPROB, col * SQ:(col + 1) * SQ],
                                              start=(kb == 0), stop=(kb == p.NKB - 1))
                    if part == 1:
                        mm.then_inc(product, 1)

                def turn(b, G):
                    pe.wait_ge(out_read, b * NG + G + 1)
                    wait_at_least(pe, normed, b, NG, G)
                    for qb in range(QB):
                        mm = nc.tensor.transpose(turn_psum[:, qb, :], out_T[:, qb * P:(qb + 1) * P], ident[:])
                    mm.then_inc(turned, 1)

                for n in range(p.NI):
                    item(0, 0, n)

                def body(b, first, last):
                    for G in range(NG):
                        before = (b, G - 1) if G else (b - 1, NG - 1)
                        nxt = (b, G + 1) if G + 1 < NG else (b + 1, 0)
                        for what, i, part in p.ORDER:
                            if what == "scores":
                                scores(b, G, i, part)
                            elif what == "own":
                                products(b, G, i, part)
                            elif what == "item" and not (last and G == NG - 1):
                                item(*nxt, i)
                            elif what == "prev" and (G or not first):
                                products(*before, i, part)
                            elif what == "turn" and (G or not first):
                                turn(*before)
                each_batch(pe, body)
                for what, i, part in p.ORDER:
                    if what == "prev":
                        products(B - 1, NG - 1, i, part)
                turn(B - 1, NG - 1)

            pe.wait_ge(constants, CONSTS)
            choose(pe, flag, lambda: program(general), lambda: program(short))

        @block.scalar
        def _(act):
            def program(p):
                def rows(b, G, n):
                    half = p.ITEMS[n][1]
                    act.wait_ge(first_full, (b * NG + G) * p.NI + n + 1)
                    nc.scalar.copy(queries[G % SLOTS][EXTRA:KROWS, 2 * half:2 * half + 2, :].rearrange("p a q -> p (a q)"),
                                   first_psum[EXTRA:KROWS, p.BANK[n], :]).then_inc(m_rows, 1)

                def exps(b, G, s):
                    act.wait_ge(second_full, (b * NG + G) * p.NS + s + 1)
                    pg, ps = divmod(G * p.NS + s - NPROB, p.NS)
                    kb = max(kb for kb, parts in enumerate(p.PARTS) if any(part[0] == ps for part in parts))
                    wait_at_least(act, product, b, NG * p.NKB, pg * p.NKB + kb + 1)
                    cols = len(p.STEPS[s]) * SQ
                    nc.scalar.activation(probs[:, (G * p.NS + s) % NPROB, 0:cols], second_psum[:, (G * p.NS + s) % 2, 0:cols],
                                         ACT.Exp).then_inc(probs_ready, 1)

                def read_out(b, G):
                    act.wait_ge(product, (b * NG + G + 1) * p.NKB)
                    wait_at_least(act, turned, b, NG, G)
                    nc.scalar.copy(out_T[:], out_psum).then_inc(out_read, 1)

                M_ITEMS = [n for n, (kind, _) in enumerate(p.ITEMS) if kind == "m"]
                for n in M_ITEMS:
                    rows(0, 0, n)

                def body(b, first, last):
                    for G in range(NG):
                        before = (b, G - 1) if G else (b - 1, NG - 1)
                        nxt = (b, G + 1) if G + 1 < NG else (b + 1, 0)
                        for what, i, part in p.ORDER:
                            if what == "scores" and part == 1:
                                if i == p.END + 1 and (G or not first):
                                    read_out(*before)
                                exps(b, G, i)
                            elif what == "item" and i in M_ITEMS and not (last and G == NG - 1):
                                rows(*nxt, i)
                each_batch(act, body)
                read_out(B - 1, NG - 1)

            act.wait_ge(constants, CONSTS)
            choose(act, flag, lambda: program(general), lambda: program(short))

        @block.vector
        def _(dve):
            def program(p):
                def scores(b, G, n):
                    i = p.ITEMS[n][1]
                    jq, c = divmod(i, p.CH)
                    w = p.cuts[c + 1] - p.cuts[c]
                    if i == 0 and p.masked and G == 0:
                        dve.wait_ge(mask_in, 16 * (b + 1))
                    if i % p.HALF == 0:
                        wait_at_least(dve, m_step, b, NG * 2 * p.MS, (2 * (G - 1) + i // p.HALF) * p.MS + 1)
                    dve.wait_ge(first_full, (b * NG + G) * p.NI + n + 1)
                    bank = first_psum[:, p.BANK[n], 0:w]
                    if p.masked:
                        dve.nop(nofuse=True)
                        dve.tensor_tensor_reduce(bank, bank, mask_q[:, jq % QB, p.cuts[c]:p.cuts[c + 1]], 1.0, -3.0e38,
                                                 ALU.add, ALU.max, maxima[:, jq, c:c + 1]).then_inc(first_free, 1)
                    else:
                        dve.tensor_reduce(maxima[:, jq, c:c + 1], bank, AX.X, ALU.max).then_inc(first_free, 1)
                    if 0 <= i - p.HALF < p.MS:
                        pieces(b, G, 0, i - p.HALF)
                    if i == p.NSI - 1:
                        for k in range(p.MS):
                            pieces(b, G, 1, k)

                def pieces(b, G, half, k):
                    a = slice(half * NJ // 2, (half + 1) * NJ // 2)
                    m, rest, p1, p2, p3 = [x.unsqueeze(2) for x in (m_all[:, a], m_rest[:, a])] + \
                                          [m_cols[:, a, i:i + 1] for i in (1, 2, 3)]
                    if k == 0:
                        dve.wait_ge(first_free, (b * NG + G) * p.NSI + (half + 1) * p.HALF)
                    wait_at_least(dve, m_step, b, NG * 2 * p.MS, (G * 2 + half) * p.MS + k)
                    if k == 0:
                        ins = dve.tensor_reduce(m, maxima[:, a, 0:p.CH], AX.X, ALU.max)
                    elif k == 1:
                        ins = dve.tensor_scalar(p1, m, -1.0, None, ALU.mult)
                    elif k == 2:
                        ins = dve.tensor_tensor(rest, m, p1, ALU.add)
                    elif k == 3:
                        ins = dve.tensor_scalar(p2, rest, -1.0, None, ALU.mult)
                    elif k == 4:
                        ins = dve.tensor_tensor(m, rest, p2, ALU.add)
                    else:
                        ins = dve.tensor_scalar(p3, m, -1.0, None, ALU.mult)
                    ins.then_inc(m_step, 1)

                def norm(b, G, part):
                    out4 = turn_psum.rearrange("p a (j w) -> p a j w", w=32)
                    if part == 0:
                        dve.wait_ge(turned, b * NG + G + 1)
                        wait_at_least(dve, normed, b, NG, G)
                        dve.reciprocal(recip[:].unsqueeze(3), out4[:, :, :, D:D + 1]).then_inc(recip_done, 1)
                    else:
                        dve.wait_ge(recip_done, b * NG + G + 1)
                        wait_at_least(dve, stored[G % 2], b, 16 * (NG // 2), 16 * (G // 2))
                        dve.tensor_tensor(out_n[:, G % 2, :, :].rearrange("p a (j d) -> p a j d", d=D), out4[:, :, :, 0:D],
                                          recip[:].unsqueeze(3).to_broadcast([P, QB, 4, D]), ALU.mult).then_inc(normed, 1)

                S_ITEMS = [n for n, (kind, _) in enumerate(p.ITEMS) if kind == "s"]
                for n in S_ITEMS:
                    scores(0, 0, n)

                def body(b, first, last):
                    for G in range(NG):
                        before = (b, G - 1) if G else (b - 1, NG - 1)
                        nxt = (b, G + 1) if G + 1 < NG else (b + 1, 0)
                        for what, i, part in p.ORDER:
                            if what == "item" and i in S_ITEMS and not (last and G == NG - 1):
                                scores(*nxt, i)
                            elif what == "norm" and (G or not first):
                                norm(*before, part)
                each_batch(dve, body)
                norm(B - 1, NG - 1, 0)
                norm(B - 1, NG - 1, 1)

            dve.wait_ge(constants, CONSTS)
            choose(dve, flag, lambda: program(general), lambda: program(short))


CT = 4
NT = B * QB
NCH = NT // CT
NF = F // P


def identity(pool, tile, sem):
    pool.memset(tile[:], 0.0).then_inc(sem, 1)
    pool.wait_ge(sem, 1)
    pool.affine_select(out=tile[:], in_=tile[:], compare_op=ALU.not_equal, fill=1.0, base=0,
                       pattern=[[-1, P]], channel_multiplier=1).then_inc(sem, 1)


def middle(nc, t, scratch):
    ORDER = [("T", 0), ("O", 0), ("T", 1), ("O", 1), ("Y", 0), ("U", 0), ("T", 2), ("O", 2), ("Y", 1), ("D", 0),
             ("U", 1), ("X", 0), ("T", 3), ("O", 3), ("Y", 2), ("D", 1), ("Q", 0), ("U", 2), ("X", 1), ("Y", 3),
             ("D", 2), ("Q", 1), ("U", 3), ("X", 2), ("D", 3), ("Q", 2), ("X", 3), ("Q", 3)]
    TURNS = [x for x in ORDER if x[0] in "TYX"]
    turn_no = {x: i for i, x in enumerate(TURNS)}
    GELU_A, GELU_B = 0.7978845608028654, 0.044715
    SCALE = float(D1) ** -0.5

    def gelu_at(step, n):
        c, f = divmod(n, NF)
        if step == "inner":
            return c * 3 * NF + (3 * f + 1 if f else 2)
        return c * 3 * NF + min(3 * (f + 1) + 2, 3 * NF)

    with ExitStack() as ctx:
        sb = lambda name, shape, dt: ctx.enter_context(nc.sbuf_tensor("mid_" + name, shape, dt))
        sem = lambda name: ctx.enter_context(nc.semaphore("mid_" + name))
        psum = ctx.enter_context(nc.psum_tensor("mid_psum", [P, 8, 512], F32))
        turn_ps, proj_ps, up_ps, down_ps, q_ps = (psum[:, 0:2], psum[:, 2:4], psum[:, 4:6], psum[:, 6], psum[:, 7])
        w_o = sb("w_o", [P, HALVES, H], F32)
        w_1 = sb("w_1", [P, HALVES, F], F32)
        w_2 = sb("w_2", [P, NF, H], F32)
        w_q = sb("w_q", [P, HALVES, H], F32)
        b_o = sb("b_o", [P, H], F32)
        b_2 = sb("b_2", [P, H], F32)
        w_n = sb("w_n", [P, H], F32)
        b_1 = sb("b_1", [P, NF], F32)
        b_q = sb("b_q", [P, HALVES], F32)
        b_qs = sb("b_qs", [P, HALVES], F32)
        ident = sb("ident", [P, P], F32)
        attn = sb("attn", [P, NT, H], F32)
        x_o = sb("x_o", [P, NT, H], F32)
        x_2 = sb("x_2", [P, NT, H], F32)
        x_1 = sb("x_1", [P, NT, H], F32)
        turned = {"T": sb("attn_T", [P, 2, HALVES, 512], F32), "Y": sb("norm_T", [P, 2, HALVES, 512], F32),
                  "X": sb("x_1_T", [P, 2, HALVES, 512], F32)}
        hidden = sb("hidden", [P, 2, NF, 512], F32)
        up = sb("up", [P, 2, 512], F32)
        cubic = sb("cubic", [P, 2, 512], F32)
        sumsq = sb("sumsq", [P, NT], F32)
        square = sb("square", [P, H], F32)
        rms = sb("rms", [P, NT], F32)
        qf = sb("qf", [P, 512], F32)
        q_pc = sb("q_pc", [P, 2, HALVES, 3, 512], BF16)
        mask = sb("mask", [P, 2, SC], F32)
        mask_sums = sb("mask_sums", [P, NT], F32)
        mask_any = sb("mask_any", [P, 2], F32)
        ones = sb("ones", [P, 1], F32)
        flag = sb("flag", [1, 1], I32)

        mask_in = [sem(f"mask_in{i}") for i in range(2)]
        mask_seen, flag_step, flag_sum, flag_done = sem("mask_seen"), sem("flag_step"), sem("flag_sum"), sem("flag_done")
        flag_stored = sem("flag_stored")
        weights_in, x_in, attn_in = sem("weights_in"), sem("x_in"), sem("attn_in")
        ident_done, bias_step = sem("ident_done"), sem("bias_step")
        x_step = sem("x_step")
        turn_full, turn_read = sem("turn_full"), sem("turn_read")
        proj_full, proj_read = sem("proj_full"), sem("proj_read")
        up_full, up_read = sem("up_full"), sem("up_read")
        down_full, down_read = sem("down_full"), sem("down_read")
        q_full, q_read = sem("q_full"), sem("q_read")
        norm_step, root, gelu_step, tanh_done = sem("norm_step"), sem("root"), sem("gelu_step"), sem("tanh_done")
        q_step, x_stored = sem("q_step"), sem("x_stored")
        q_stored = [sem(f"q_stored{i}") for i in range(2)]
        NSTEPS = 2 * CT + 2 + CT
        W = 9

        with nc.Block() as block:
            @block.sync
            def _(sp):
                row = lambda name: t[name].rearrange("(a n) -> a n", a=1).to_broadcast([P, H])
                sp.dma_start(attn[:].rearrange("p (b a) h -> p b (a h)", a=QB), scratch["attn0"].rearrange("b p a h -> p b (a h)")).then_inc(attn_in, 16)
                sp.dma_start(x_2[:], t["x"].rearrange("b (a p) h -> p (b a) h", p=P)).then_inc(x_in, 16)
                for dst, src in ((w_o, t["ow0"]), (w_1, t["w1"]), (w_2, t["w2"]), (w_q, t["qw1"])):
                    sp.dma_start(dst[:], src.rearrange("(i p) n -> p i n", p=P)).then_inc(weights_in, 16)
                sp.dma_start(b_o[:], row("ob0")).then_inc(weights_in, 16)
                sp.dma_start(b_2[:], row("b2")).then_inc(weights_in, 16)
                sp.dma_start(w_n[:], row("nw")).then_inc(weights_in, 16)
                sp.dma_start(b_1[:], t["b1"]).then_inc(weights_in, 16)
                sp.dma_start(b_q[:], t["qb1"]).then_inc(weights_in, 16)
                for n in range(NT):
                    if n >= 2:
                        sp.wait_ge(mask_seen, n - 1)
                    sp.dma_start(mask[:, n % 2], t["mask1"][n // QB, n % QB * P:(n % QB + 1) * P, :]).then_inc(mask_in[n % 2], 16)
                for c in range(NCH):
                    sp.wait_ge(q_step, (c + 1) * HALVES * 3)
                    sp.wait_ge(q_read, (c + 1) * HALVES * 2)
                    for o in range(HALVES):
                        sp.dma_start(scratch["qp1"][o, :, :, c * 512:(c + 1) * 512], q_pc[:, c % 2, o]).then_inc(q_stored[c % 2], 16)
                sp.wait_ge(down_read, NT)
                sp.dma_start(scratch["x1"].rearrange("b p a h -> p b (a h)"), x_1[:].rearrange("p (b a) h -> p b (a h)", a=QB)).then_inc(x_stored, 16)
                for i in range(2):
                    sp.wait_ge(q_stored[i], 16 * HALVES * NCH // 2)
                sp.wait_ge(x_stored, 16)
                sp.wait_ge(flag_done, 1)
                sp.dma_start(scratch["flag1"], flag[:]).then_inc(flag_stored, 16)
                sp.wait_ge(flag_stored, 16)

            @block.gpsimd
            def _(pool):
                identity(pool, ident, ident_done)
                pool.wait_ge(weights_in, 16 * W)
                pool.wait_ge(x_in, 16)
                for T in range(NT):
                    pool.tensor_tensor(x_o[:, T], x_2[:, T], b_o[:], ALU.add).then_inc(x_step, 1)
                pool.wait_ge(x_step, NT)
                for T in range(NT):
                    pool.tensor_tensor(x_2[:, T], x_2[:, T], b_2[:], ALU.add).then_inc(x_step, 1)

            @block.tensor
            def _(pe):
                pe.wait_ge(ident_done, 2)
                pe.wait_ge(attn_in, 16)
                pe.wait_ge(weights_in, 16 * W)
                src = {"T": attn, "Y": attn, "X": x_1}
                for kind, c in ORDER:
                    if kind in "TYX":
                        if kind == "Y":
                            pe.wait_ge(norm_step, (c + 1) * NSTEPS)
                        if kind == "X":
                            pe.wait_ge(down_read, (c + 1) * CT)
                        for k in range(CT):
                            n = turn_no[kind, c] * CT + k
                            if n >= 2:
                                pe.wait_ge(turn_read, n - 1)
                            for i in range(HALVES):
                                mm = nc.tensor.transpose(turn_ps[:, n % 2, i * P:(i + 1) * P],
                                                         src[kind][:, c * CT + k, i * P:(i + 1) * P], ident[:])
                            mm.then_inc(turn_full, 1)
                    if kind == "O":
                        pe.wait_ge(turn_read, (turn_no["T", c] + 1) * CT)
                        for k in range(CT):
                            n = c * CT + k
                            if n >= 2:
                                pe.wait_ge(proj_read, n - 1)
                            for i in range(HALVES):
                                mm = nc.tensor.matmul(proj_ps[:, n % 2, 0:H], turned["T"][:, c % 2, i, k * P:(k + 1) * P],
                                                      w_o[:, i, :], start=(i == 0), stop=(i == HALVES - 1))
                            mm.then_inc(proj_full, 1)
                    if kind == "U":
                        pe.wait_ge(turn_read, (turn_no["Y", c] + 1) * CT)
                        for f in range(NF):
                            n = c * NF + f
                            if n >= 2:
                                pe.wait_ge(up_read, 2 * (n - 1))
                            for i in range(HALVES):
                                mm = nc.tensor.matmul(up_ps[:, n % 2, :], w_1[:, i, f * P:(f + 1) * P],
                                                      turned["Y"][:, c % 2, i, :], start=(i == 0), stop=(i == HALVES - 1))
                            mm.then_inc(up_full, 1)
                    if kind == "D":
                        pe.wait_ge(gelu_step, (c + 1) * NF * 3)
                        for k in range(CT):
                            n = c * CT + k
                            if n >= 1:
                                pe.wait_ge(down_read, n)
                            for f in range(NF):
                                mm = nc.tensor.matmul(down_ps[:, 0:H], hidden[:, c % 2, f, k * P:(k + 1) * P], w_2[:, f, :],
                                                      start=(f == 0), stop=(f == NF - 1))
                            mm.then_inc(down_full, 1)
                    if kind == "Q":
                        pe.wait_ge(turn_read, (turn_no["X", c] + 1) * CT)
                        for o in range(HALVES):
                            n = c * HALVES + o
                            if n >= 1:
                                pe.wait_ge(q_read, 2 * n)
                            for i in range(HALVES):
                                mm = nc.tensor.matmul(q_ps[:, :], w_q[:, i, o * P:(o + 1) * P], turned["X"][:, c % 2, i, :],
                                                      start=(i == 0), stop=(i == HALVES - 1))
                            mm.then_inc(q_full, 1)
                pe.wait_ge(flag_step, 3)
                pe.wait_ge(q_read, 2 * HALVES * NCH)
                nc.tensor.matmul(q_ps[0:1, 0:1], mask_any[:, 1:2], ones[:], start=True, stop=True).then_inc(flag_sum, 1)

            @block.scalar
            def _(act):
                def see_mask(n):
                    act.wait_ge(mask_in[n % 2], 16 * (n // 2 + 1))
                    nc.scalar.activation(mask[:, n % 2], mask[:, n % 2], ACT.Abs,
                                         accum_out=mask_sums[:, n:n + 1]).then_inc(mask_seen, 1)

                act.wait_ge(weights_in, 16 * W)
                act.wait_ge(bias_step, 1)
                for kind, c in ORDER:
                    if kind == "O":
                        act.wait_ge(norm_step, c * NSTEPS + 2 * CT + 1)
                        nc.scalar.activation(rms[:, c * CT:(c + 1) * CT], rms[:, c * CT:(c + 1) * CT], ACT.Sqrt).then_inc(root, 1)
                    if kind == "U":
                        for f in range(NF + 1):
                            n = c * NF + f
                            if f < NF:
                                act.wait_ge(up_full, n + 1)
                                if n >= 2:
                                    act.wait_ge(gelu_step, gelu_at("last", n - 2))
                                nc.scalar.activation(up[:, n % 2], up_ps[:, n % 2], ACT.Identity,
                                                     bias=b_1[:, f:f + 1]).then_inc(up_read, 1)
                                nc.scalar.activation(cubic[:, n % 2], up_ps[:, n % 2], ACT.Square,
                                                     bias=b_1[:, f:f + 1]).then_inc(up_read, 1)
                            if f:
                                act.wait_ge(gelu_step, gelu_at("inner", n - 1))
                                nc.scalar.activation(cubic[:, (n - 1) % 2], cubic[:, (n - 1) % 2], ACT.Tanh,
                                                     scale=GELU_A).then_inc(tanh_done, 1)
                            if f % 2 == 1 and (n // 2) < NT:
                                see_mask(n // 2)
                    if kind == "Q":
                        for o in range(HALVES):
                            n = c * HALVES + o
                            act.wait_ge(q_full, n + 1)
                            if n >= 1:
                                act.wait_ge(q_step, 3 * n)
                            if c >= 2 and o == 0:
                                act.wait_ge(q_stored[c % 2], 16 * HALVES * (c // 2))
                            nc.scalar.activation(qf[:], q_ps[:, :], ACT.Identity, bias=b_qs[:, o:o + 1],
                                                 scale=SCALE).then_inc(q_read, 1)
                            nc.scalar.activation(q_pc[:, c % 2, o, 0], q_ps[:, :], ACT.Identity, bias=b_qs[:, o:o + 1],
                                                 scale=SCALE).then_inc(q_read, 1)

            @block.vector
            def _(dve):
                dve.wait_ge(weights_in, 16 * W)
                dve.tensor_scalar(b_qs[:], b_q[:], SCALE, None, ALU.mult).then_inc(bias_step, 1)

                def norm(c):
                    a, base = slice(c * CT, (c + 1) * CT), c * NSTEPS
                    for k in range(CT):
                        T = c * CT + k
                        dve.wait_ge(proj_full, T + 1)
                        dve.wait_ge(x_step, T + 1)
                        dve.wait_ge(turn_full, (turn_no["T", c] + 1) * CT)
                        dve.tensor_tensor(attn[:, T], proj_ps[:, T % 2, 0:H], x_o[:, T], ALU.add).then_inc(proj_read, 1)
                        dve.wait_ge(proj_read, T + 1)
                        if T:
                            dve.wait_ge(norm_step, base + 2 * k if k else base)
                        dve.tensor_tensor_reduce(square[:], attn[:, T], attn[:, T], 1.0, 0.0, ALU.mult, ALU.add,
                                                 sumsq[:, T:T + 1]).then_inc(norm_step, 2)
                    dve.wait_ge(norm_step, base + 2 * CT)
                    dve.tensor_scalar(rms[:, a], sumsq[:, a], 1.0 / H, EPS, ALU.mult, ALU.add).then_inc(norm_step, 1)
                    dve.wait_ge(root, c + 1)
                    dve.reciprocal(sumsq[:, a], rms[:, a]).then_inc(norm_step, 1)
                    dve.wait_ge(norm_step, base + 2 * CT + 2)
                    for k in range(CT):
                        T = c * CT + k
                        dve.scalar_tensor_tensor(out=attn[:, T], in0=attn[:, T], scalar=sumsq[:, T:T + 1], in1=w_n[:],
                                                 op0=ALU.mult, op1=ALU.mult).then_inc(norm_step, 1)

                for kind, c in ORDER:
                    if kind in "TYX":
                        for k in range(CT):
                            n = turn_no[kind, c] * CT + k
                            dve.wait_ge(turn_full, n + 1)
                            dve.tensor_copy(turned[kind][:, c % 2, :, k * P:(k + 1) * P],
                                            turn_ps[:, n % 2, 0:H].rearrange("p (i q) -> p i q", i=HALVES)).then_inc(turn_read, 1)
                    if kind == "O":
                        norm(c)
                    if kind == "U":
                        for f in range(NF + 1):
                            n = c * NF + f
                            if f < NF:
                                buf = n % 2
                                dve.wait_ge(up_read, 2 * (n + 1))
                                dve.tensor_scalar(cubic[:, buf], cubic[:, buf], GELU_B, 1.0, ALU.mult, ALU.add).then_inc(gelu_step, 1)
                                dve.wait_ge(gelu_step, gelu_at("inner", n) - 1)
                                dve.tensor_tensor(cubic[:, buf], cubic[:, buf], up[:, buf], ALU.mult).then_inc(gelu_step, 1)
                            if f:
                                m = n - 1
                                dve.wait_ge(tanh_done, m + 1)
                                dve.scalar_tensor_tensor(out=hidden[:, c % 2, f - 1], in0=cubic[:, m % 2], scalar=1.0,
                                                         in1=up[:, m % 2], op0=ALU.add, op1=ALU.mult).then_inc(gelu_step, 1)
                    if kind == "D":
                        for k in range(CT):
                            T = c * CT + k
                            dve.wait_ge(down_full, T + 1)
                            dve.wait_ge(x_step, NT + T + 1)
                            dve.scalar_tensor_tensor(out=x_1[:, T], in0=down_ps[:, 0:H], scalar=0.5, in1=x_2[:, T],
                                                     op0=ALU.mult, op1=ALU.add).then_inc(down_read, 1)
                    if kind == "Q":
                        for o in range(HALVES):
                            n = c * HALVES + o
                            pc = lambda i: q_pc[:, c % 2, o, i]
                            dve.wait_ge(q_read, 2 * (n + 1))
                            dve.tensor_tensor(qf[:], qf[:], pc(0), ALU.subtract).then_inc(q_step, 1)
                            dve.wait_ge(q_step, 3 * n + 1)
                            dve.tensor_copy(pc(1), qf[:]).then_inc(q_step, 1)
                            dve.wait_ge(q_step, 3 * n + 2)
                            dve.tensor_tensor(pc(2), qf[:], pc(1), ALU.subtract).then_inc(q_step, 1)
                dve.memset(ones[:], 1.0).then_inc(flag_step, 1)
                dve.wait_ge(mask_seen, NT)
                dve.tensor_reduce(mask_any[:, 0:1], mask_sums[:], AX.X, ALU.add).then_inc(flag_step, 1)
                dve.wait_ge(flag_step, 2)
                dve.tensor_scalar(mask_any[:, 1:2], mask_any[:, 0:1], 0.0, None, ALU.not_equal).then_inc(flag_step, 1)
                dve.wait_ge(flag_sum, 1)
                dve.tensor_copy(flag[:], q_ps[0:1, 0:1]).then_inc(flag_done, 1)


def finish(nc, t, scratch, out):
    with ExitStack() as ctx:
        sb = lambda name, shape, dt: ctx.enter_context(nc.sbuf_tensor("fin_" + name, shape, dt))
        sem = lambda name: ctx.enter_context(nc.semaphore("fin_" + name))
        psum = ctx.enter_context(nc.psum_tensor("fin_psum", [P, 8, 512], F32))
        w_o = sb("w_o", [P, HALVES, H], F32)
        b_o, gamma, beta = sb("b_o", [P, H], F32), sb("gamma", [P, H], F32), sb("beta", [P, H], F32)
        ident = sb("ident", [P, P], F32)
        attn = sb("attn", [P, NT, H], F32)
        x_1 = sb("x_1", [P, NT, H], F32)
        y = sb("y", [P, NT, H], F32)
        attn_T = sb("attn_T", [P, 4, HALVES, P], F32)
        stats = sb("stats", [P, NT, 6], F32)
        mean_var = sb("mean_var", [P, NT, 2], F32)
        std = sb("std", [P, NT], F32)
        weights_in, attn_in, x_in, ident_done = sem("weights_in"), sem("attn_in"), sem("x_in"), sem("ident_done")
        x_step, turn_full, turn_read = sem("x_step"), sem("turn_full"), sem("turn_read")
        proj_full, proj_read, stat_step, root = sem("proj_full"), sem("proj_read"), sem("stat_step"), sem("root")
        norm_step, scaled, stored = sem("norm_step"), sem("scaled"), sem("stored")

        with nc.Block() as block:
            @block.sync
            def _(sp):
                sp.dma_start(attn[:].rearrange("p (b a) h -> p b (a h)", a=QB), scratch["attn1"].rearrange("b p a h -> p b (a h)")).then_inc(attn_in, 16)
                sp.dma_start(w_o[:], t["ow1"].rearrange("(i p) n -> p i n", p=P)).then_inc(weights_in, 16)
                for dst, name in ((b_o, "ob1"), (gamma, "gamma"), (beta, "beta")):
                    sp.dma_start(dst[:], t[name].rearrange("(a n) -> a n", a=1).to_broadcast([P, H])).then_inc(weights_in, 16)
                sp.dma_start(x_1[:].rearrange("p (b a) h -> p b (a h)", a=QB), scratch["x1"].rearrange("b p a h -> p b (a h)")).then_inc(x_in, 16)
                for b in range(B):
                    sp.wait_ge(scaled, 2 * QB * (b + 1))
                    sp.dma_start(out[b].rearrange("(a p) h -> p a h", p=P), y[:, b * QB:(b + 1) * QB]).then_inc(stored, 16)
                sp.wait_ge(stored, 16 * B)

            @block.gpsimd
            def _(pool):
                identity(pool, ident, ident_done)
                pool.wait_ge(weights_in, 64)
                pool.wait_ge(x_in, 16)
                for T in range(NT):
                    pool.tensor_tensor(x_1[:, T], x_1[:, T], b_o[:], ALU.add).then_inc(x_step, 1)

            @block.tensor
            def _(pe):
                pe.wait_ge(ident_done, 2)
                pe.wait_ge(attn_in, 16)
                pe.wait_ge(weights_in, 64)
                for T in range(NT + 1):
                    if T < NT:
                        if T >= 4:
                            pe.wait_ge(turn_read, T - 3)
                        for i in range(HALVES):
                            mm = nc.tensor.transpose(psum[:, T % 4, i * P:(i + 1) * P], attn[:, T, i * P:(i + 1) * P], ident[:])
                        mm.then_inc(turn_full, 1)
                    if T:
                        n = T - 1
                        pe.wait_ge(turn_read, n + 1)
                        if n >= 4:
                            pe.wait_ge(proj_read, n - 3)
                        for i in range(HALVES):
                            mm = nc.tensor.matmul(psum[:, 4 + n % 4, 0:H], attn_T[:, n % 4, i, :], w_o[:, i, :],
                                                  start=(i == 0), stop=(i == HALVES - 1))
                        mm.then_inc(proj_full, 1)

            @block.scalar
            def _(act):
                for T in range(NT):
                    act.wait_ge(turn_full, T + 1)
                    if T >= 4:
                        act.wait_ge(proj_full, T - 3)
                    nc.scalar.copy(attn_T[:, T % 4].rearrange("p i q -> p (i q)"), psum[:, T % 4, 0:H]).then_inc(turn_read, 1)
                act.wait_ge(stat_step, 2 * NT + 1)
                nc.scalar.activation(std[:], std[:], ACT.Sqrt).then_inc(root, 1)

            @block.vector
            def _(dve):
                for T in range(NT):
                    dve.wait_ge(proj_full, T + 1)
                    dve.wait_ge(x_step, T + 1)
                    dve.tensor_tensor(y[:, T], psum[:, 4 + T % 4, 0:H], x_1[:, T], ALU.add).then_inc(proj_read, 1)
                    dve.wait_ge(proj_read, T + 1)
                    dve.bn_stats(stats[:, T], y[:, T]).then_inc(stat_step, 1)
                    dve.wait_ge(stat_step, 2 * T + 1)
                    dve.bn_aggr(mean_var[:, T], stats[:, T]).then_inc(stat_step, 1)
                dve.wait_ge(stat_step, 2 * NT)
                dve.tensor_scalar(std[:].unsqueeze(2), mean_var[:, :, 1:2], EPS, None, ALU.add).then_inc(stat_step, 1)
                dve.wait_ge(root, 1)
                dve.reciprocal(std[:], std[:]).then_inc(norm_step, 1)
                dve.wait_ge(norm_step, 1)
                for T in range(NT):
                    dve.tensor_scalar(y[:, T], y[:, T], mean_var[:, T, 0:1], std[:, T:T + 1], ALU.subtract, ALU.mult)\
                       .then_inc(norm_step, 1)
                    dve.wait_ge(norm_step, T + 2)
                    dve.tensor_tensor(y[:, T], y[:, T], gamma[:], ALU.mult).then_inc(scaled, 1)
                    dve.wait_ge(scaled, 2 * T + 1)
                    dve.tensor_tensor(y[:, T], y[:, T], beta[:], ALU.add).then_inc(scaled, 1)


def build(nc, t, out):
    dram = lambda name, shape, dt: nc.dram_tensor(name, shape, dt, kind="Internal").ap()
    scratch = {
        "kp0": dram("kp0", (B, P, HALVES, 3, K0), BF16),
        "qp0": dram("qp0", (B, P, HALVES, 3, SQ), BF16),
        "kp1": dram("kp1", (B, KV1, 3, K1), BF16),
        "qp1": dram("qp1", (HALVES, P, 3, B * SQ), BF16),
        "v0": dram("v0", (B, P, NKB0, H), F32),
        "v1": dram("v1", (B, P, NKB1, KV1), F32),
        "bias0": dram("bias0_rows", (B, K0), BF16),
        "bias1": dram("bias1_row", (1, K1), BF16),
        "attn0": dram("attn0", (B, P, QB, H), F32),
        "attn1": dram("attn1", (B, P, QB, H), F32),
        "x1": dram("x1", (B, P, QB, H), F32),
        "flag0": dram("flag0", (1, 1), I32),
        "flag1": dram("flag1", (1, 1), I32),
    }
    project_inputs(nc, t, scratch)
    attention(nc, t, scratch, 0)
    middle(nc, t, scratch)
    attention(nc, t, scratch, 1)
    finish(nc, t, scratch, out)


def kernel(**inputs):
    import numpy as np
    import concourse.bacc as bacc
    from concourse.bass_utils import run_bass_kernel_spmd

    a = {name: np.asarray(v) for name, v in inputs.items()}
    kw = a["L0_xattn_kv_w"].reshape(H, H, 2)
    kb = a["L0_xattn_kv_b"].reshape(H, 2)
    column = lambda v: v.reshape(-1, P).T
    laid = {
        "x": a["x"], "xT": a["x"].transpose(0, 2, 1), "ctxT": a["ctx_2048"].transpose(0, 2, 1),
        "mask0": a["mask_BxS2_ik0"], "mask1": a["mask_Bx1xSxS2_ff0"][:, 0], "mask1T": a["mask_Bx1xSxS2_ff0"][:, 0].transpose(0, 2, 1),
        "qw0": a["L0_xattn_q_w"], "qb0": column(a["L0_xattn_q_b"]), "kw0": kw[:, :, 0], "vw0": kw[:, :, 1],
        "kb0": column(kb[:, 0]), "vb0": kb[:, 1], "ow0": a["L0_xattn_out_w"], "ob0": a["L0_xattn_out_b"],
        "nw": a["L0_xattn_postnorm_w"], "w1": a["L0_xattn_mlp_w1"], "b1": column(a["L0_xattn_mlp_b1"]),
        "w2": a["L0_xattn_mlp_w2"], "b2": a["L0_xattn_mlp_b2"],
        "qw1": a["L1_xattn_Wq"], "qb1": column(a["L1_xattn_bq"]), "kw1": a["L1_xattn_Wk"], "kb1": a["L1_xattn_bk"][:, None],
        "vw1": a["L1_xattn_Wv"], "vb1": a["L1_xattn_bv"], "ow1": a["L1_xattn_Wo"], "ob1": a["L1_xattn_bo"],
        "gamma": a["L1_xattn_gamma"], "beta": a["L1_xattn_beta"],
    }
    nc = bacc.Bacc("TRN2", target_bir_lowering=False, num_devices=1)
    arrays, t = {}, {}
    for name, v in laid.items():
        arrays[f"in_{name}"] = np.ascontiguousarray(v)
        t[name] = nc.dram_tensor(f"in_{name}", v.shape, mybir.dt.from_np(v.dtype), kind="ExternalInput").ap()
    out = nc.dram_tensor("out_0", (B, SQ, H), F32, kind="ExternalOutput").ap()
    build(nc, t, out)
    r = run_bass_kernel_spmd(nc, [arrays], core_ids=[0])
    return r.results[0]["out_0"]
```

```python
from contextlib import ExitStack

import concourse.bass as bass
from concourse import mybir

F32 = mybir.dt.float32
BF16 = mybir.dt.bfloat16
I32 = mybir.dt.int32
ALU = mybir.AluOpType
ACT = mybir.ActivationFunctionType
AX = mybir.AxisListType

P = 128
B, SQ, H, SC = 8, 256, 256, 1601
HALVES = H // P
QB = SQ // P
F = 4 * H
EPS = 1e-6

NKB0 = -(-(SC + SQ) // P)
NKB1 = -(-SC // P)
K0, K1 = NKB0 * P, NKB1 * P
SKIP0 = 9
G0, G1 = 4, 8
D0, D1 = 16, 8
KV1 = H // 4
VW = H + KV1
NEG = -1.0e30

COMBOS = [(0, 0), (0, 1), (1, 0), (1, 1), (0, 2), (2, 0)]
EXTRA = 96
KROWS = 100


def each_batch(eng, body):
    body(0, True, False)
    with eng.Fori(1, B - 1) as b:
        body(b, False, False)
    body(B - 1, False, True)


def wait_at_least(eng, sem, b, per_batch, count):
    if isinstance(b, int):
        if b * per_batch + count > 0:
            eng.wait_ge(sem, b * per_batch + count)
    else:
        eng.wait_ge(sem, b * per_batch + count)


def project_inputs(nc, t, scratch):
    def items():
        out = []
        for o in range(HALVES):
            for c in range(0, K0, 512):
                out.append(("k0", o, c, min(512, K0 - c)))
        for c in range(0, K1, 512):
            out.append(("k1", 0, c, min(512, K1 - c)))
        for o in range(HALVES):
            out.append(("q0", o, SC, SQ))
        return out
    ITEMS = items()
    NI = len(ITEMS)
    PB = 4

    with ExitStack() as ctx:
        sb = lambda name, shape, dt: ctx.enter_context(nc.sbuf_tensor(name, shape, dt))
        sem = lambda name: ctx.enter_context(nc.semaphore(name))
        psum = ctx.enter_context(nc.psum_tensor("proj_psum", [P, 8, 512], F32))
        w_k0 = sb("w_k0", [P, HALVES, H], F32)
        w_q0 = sb("w_q0", [P, HALVES, H], F32)
        w_k1 = sb("w_k1", [P, HALVES, KV1], F32)
        w_v = sb("w_v", [P, HALVES, VW], F32)
        b_k0 = sb("b_k0", [P, HALVES], F32)
        b_q0 = sb("b_q0", [P, HALVES], F32)
        b_q0s = sb("b_q0s", [P, HALVES], F32)
        b_k1 = sb("b_k1", [KV1, 1], F32)
        b_v = sb("b_v", [P, VW], F32)
        hT = [sb(f"hT{i}", [P, HALVES, K0], F32) for i in range(2)]
        pc_k0 = [sb(f"pc_k0_{i}", [P, HALVES, 3, K0], BF16) for i in range(2)]
        pc_k1 = [sb(f"pc_k1_{i}", [KV1, 3, K1], BF16) for i in range(2)]
        pc_q0 = [sb(f"pc_q0_{i}", [P, HALVES, 3, SQ], BF16) for i in range(2)]
        vals = [sb(f"vals{i}", [P, NKB0, VW], F32) for i in range(2)]
        xf = sb("xf", [P, 4, 512], F32)
        r1 = sb("r1", [P, 2, 512], F32)
        mask_i = sb("mask_i", [B, SC], I32)
        mask_f = sb("mask_f", [B, SC], F32)
        bias0 = sb("bias0", [B, K0], BF16)
        bias1 = sb("bias1", [1, K1], BF16)
        attended = sb("attended", [B, SKIP0 * P], BF16)
        any_row = sb("any_row", [B, 1], F32)
        ones = sb("ones", [B, 1], F32)
        flag = sb("flag", [1, 1], I32)

        weights_in = sem("proj_weights_in")
        hT_in = [sem(f"proj_hT_in{i}") for i in range(2)]
        pads_zero = sem("proj_pads_zero")
        item_psum = sem("proj_item_psum")
        item_read = sem("proj_item_read")
        val_psum = sem("proj_val_psum")
        val_read = sem("proj_val_read")
        piece_step = sem("proj_piece_step")
        bias_done = sem("proj_bias_done")
        qbias = sem("proj_qbias")
        stored = [sem(f"proj_stored{i}") for i in range(2)]
        bias_stored = sem("proj_bias_stored")
        flag_rows, flag_sum, flag_done = sem("proj_flag_rows"), sem("proj_flag_sum"), sem("proj_flag_done")
        STEPS = 4
        STORES = 6

        def rows(kind):
            return KV1 if kind == "k1" else P

        def piece(b, kind, o, pc, c, n):
            if kind == "k0":
                return pc_k0[b % 2][:, o, pc, c:c + n]
            if kind == "k1":
                return pc_k1[b % 2][:, pc, c:c + n]
            return pc_q0[b % 2][:, o, pc, :]

        with nc.Block() as block:
            @block.sync
            def _(sp):
                for dst, src in ((w_k0, t["kw0"]), (w_q0, t["qw0"]), (w_k1, t["kw1"])):
                    sp.dma_start(dst[:], src.rearrange("(i p) n -> p i n", p=P)).then_inc(weights_in, 16)
                sp.dma_start(w_v[:, :, 0:H], t["vw0"].rearrange("(i p) n -> p i n", p=P)).then_inc(weights_in, 16)
                sp.dma_start(w_v[:, :, H:VW], t["vw1"].rearrange("(i p) n -> p i n", p=P)).then_inc(weights_in, 16)
                sp.dma_start(b_k0[:], t["kb0"]).then_inc(weights_in, 16)
                sp.dma_start(b_q0[:], t["qb0"]).then_inc(weights_in, 16)
                sp.dma_start(b_k1[:], t["kb1"]).then_inc(weights_in, 16)
                sp.dma_start(b_v[:, 0:H], t["vb0"].rearrange("(a n) -> a n", a=1).to_broadcast([P, H])).then_inc(weights_in, 16)
                sp.dma_start(b_v[:, H:VW], t["vb1"].rearrange("(a n) -> a n", a=1).to_broadcast([P, KV1])).then_inc(weights_in, 16)
                sp.dma_start(mask_i[:], t["mask0"]).then_inc(weights_in, 16)

                def load(b):
                    if b >= 2:
                        sp.wait_ge(val_psum, (b - 1) * NKB0)
                        sp.wait_ge(item_psum, (b - 1) * NI)
                    for i in range(HALVES):
                        sp.dma_start(hT[b % 2][:, i, 0:SC], t["ctxT"][b, i * P:(i + 1) * P, :]).then_inc(hT_in[b % 2], 16)
                        sp.dma_start(hT[b % 2][:, i, SC:SC + SQ], t["xT"][b, i * P:(i + 1) * P, :]).then_inc(hT_in[b % 2], 16)
                load(0)
                load(1)
                for b in range(B):
                    for o in range(HALVES):
                        done = b * NI + (o + 1) * (K0 // 512 + (K0 % 512 > 0))
                        sp.wait_ge(piece_step, done * STEPS)
                        sp.wait_ge(item_read, 2 * done)
                        sp.dma_start(scratch["kp0"][b, :, o], pc_k0[b % 2][:, o]).then_inc(stored[b % 2], 16)
                    sp.wait_ge(piece_step, (b + 1) * NI * STEPS)
                    sp.wait_ge(item_read, 2 * (b + 1) * NI)
                    sp.wait_ge(val_read, (b + 1) * NKB0)
                    sp.dma_start(scratch["kp1"][b], pc_k1[b % 2][:]).then_inc(stored[b % 2], 16)
                    sp.dma_start(scratch["qp0"][b], pc_q0[b % 2][:]).then_inc(stored[b % 2], 16)
                    sp.dma_start(scratch["v0"][b], vals[b % 2][:, :, 0:H]).then_inc(stored[b % 2], 16)
                    sp.dma_start(scratch["v1"][b], vals[b % 2][:, 0:NKB1, H:VW]).then_inc(stored[b % 2], 16)
                    if b + 2 < B:
                        load(b + 2)
                sp.wait_ge(bias_done, 5)
                sp.dma_start(scratch["bias0"], bias0[:]).then_inc(bias_stored, 16)
                sp.dma_start(scratch["bias1"], bias1[:]).then_inc(bias_stored, 16)
                sp.wait_ge(flag_done, 1)
                sp.dma_start(scratch["flag0"], flag[:]).then_inc(bias_stored, 16)
                for i in range(2):
                    sp.wait_ge(stored[i], 16 * STORES * B // 2)
                sp.wait_ge(bias_stored, 48)

            @block.gpsimd
            def _(pool):
                for i in range(2):
                    pool.memset(hT[i][:, :, SC + SQ:K0], 0.0).then_inc(pads_zero, 1)
                pool.memset(bias0[:], NEG).then_inc(bias_done, 1)
                pool.memset(bias1[:], 0.0).then_inc(bias_done, 1)
                pool.wait_ge(bias_done, 2)
                pool.memset(bias0[:, SC:SC + SQ], 0.0).then_inc(bias_done, 1)
                pool.memset(bias1[:, SC:K1], NEG).then_inc(bias_done, 1)

            @block.tensor
            def _(pe):
                w = {"k0": w_k0, "k1": w_k1, "q0": w_q0}
                pe.wait_ge(weights_in, 16 * 11)
                pe.wait_ge(pads_zero, 2)

                def item(b, n):
                    kind, o, c, cols = ITEMS[n]
                    count = b * NI + n
                    if count >= PB:
                        pe.wait_ge(item_read, 2 * (count - PB + 1))
                    for i in range(HALVES):
                        mm = nc.tensor.matmul(psum[0:rows(kind), count % PB, 0:cols],
                                              w[kind][:, i, o * P:o * P + rows(kind)], hT[b % 2][:, i, c:c + cols],
                                              start=(i == 0), stop=(i == HALVES - 1))
                    mm.then_inc(item_psum, 1)

                def values(b, kb):
                    count = b * NKB0 + kb
                    if count >= PB:
                        pe.wait_ge(val_read, count - PB + 1)
                    for i in range(HALVES):
                        mm = nc.tensor.matmul(psum[:, PB + count % PB, 0:VW], hT[b % 2][:, i, kb * P:(kb + 1) * P],
                                              w_v[:, i, :], start=(i == 0), stop=(i == HALVES - 1))
                    mm.then_inc(val_psum, 1)

                for b in range(B):
                    pe.wait_ge(hT_in[b % 2], 64 * (b // 2 + 1))
                    for n in range(max(NI, NKB0)):
                        if n < NI:
                            item(b, n)
                        if n < NKB0:
                            values(b, n)
                pe.wait_ge(flag_rows, 2)
                pe.wait_ge(item_read, 2 * B * NI)
                nc.tensor.matmul(psum[0:1, 0, 0:1], any_row[:], ones[:], start=True, stop=True).then_inc(flag_sum, 1)

            @block.scalar
            def _(act):
                act.wait_ge(weights_in, 16 * 11)
                act.wait_ge(qbias, 1)
                bias = {"k0": b_k0, "q0": b_q0s, "k1": b_k1}
                for b in range(B):
                    for n, (kind, o, c, cols) in enumerate(ITEMS):
                        count = b * NI + n
                        r = rows(kind)
                        scale = 1.0 / D0 if kind == "q0" else 1.0
                        act.wait_ge(item_psum, count + 1)
                        if b >= 2 and n == 0:
                            act.wait_ge(stored[b % 2], 16 * STORES * (b // 2))
                        if count >= 4:
                            act.wait_ge(piece_step, (count - 3) * STEPS)
                        src = psum[0:r, count % PB, 0:cols]
                        nc.scalar.activation(xf[0:r, count % 4, 0:cols], src, ACT.Identity,
                                             bias=bias[kind][0:r, o:o + 1], scale=scale).then_inc(item_read, 1)
                        nc.scalar.activation(piece(b, kind, o, 0, c, cols), src, ACT.Identity,
                                             bias=bias[kind][0:r, o:o + 1], scale=scale).then_inc(item_read, 1)

            @block.vector
            def _(dve):
                dve.wait_ge(weights_in, 16 * 11)
                dve.tensor_scalar(b_q0s[:], b_q0[:], 1.0 / D0, None, ALU.mult).then_inc(qbias, 1)
                dve.tensor_copy(mask_f[:], mask_i[:]).then_inc(qbias, 1)
                dve.wait_ge(qbias, 2)
                dve.wait_ge(bias_done, 4)
                dve.tensor_scalar(bias0[:, 0:SC], mask_f[:], 0.0, NEG, ALU.is_equal, ALU.mult).then_inc(bias_done, 1)
                dve.memset(ones[:], 1.0).then_inc(flag_rows, 1)
                dve.tensor_scalar(attended[:], mask_f[:, 0:SKIP0 * P], 0.0, None, ALU.not_equal, ALU.max,
                                  accum_out=any_row[:]).then_inc(flag_rows, 1)

                def split(b, n):
                    kind, o, c, cols = ITEMS[n]
                    count = b * NI + n
                    r = rows(kind)
                    x, rest = xf[0:r, count % 4, 0:cols], r1[0:r, count % 2, 0:cols]
                    dve.wait_ge(item_read, 2 * (count + 1))
                    if count >= 2:
                        dve.wait_ge(piece_step, (count - 1) * STEPS)
                    dve.tensor_tensor(rest, x, piece(b, kind, o, 0, c, cols), ALU.subtract).then_inc(piece_step, 1)
                    dve.wait_ge(piece_step, count * STEPS + 1)
                    dve.tensor_copy(piece(b, kind, o, 1, c, cols), rest).then_inc(piece_step, 1)
                    dve.wait_ge(piece_step, count * STEPS + 2)
                    dve.tensor_tensor(piece(b, kind, o, 2, c, cols), rest, piece(b, kind, o, 1, c, cols),
                                      ALU.subtract).then_inc(piece_step, 2)

                def values(b, kb):
                    count = b * NKB0 + kb
                    dve.wait_ge(val_psum, count + 1)
                    if b >= 2 and kb == 0:
                        dve.wait_ge(stored[b % 2], 16 * STORES * (b // 2))
                    dve.tensor_tensor(vals[b % 2][:, kb, :], psum[:, PB + count % PB, 0:VW], b_v[:], ALU.add)\
                       .then_inc(val_read, 1)

                for b in range(B):
                    for n in range(max(NI, NKB0)):
                        if n < NKB0:
                            values(b, n)
                        if n < NI:
                            split(b, n)
                dve.wait_ge(flag_sum, 1)
                dve.tensor_copy(flag[:], psum[0:1, 0, 0:1]).then_inc(flag_done, 1)


class Plan:

    def __init__(self, layer, first_kb, masked):
        L0 = self.L0 = layer == 0
        self.masked = masked
        self.first_kb = first_kb
        self.NG, nkb, self.D = (G0, NKB0, D0) if L0 else (G1, NKB1, D1)
        self.NKB = nkb - first_kb
        self.KH = 4 if L0 else 1
        last_key = SC + SQ if L0 else SC
        n = last_key - first_kb * P
        self.CH = -(-n // 512)
        self.cuts = [first_kb * P]
        for i in range(self.CH):
            self.cuts.append(self.cuts[-1] + -(-(last_key - self.cuts[-1]) // (self.CH - i)))
        self.HALF = HALF = 4 * QB * self.CH // 2
        self.MS = 5 if masked else 3
        late = self.MS + 2
        self.ITEMS = [("s", i) for i in range(HALF + late)] + [("m", 0)]
        self.ITEMS += [("s", HALF + i) for i in range(late, HALF)] + [("m", 1)]
        self.NI, self.NSI = len(self.ITEMS), 2 * HALF
        if L0:
            units = -(-self.NKB // 4)
            edge = [self.NKB * u // units for u in range(units + 1)]
            self.STEPS = [[(kb, j) for kb in range(edge[u], edge[u + 1])] for u in range(units) for j in range(4)]
        else:
            self.STEPS = [[(kb, j) for j in range(4)] for kb in range(self.NKB)]
        self.NS = NS = len(self.STEPS)
        assert self.NG * NS % NPROB == 0 and self.NG * NS % 2 == 0
        self.PARTS = [[(s, step.index((kb, j)), j) for j in range(4) for s, step in enumerate(self.STEPS) if (kb, j) in step]
                      for kb in range(self.NKB)]
        lag = 4 if L0 else 3
        self.AFTER = []
        for kb in range(self.NKB):
            if L0:
                u = max(i for i, e in enumerate(edge[:-1]) if e <= kb)
                self.AFTER.append(4 * u + lag + min(3, 4 * (kb - edge[u]) // (edge[u + 1] - edge[u])))
            else:
                self.AFTER.append(kb + lag)
        self.END = self.AFTER[-1] - NS
        self.AFTER = [max(at, self.END + 4 + kb // 3) for kb, at in enumerate(self.AFTER)]
        base = []
        for s in range(NS):
            work = [("prev", kb, 0) for kb in range(self.NKB) if self.AFTER[kb] == NS + s]
            work += [("own", kb, 0) for kb in range(self.NKB) if self.AFTER[kb] == s]
            work = [(w, kb, part) for w, kb, _ in work for part in (0, 1)]
            if s == 0:
                base += work + [("scores", s, 0), ("scores", s, 1)]
            else:
                base += [("scores", s, 0)] + work[:2] + [("scores", s, 1)] + work[2:]
            if s == self.END + 2:
                base[-1:-1] = [("turn", 0, 0)]
            if s == self.END + 3:
                base[-4:-4] = [("norm", 0, 0)]
                base[-2:-2] = [("norm", 0, 1)]
        place = lambda n: n * (len(base) - TAIL[layer]) / (self.NI - 1) if n < self.NI - 1 else len(base) - 1
        self.ORDER, n = [], 0
        for i, x in enumerate(base):
            while n < self.NI and place(n) <= i:
                self.ORDER.append(("item", n, 0))
                n += 1
            self.ORDER.append(x)
        assert n == self.NI

        assert late <= HALF

        shifts = -self.NI % NFIRST
        self.BANK = [(n + shifts * n // (self.NI - NFIRST) if n < self.NI - NFIRST else n - self.NI) % NFIRST
                     for n in range(self.NI)]

    def bank_before(self, n):
        earlier = [i for i in range(n) if self.BANK[i] == self.BANK[n]]
        if earlier:
            return 0, earlier[-1]
        return 1, max(i for i in range(self.NI) if self.BANK[i] == self.BANK[n])


NPROB = 8
NFIRST = 3
SLOTS = 4
TAIL = (8, 7)


def choose(eng, flag, general, short):
    value = eng.value_load(flag[0:1, 0:1], min_val=0, max_val=B * P)
    with eng.If(value > 0):
        general()
    with eng.Else():
        short()


def attention(nc, t, scratch, layer):
    L0 = layer == 0
    general = Plan(layer, 0, not L0)
    short = Plan(layer, SKIP0 if L0 else 0, False)
    NG, NKB, D, KH = general.NG, general.NKB, general.D, general.KH
    KEYS = NKB * P
    NJ = 4 * QB
    LOADS = 2 * len(COMBOS) + KH

    with ExitStack() as ctx:
        nm = f"a{layer}_"
        sb = lambda name, shape, dt: ctx.enter_context(nc.sbuf_tensor(nm + name, shape, dt))
        sem = lambda name: ctx.enter_context(nc.semaphore(nm + name))
        first_psum = ctx.enter_context(nc.psum_tensor(nm + "first", [P, NFIRST, 512], F32))
        second_psum = ctx.enter_context(nc.psum_tensor(nm + "second", [P, 2, 1024], F32))
        out_bank = ctx.enter_context(nc.psum_tensor(nm + "out", [P, 512], F32))
        out_psum, turn_psum = out_bank[:, 0:SQ], out_bank[:, SQ:].rearrange("p (a w) -> p a w", a=QB)

        keys = [sb(f"keys{i}", [P, KH, KEYS], BF16) for i in range(SLOTS)]
        queries = [sb(f"queries{i}", [P, 4, SQ], BF16) for i in range(SLOTS)]
        values_in = [sb(f"values_in{i}", [P, NKB, KH * D], F32) for i in range(2)]
        values = [sb(f"values{i}", [P, NKB, KH, 32], F32) for i in range(2)]
        probs = sb("probs", [P, NPROB, 1024], F32)
        maxima = sb("maxima", [P, NJ, general.CH], F32)
        m_all = sb("m_all", [P, NJ], F32)
        m_rest = sb("m_rest", [P, NJ], F32)
        m_cols = sb("m_cols", [P, NJ, 4], BF16)
        ident = sb("ident", [P, P], F32)
        ident_b = sb("ident_b", [P, P], BF16)
        out_T = sb("out_T", [P, SQ], F32)
        recip = sb("recip", [P, QB, 4], F32)
        out_n = sb("out_n", [P, 2, QB, 4 * D], F32)
        if not L0:
            mask_q = sb("mask_q", [P, QB, SC], F32)
            mask_k = sb("mask_k", [P, NKB, SQ], F32)
            mask_p = sb("mask_p", [P, 3, NKB, SQ], BF16)

        constants = sem("constants")
        rows_set = [sem(f"rows_set{i}") for i in range(SLOTS)]
        loaded = [sem(f"loaded{i}") for i in range(SLOTS)]
        v_loaded = [sem(f"v_loaded{i}") for i in range(2)]
        v_placed = sem("v_placed")
        first_full = sem("first_full")
        first_free = sem("first_free")
        m_step = sem("m_step")
        m_rows = sem("m_rows")
        second_full = sem("second_full")
        probs_ready = sem("probs_ready")
        product = sem("product")
        out_read = sem("out_read")
        turned = sem("turned")
        recip_done = sem("recip_done")
        normed = sem("normed")
        stored = [sem(f"stored{i}") for i in range(2)]
        mask_in = sem("mask_in")
        mask_k_in = sem("mask_k_in")
        mask_step = sem("mask_step")
        MSTEPS = 4
        CONSTS = 10 if L0 else 11
        ROW_STEPS = 2 if L0 else 4
        flag = scratch[f"flag{layer}"]
        dst = scratch["attn0" if L0 else "attn1"]

        def constant_rows(eng, p, n):
            rows = [(keys[n][:], 0.0), (queries[n][:], 0.0)] if not L0 else []
            rows += [(keys[n][EXTRA:KROWS, :, p.first_kb * P:], 1.0), (queries[n][EXTRA:EXTRA + 1], 1.0)]
            assert len(rows) == ROW_STEPS
            for i, (r, value) in enumerate(rows):
                eng.memset(r, value).then_inc(rows_set[n], 1)
                eng.wait_ge(rows_set[n], i + 1)

        block = ctx.enter_context(nc.Block())

        @block.sync
        def _(sp):
            def program(p):
                def load(b, G):
                    if isinstance(b, int) and b == 0 and G < SLOTS:
                        sp.wait_ge(rows_set[G], ROW_STEPS)
                    n, k0 = G % SLOTS, p.first_kb * P
                    wait_at_least(sp, second_full, b, NG * p.NS, (G - SLOTS + 1) * p.NS)
                    if L0:
                        lo, o = 64 * (G % 2), G // 2
                        kp = scratch["kp0"][b, lo:lo + 64, o, :, k0:].rearrange("(j d) c k -> d c j k", d=D)
                        qp = scratch["qp0"][b, lo:lo + 64, o, :, :].rearrange("(j d) c q -> d c j q", d=D)
                    else:
                        lo, o = 32 * (G % 4), G // 4
                        kp = scratch["kp1"][b, D * G:D * G + D, :, :].rearrange("d c (a k) -> d c a k", a=1)
                        qp = scratch["qp1"][o, lo:lo + 32, :, bass.ds(b * SQ, SQ)].rearrange("(j d) c q -> d c j q", d=D)
                    for c, (qc, kc) in enumerate(COMBOS):
                        sp.dma_start(queries[n][D * c:D * c + D, :, :], qp[:, qc]).then_inc(loaded[n], 16)
                        sp.dma_start(keys[n][D * c:D * c + D, :, k0:], kp[:, kc]).then_inc(loaded[n], 16)
                    row = scratch["bias0"][bass.ds(b, 1), k0:] if L0 else scratch["bias1"]
                    for h in range(KH):
                        sp.dma_start(keys[n][EXTRA:EXTRA + 1, h, k0:], row).then_inc(loaded[n], 16)
                    wait_at_least(sp, v_placed, b, NG, G - 1)
                    v = scratch["v0"][b, :, p.first_kb:, 64 * G:64 * G + 64] if L0 else scratch["v1"][b, :, :, D * G:D * G + D]
                    sp.dma_start(values_in[G % 2][:, p.first_kb:, :], v).then_inc(v_loaded[G % 2], 16)

                def load_mask(b):
                    wait_at_least(sp, first_free, b, NG * p.NSI, 0)
                    sp.dma_start(mask_q[:], t["mask1"][b].rearrange("(a p) k -> p a k", p=P)).then_inc(mask_in, 16)

                def load_mask_k(b):
                    wait_at_least(sp, mask_step, b, MSTEPS, 0)
                    sp.dma_start(mask_k[:, 0:NKB - 1, :],
                                 t["mask1T"][b, 0:(NKB - 1) * P, :].rearrange("(a p) q -> p a q", p=P)).then_inc(mask_k_in, 16)
                    sp.dma_start(mask_k[0:SC - (NKB - 1) * P, NKB - 1, :], t["mask1T"][b, (NKB - 1) * P:SC, :]).then_inc(mask_k_in, 16)

                def store(b, G):
                    sp.wait_ge(normed, b * NG + G + 1)
                    sp.dma_start(dst[b, :, :, 4 * D * G:4 * D * G + 4 * D], out_n[:, G % 2, :, :]).then_inc(stored[G % 2], 16)

                if p.masked:
                    load_mask(0)
                    sp.wait_ge(constants, 1)
                    load_mask_k(0)
                for G in range(SLOTS - 1):
                    load(0, G)

                def body(b, first, last):
                    for G in range(NG):
                        ahead = G + SLOTS - 1
                        if p.masked and G == NG - 1 and not last:
                            load_mask(b + 1)
                        if p.masked and G == 1 and not last:
                            load_mask_k(b + 1)
                        if ahead < NG:
                            load(b, ahead)
                        elif not last:
                            load(b + 1, ahead - NG)
                        if G:
                            store(b, G - 1)
                        elif not first:
                            store(b - 1, NG - 1)
                each_batch(sp, body)
                store(B - 1, NG - 1)

            choose(sp, flag, lambda: program(general), lambda: program(short))
            for i in range(2):
                sp.wait_ge(stored[i], 16 * B * NG // 2)

        @block.gpsimd
        def _(pool):
            def fill_constants(p):
                made = 0

                def constant(ins):
                    nonlocal made
                    made += 1
                    ins.then_inc(constants, 1)
                    pool.wait_ge(constants, made)

                if not L0:
                    constant(pool.memset(mask_k[:, NKB - 1, :], 0.0))
                for m in [m_cols[:], ident[:], ident_b[:]] + [v[:, p.first_kb:] for v in values]:
                    constant(pool.memset(m, 0.0))
                for v in values:
                    constant(pool.memset(v[:, p.first_kb:, :, D:D + 1], 1.0))
                constant(pool.memset(m_cols[:, :, 0:1], 1.0))
                for m in (ident, ident_b):
                    constant(pool.affine_select(out=m[:], in_=m[:], compare_op=ALU.not_equal, fill=1.0, base=0,
                                                pattern=[[-1, P]], channel_multiplier=1))
                assert made == CONSTS

            def program(p):
                def place(b, G):
                    uses = NG // 2
                    pool.wait_ge(v_loaded[G % 2], 16 * (b * uses + G // 2 + 1))
                    wait_at_least(pool, product, b, NG * p.NKB, (G - 1) * p.NKB)
                    pool.nop(nofuse=True)
                    pool.tensor_copy(values[G % 2][:, p.first_kb:, :, 0:D],
                                     values_in[G % 2][:, p.first_kb:, :].rearrange("p k (h d) -> p k h d", h=KH)).then_inc(v_placed, 1)

                def split_mask(b):
                    pool.wait_ge(mask_k_in, 32 * (b + 1))
                    wait_at_least(pool, second_full, b, NG * p.NS, 0)
                    pool.nop(nofuse=True)
                    pool.tensor_copy(mask_p[:, 0], mask_k[:]).then_inc(mask_step, 1)
                    pool.wait_ge(mask_step, b * MSTEPS + 1)
                    pool.nop(nofuse=True)
                    pool.tensor_tensor(mask_k[:], mask_k[:], mask_p[:, 0], ALU.subtract).then_inc(mask_step, 1)
                    pool.wait_ge(mask_step, b * MSTEPS + 2)
                    pool.nop(nofuse=True)
                    pool.tensor_copy(mask_p[:, 1], mask_k[:]).then_inc(mask_step, 1)
                    pool.wait_ge(mask_step, b * MSTEPS + 3)
                    pool.nop(nofuse=True)
                    pool.tensor_tensor(mask_p[:, 2], mask_k[:], mask_p[:, 1], ALU.subtract).then_inc(mask_step, 1)

                def body(b, first, last):
                    for G in range(NG):
                        place(b, G)
                        if G == 0 and p.masked:
                            split_mask(b)

                constant_rows(pool, p, 0)
                fill_constants(p)
                constant_rows(pool, p, 2)
                each_batch(pool, body)

            choose(pool, flag, lambda: program(general), lambda: program(short))

        @block.tensor
        def _(pe):
            def program(p):
                def item(b, G, n):
                    kind, i = p.ITEMS[n]
                    slot, bank = G % SLOTS, p.BANK[n]
                    if n == 0:
                        pe.wait_ge(loaded[slot], 16 * LOADS * (b * (NG // SLOTS) + G // SLOTS + 1))
                    back, n0 = p.bank_before(n)
                    what, i0 = p.ITEMS[n0]
                    if what == "s":
                        wait_at_least(pe, first_free, b, NG * p.NSI, (G - back) * p.NSI + i0 + 1)
                    else:
                        wait_at_least(pe, m_rows, b, 2 * NG, 2 * (G - back) + i0 + 1)
                    if kind == "s":
                        j, rest = divmod(i, QB * p.CH)
                        qb, c = divmod(rest, p.CH)
                        nc.tensor.matmul(first_psum[:, bank, 0:p.cuts[c + 1] - p.cuts[c]],
                                         queries[slot][0:EXTRA + 1, j, qb * P:(qb + 1) * P],
                                         keys[slot][0:EXTRA + 1, j % KH, p.cuts[c]:p.cuts[c + 1]],
                                         start=True, stop=True).then_inc(first_full, 1)
                    else:
                        pe.wait_ge(m_step, (b * NG + G) * 2 * p.MS + (i + 1) * p.MS)
                        for k in range(NJ // 2):
                            mm = nc.tensor.matmul(first_psum[EXTRA:KROWS, bank, k * P:(k + 1) * P],
                                                  m_cols[:, i * NJ // 2 + k, :], ident_b[:], start=True, stop=True)
                        mm.then_inc(first_full, 1)

                def scores(b, G, s, part):
                    slot, step = G % SLOTS, p.STEPS[s]
                    if part == 0:
                        if s == 0 or (L0 and s == 2):
                            half = 2 if not L0 or s else 1
                            pe.wait_ge(m_rows, (b * NG + G) * 2 + half)
                        wait_at_least(pe, probs_ready, b, NG * p.NS, G * p.NS + s - 1)
                    unit = (G * p.NS + s) % 2
                    if L0:
                        half = -(-len(step) // 2)
                        for k in range(half) if part == 0 else range(half, len(step)):
                            kb, j = step[k]
                            k0 = (p.first_kb + kb) * P
                            mm = nc.tensor.matmul(second_psum[:, unit, k * SQ:(k + 1) * SQ], keys[slot][0:KROWS, j, k0:k0 + P],
                                                  queries[slot][0:KROWS, j, :], start=True, stop=True)
                    else:
                        if p.masked and G == 0 and s == 0 and part == 0:
                            pe.wait_ge(mask_step, (b + 1) * MSTEPS)
                        bank = second_psum[:, unit, 512 * part:512 * part + 512]
                        mm = nc.tensor.matmul(bank, keys[slot][0:KROWS, 0, s * P:(s + 1) * P],
                                              queries[slot][0:KROWS, 2 * part:2 * part + 2, :].rearrange("p a q -> p (a q)"),
                                              start=True, stop=not p.masked)
                        for pc in range(3 if p.masked else 0):
                            mm = nc.tensor.matmul(bank.rearrange("p (a q) -> p a q", a=2), ident_b[:],
                                                  mask_p[:, pc, s, :].unsqueeze(1).to_broadcast([P, 2, SQ]),
                                                  start=False, stop=(pc == 2))
                    if part == 1:
                        mm.then_inc(second_full, 1)

                def products(b, G, kb, part):
                    parts = p.PARTS[kb]
                    if part == 0:
                        if kb == 0:
                            pe.wait_ge(v_placed, b * NG + G + 1)
                            wait_at_least(pe, out_read, b, NG, G)
                            wait_at_least(pe, normed, b, NG, G)
                        pe.wait_ge(probs_ready, (b * NG + G) * p.NS + max(s for s, _, _ in parts) + 1)
                    for s, col, j in parts[2 * part:2 * part + 2]:
                        mm = nc.tensor.matmul(out_psum[32 * j:32 * j + 32, 0:SQ], values[G % 2][:, p.first_kb + kb, j % KH, :],
                                              probs[:, (G * p.NS + s) % NPROB, col * SQ:(col + 1) * SQ],
                                              start=(kb == 0), stop=(kb == p.NKB - 1))
                    if part == 1:
                        mm.then_inc(product, 1)

                def turn(b, G):
                    pe.wait_ge(out_read, b * NG + G + 1)
                    wait_at_least(pe, normed, b, NG, G)
                    for qb in range(QB):
                        mm = nc.tensor.transpose(turn_psum[:, qb, :], out_T[:, qb * P:(qb + 1) * P], ident[:])
                    mm.then_inc(turned, 1)

                for n in range(p.NI):
                    if p.ITEMS[n] == ("m", 0):
                        pe.wait_ge(constants, CONSTS)
                    item(0, 0, n)

                def body(b, first, last):
                    for G in range(NG):
                        before = (b, G - 1) if G else (b - 1, NG - 1)
                        nxt = (b, G + 1) if G + 1 < NG else (b + 1, 0)
                        for what, i, part in p.ORDER:
                            if what == "scores":
                                scores(b, G, i, part)
                            elif what == "own":
                                products(b, G, i, part)
                            elif what == "item" and not (last and G == NG - 1):
                                item(*nxt, i)
                            elif what == "prev" and (G or not first):
                                products(*before, i, part)
                            elif what == "turn" and (G or not first):
                                turn(*before)
                each_batch(pe, body)
                for what, i, part in p.ORDER:
                    if what == "prev":
                        products(B - 1, NG - 1, i, part)
                turn(B - 1, NG - 1)

            choose(pe, flag, lambda: program(general), lambda: program(short))

        @block.scalar
        def _(act):
            def program(p):
                def rows(b, G, n):
                    half = p.ITEMS[n][1]
                    act.wait_ge(first_full, (b * NG + G) * p.NI + n + 1)
                    nc.scalar.copy(queries[G % SLOTS][EXTRA:KROWS, 2 * half:2 * half + 2, :].rearrange("p a q -> p (a q)"),
                                   first_psum[EXTRA:KROWS, p.BANK[n], :]).then_inc(m_rows, 1)

                def exps(b, G, s):
                    act.wait_ge(second_full, (b * NG + G) * p.NS + s + 1)
                    pg, ps = divmod(G * p.NS + s - NPROB, p.NS)
                    kb = max(kb for kb, parts in enumerate(p.PARTS) if any(part[0] == ps for part in parts))
                    wait_at_least(act, product, b, NG * p.NKB, pg * p.NKB + kb + 1)
                    cols = len(p.STEPS[s]) * SQ
                    nc.scalar.activation(probs[:, (G * p.NS + s) % NPROB, 0:cols], second_psum[:, (G * p.NS + s) % 2, 0:cols],
                                         ACT.Exp).then_inc(probs_ready, 1)

                def read_out(b, G):
                    act.wait_ge(product, (b * NG + G + 1) * p.NKB)
                    wait_at_least(act, turned, b, NG, G)
                    nc.scalar.copy(out_T[:], out_psum).then_inc(out_read, 1)

                M_ITEMS = [n for n, (kind, _) in enumerate(p.ITEMS) if kind == "m"]
                for n in M_ITEMS:
                    rows(0, 0, n)

                def body(b, first, last):
                    for G in range(NG):
                        before = (b, G - 1) if G else (b - 1, NG - 1)
                        nxt = (b, G + 1) if G + 1 < NG else (b + 1, 0)
                        for what, i, part in p.ORDER:
                            if what == "scores" and part == 1:
                                if i == p.END + 1 and (G or not first):
                                    read_out(*before)
                                exps(b, G, i)
                            elif what == "item" and i in M_ITEMS and not (last and G == NG - 1):
                                rows(*nxt, i)
                each_batch(act, body)
                read_out(B - 1, NG - 1)

            choose(act, flag, lambda: program(general), lambda: program(short))

        @block.vector
        def _(dve):
            def program(p):
                def scores(b, G, n):
                    i = p.ITEMS[n][1]
                    jq, c = divmod(i, p.CH)
                    w = p.cuts[c + 1] - p.cuts[c]
                    if i == 0 and p.masked and G == 0:
                        dve.wait_ge(mask_in, 16 * (b + 1))
                    if i % p.HALF == 0:
                        wait_at_least(dve, m_step, b, NG * 2 * p.MS, (2 * (G - 1) + i // p.HALF) * p.MS + 1)
                    dve.wait_ge(first_full, (b * NG + G) * p.NI + n + 1)
                    bank = first_psum[:, p.BANK[n], 0:w]
                    if p.masked:
                        dve.nop(nofuse=True)
                        dve.tensor_tensor_reduce(bank, bank, mask_q[:, jq % QB, p.cuts[c]:p.cuts[c + 1]], 1.0, -3.0e38,
                                                 ALU.add, ALU.max, maxima[:, jq, c:c + 1]).then_inc(first_free, 1)
                    else:
                        dve.tensor_reduce(maxima[:, jq, c:c + 1], bank, AX.X, ALU.max).then_inc(first_free, 1)
                    if 0 <= i - p.HALF < p.MS:
                        pieces(b, G, 0, i - p.HALF)
                    if i == p.NSI - 1:
                        for k in range(p.MS):
                            pieces(b, G, 1, k)

                def pieces(b, G, half, k):
                    a = slice(half * NJ // 2, (half + 1) * NJ // 2)
                    m, rest, p1, p2, p3 = [x.unsqueeze(2) for x in (m_all[:, a], m_rest[:, a])] + \
                                          [m_cols[:, a, i:i + 1] for i in (1, 2, 3)]
                    if k == 0:
                        dve.wait_ge(first_free, (b * NG + G) * p.NSI + (half + 1) * p.HALF)
                    wait_at_least(dve, m_step, b, NG * 2 * p.MS, (G * 2 + half) * p.MS + k)
                    if k == 0:
                        ins = dve.tensor_reduce(m, maxima[:, a, 0:p.CH], AX.X, ALU.max)
                    elif k == 1:
                        ins = dve.tensor_scalar(p1, m, -1.0, None, ALU.mult)
                    elif k == 2:
                        ins = dve.scalar_tensor_tensor(out=rest if p.masked else p2, in0=m, scalar=-1.0, in1=p1,
                                                       op0=ALU.mult, op1=ALU.subtract)
                    elif k == 3:
                        ins = dve.tensor_copy(p2, rest)
                    else:
                        ins = dve.tensor_tensor(p3, rest, p2, ALU.subtract)
                    ins.then_inc(m_step, 1)

                def norm(b, G, part):
                    out4 = turn_psum.rearrange("p a (j w) -> p a j w", w=32)
                    if part == 0:
                        dve.wait_ge(turned, b * NG + G + 1)
                        wait_at_least(dve, normed, b, NG, G)
                        dve.reciprocal(recip[:].unsqueeze(3), out4[:, :, :, D:D + 1]).then_inc(recip_done, 1)
                    else:
                        dve.wait_ge(recip_done, b * NG + G + 1)
                        wait_at_least(dve, stored[G % 2], b, 16 * (NG // 2), 16 * (G // 2))
                        dve.tensor_tensor(out_n[:, G % 2, :, :].rearrange("p a (j d) -> p a j d", d=D), out4[:, :, :, 0:D],
                                          recip[:].unsqueeze(3).to_broadcast([P, QB, 4, D]), ALU.mult).then_inc(normed, 1)

                S_ITEMS = [n for n, (kind, _) in enumerate(p.ITEMS) if kind == "s"]
                for n in (1, 3):
                    constant_rows(dve, p, n)
                dve.wait_ge(constants, CONSTS)
                for n in S_ITEMS:
                    scores(0, 0, n)

                def body(b, first, last):
                    for G in range(NG):
                        before = (b, G - 1) if G else (b - 1, NG - 1)
                        nxt = (b, G + 1) if G + 1 < NG else (b + 1, 0)
                        for what, i, part in p.ORDER:
                            if what == "item" and i in S_ITEMS and not (last and G == NG - 1):
                                scores(*nxt, i)
                            elif what == "norm" and (G or not first):
                                norm(*before, part)
                each_batch(dve, body)
                norm(B - 1, NG - 1, 0)
                norm(B - 1, NG - 1, 1)

            choose(dve, flag, lambda: program(general), lambda: program(short))


CT = 4
NT = B * QB
NCH = NT // CT
NF = F // P
NUP = 3


def identity(pool, tile, sem):
    pool.memset(tile[:], 0.0).then_inc(sem, 1)
    pool.wait_ge(sem, 1)
    pool.affine_select(out=tile[:], in_=tile[:], compare_op=ALU.not_equal, fill=1.0, base=0,
                       pattern=[[-1, P]], channel_multiplier=1).then_inc(sem, 1)


def middle(nc, t, scratch):
    STAGES = [("T", 0), ("O", 0), ("Y", 0), ("T", 1), ("O", 1), ("U", 0), ("Y", 1), ("T", 2), ("O", 2), ("U", 1), ("X", 0),
              ("Y", 2), ("T", 3), ("O", 3), ("U", 2), ("Q", 0), ("X", 1), ("Y", 3), ("U", 3), ("Q", 1), ("X", 2), ("D", 3),
              ("Q", 2), ("X", 3), ("Q", 3)]
    ORDER = []
    for kind, c in STAGES:
        for i in range(NF + 1 if kind == "U" else CT if kind == "D" else 1):
            ORDER.append((kind, c, i))
            if kind == "U" and c and i % 2 == 1:
                ORDER.append(("D", c - 1, i // 2))
    TURNS = [x for x in STAGES if x[0] in "TYX"]
    turn_no = {x: i for i, x in enumerate(TURNS)}
    GELU_A, GELU_B = 0.7978845608028654, 0.044715
    SCALE = float(D1) ** -0.5

    def gelu_at(step, n):
        c, f = divmod(n, NF)
        if step == "inner":
            return c * 3 * NF + (3 * f + 1 if f else 2)
        return c * 3 * NF + min(3 * (f + 1) + 2, 3 * NF)

    with ExitStack() as ctx:
        sb = lambda name, shape, dt: ctx.enter_context(nc.sbuf_tensor("mid_" + name, shape, dt))
        sem = lambda name: ctx.enter_context(nc.semaphore("mid_" + name))
        psum = ctx.enter_context(nc.psum_tensor("mid_psum", [P, 8, 512], F32))
        turn_ps, proj_ps, up_ps, down_ps, q_ps = (psum[:, 0:2], psum[:, 2:4], psum[:, 4:6], psum[:, 6], psum[:, 7])
        w_o = sb("w_o", [P, HALVES, H], F32)
        w_1 = sb("w_1", [P, HALVES, F], F32)
        w_2 = sb("w_2", [P, NF, H], F32)
        w_q = sb("w_q", [P, HALVES, H], F32)
        b_o = sb("b_o", [P, H], F32)
        b_2 = sb("b_2", [P, H], F32)
        w_n = sb("w_n", [P, H], F32)
        b_1 = sb("b_1", [P, NF], F32)
        b_q = sb("b_q", [P, HALVES], F32)
        b_qs = sb("b_qs", [P, HALVES], F32)
        ident = sb("ident", [P, P], F32)
        attn = sb("attn", [P, NT, H], F32)
        x_o = sb("x_o", [P, NT, H], F32)
        x_2 = sb("x_2", [P, NT, H], F32)
        x_1 = sb("x_1", [P, NT, H], F32)
        turned = {"T": sb("attn_T", [P, 2, HALVES, 512], F32), "Y": sb("norm_T", [P, 2, HALVES, 512], F32),
                  "X": sb("x_1_T", [P, 2, HALVES, 512], F32)}
        hidden = sb("hidden", [P, 2, NF, 512], F32)
        up = sb("up", [P, NUP, 512], F32)
        cubic = sb("cubic", [P, NUP, 512], F32)
        sumsq = sb("sumsq", [P, NT], F32)
        square = sb("square", [P, H], F32)
        rms = sb("rms", [P, NT], F32)
        qf = sb("qf", [P, 512], F32)
        q_pc = sb("q_pc", [P, 2, HALVES, 3, 512], BF16)
        mask = sb("mask", [P, 2, SC], F32)
        mask_sums = sb("mask_sums", [P, NT], F32)
        mask_any = sb("mask_any", [P, 2], F32)
        ones = sb("ones", [P, 1], F32)
        flag = sb("flag", [1, 1], I32)

        mask_in = [sem(f"mask_in{i}") for i in range(2)]
        mask_seen, flag_step, flag_sum, flag_done = sem("mask_seen"), sem("flag_step"), sem("flag_sum"), sem("flag_done")
        flag_stored = sem("flag_stored")
        proj_in, mlp_in, query_in = sem("proj_in"), sem("mlp_in"), sem("query_in")
        x_in = [sem(f"x_in{c}") for c in range(NCH)]
        attn_in = [sem(f"attn_in{c}") for c in range(NCH)]
        ident_done, bias_step = sem("ident_done"), sem("bias_step")
        x_step = sem("x_step")
        turn_full, turn_read = sem("turn_full"), sem("turn_read")
        proj_full, proj_read = sem("proj_full"), sem("proj_read")
        up_full, up_read = sem("up_full"), sem("up_read")
        down_full, down_read = sem("down_full"), sem("down_read")
        q_full, q_read = sem("q_full"), sem("q_read")
        norm_step, root, gelu_step, tanh_done = sem("norm_step"), sem("root"), sem("gelu_step"), sem("tanh_done")
        q_step, x_stored = sem("q_step"), sem("x_stored")
        q_stored = [sem(f"q_stored{i}") for i in range(2)]
        NSTEPS = 2 * CT + 2 + CT

        with nc.Block() as block:
            @block.sync
            def _(sp):
                row = lambda name: t[name].rearrange("(a n) -> a n", a=1).to_broadcast([P, H])
                def chunk(c):
                    b0, b1 = c * CT // QB, (c + 1) * CT // QB
                    sp.dma_start(attn[:, c * CT:(c + 1) * CT].rearrange("p (b a) h -> p b (a h)", a=QB),
                                 scratch["attn0"][b0:b1].rearrange("b p a h -> p b (a h)")).then_inc(attn_in[c], 16)
                    sp.dma_start(x_2[:, c * CT:(c + 1) * CT], t["x"][b0:b1].rearrange("b (a p) h -> p (b a) h", p=P)).then_inc(x_in[c], 16)

                chunk(0)
                for dst, src, came in ((w_o[:], t["ow0"].rearrange("(i p) n -> p i n", p=P), proj_in),
                                       (b_o[:], row("ob0"), proj_in),
                                       (w_n[:], row("nw"), proj_in),
                                       (b_q[:], t["qb1"], proj_in),
                                       (w_1[:], t["w1"].rearrange("(i p) n -> p i n", p=P), mlp_in),
                                       (b_1[:], t["b1"], mlp_in),
                                       (w_2[:], t["w2"].rearrange("(i p) n -> p i n", p=P), mlp_in),
                                       (b_2[:], row("b2"), mlp_in),
                                       (w_q[:], t["qw1"].rearrange("(i p) n -> p i n", p=P), query_in)):
                    sp.dma_start(dst, src).then_inc(came, 16)
                for c in range(1, NCH):
                    chunk(c)
                for n in range(NT):
                    if n >= 2:
                        sp.wait_ge(mask_seen, n - 1)
                    sp.dma_start(mask[:, n % 2], t["mask1"][n // QB, n % QB * P:(n % QB + 1) * P, :]).then_inc(mask_in[n % 2], 16)
                for c in range(NCH):
                    sp.wait_ge(q_step, (c + 1) * HALVES * 3)
                    sp.wait_ge(q_read, (c + 1) * HALVES * 2)
                    for o in range(HALVES):
                        sp.dma_start(scratch["qp1"][o, :, :, c * 512:(c + 1) * 512], q_pc[:, c % 2, o]).then_inc(q_stored[c % 2], 16)
                sp.wait_ge(down_read, NT)
                sp.dma_start(scratch["x1"].rearrange("b p a h -> p b (a h)"), x_1[:].rearrange("p (b a) h -> p b (a h)", a=QB)).then_inc(x_stored, 16)
                for i in range(2):
                    sp.wait_ge(q_stored[i], 16 * HALVES * NCH // 2)
                sp.wait_ge(x_stored, 16)
                sp.wait_ge(flag_done, 1)
                sp.dma_start(scratch["flag1"], flag[:]).then_inc(flag_stored, 16)
                sp.wait_ge(flag_stored, 16)

            @block.gpsimd
            def _(pool):
                identity(pool, ident, ident_done)
                pool.wait_ge(proj_in, 16 * 4)
                for T in range(NT):
                    if T % CT == 0:
                        pool.wait_ge(x_in[T // CT], 16)
                    pool.tensor_tensor(x_o[:, T], x_2[:, T], b_o[:], ALU.add).then_inc(x_step, 1)
                pool.wait_ge(x_step, NT)
                pool.wait_ge(mlp_in, 16 * 4)
                for T in range(NT):
                    pool.tensor_tensor(x_2[:, T], x_2[:, T], b_2[:], ALU.add).then_inc(x_step, 1)

            @block.tensor
            def _(pe):
                pe.wait_ge(ident_done, 2)
                src = {"T": attn, "Y": attn, "X": x_1}
                for kind, c, step in ORDER:
                    if kind in "TYX":
                        if kind == "T":
                            pe.wait_ge(attn_in[c], 16)
                        if kind == "Y":
                            pe.wait_ge(norm_step, (c + 1) * NSTEPS)
                        if kind == "X":
                            pe.wait_ge(down_read, (c + 1) * CT)
                        for k in range(CT):
                            n = turn_no[kind, c] * CT + k
                            if n >= 2:
                                pe.wait_ge(turn_read, n - 1)
                            for i in range(HALVES):
                                mm = nc.tensor.transpose(turn_ps[:, n % 2, i * P:(i + 1) * P],
                                                         src[kind][:, c * CT + k, i * P:(i + 1) * P], ident[:])
                            mm.then_inc(turn_full, 1)
                    if kind == "O":
                        pe.wait_ge(turn_read, (turn_no["T", c] + 1) * CT)
                        if c == 0:
                            pe.wait_ge(proj_in, 16 * 4)
                        for k in range(CT):
                            n = c * CT + k
                            if n >= 2:
                                pe.wait_ge(proj_read, n - 1)
                            for i in range(HALVES):
                                mm = nc.tensor.matmul(proj_ps[:, n % 2, 0:H], turned["T"][:, c % 2, i, k * P:(k + 1) * P],
                                                      w_o[:, i, :], start=(i == 0), stop=(i == HALVES - 1))
                            mm.then_inc(proj_full, 1)
                    if kind == "U" and step < NF:
                        f, n = step, c * NF + step
                        if n == 0:
                            pe.wait_ge(mlp_in, 16 * 4)
                        if f == 0:
                            pe.wait_ge(turn_read, (turn_no["Y", c] + 1) * CT)
                        if n >= 2:
                            pe.wait_ge(up_read, 2 * (n - 1))
                        for i in range(HALVES):
                            mm = nc.tensor.matmul(up_ps[:, n % 2, :], w_1[:, i, f * P:(f + 1) * P],
                                                  turned["Y"][:, c % 2, i, :], start=(i == 0), stop=(i == HALVES - 1))
                        mm.then_inc(up_full, 1)
                    if kind == "D":
                        k, n = step, c * CT + step
                        if k == 0:
                            pe.wait_ge(gelu_step, (c + 1) * NF * 3)
                        if n >= 1:
                            pe.wait_ge(down_read, n)
                        for f in range(NF):
                            mm = nc.tensor.matmul(down_ps[:, 0:H], hidden[:, c % 2, f, k * P:(k + 1) * P], w_2[:, f, :],
                                                  start=(f == 0), stop=(f == NF - 1))
                        mm.then_inc(down_full, 1)
                    if kind == "Q":
                        pe.wait_ge(turn_read, (turn_no["X", c] + 1) * CT)
                        if c == 0:
                            pe.wait_ge(query_in, 16)
                        for o in range(HALVES):
                            n = c * HALVES + o
                            if n >= 1:
                                pe.wait_ge(q_read, 2 * n)
                            for i in range(HALVES):
                                mm = nc.tensor.matmul(q_ps[:, :], w_q[:, i, o * P:(o + 1) * P], turned["X"][:, c % 2, i, :],
                                                      start=(i == 0), stop=(i == HALVES - 1))
                            mm.then_inc(q_full, 1)
                pe.wait_ge(flag_step, 3)
                pe.wait_ge(q_read, 2 * HALVES * NCH)
                nc.tensor.matmul(q_ps[0:1, 0:1], mask_any[:, 1:2], ones[:], start=True, stop=True).then_inc(flag_sum, 1)

            @block.scalar
            def _(act):
                def see_mask(n):
                    act.wait_ge(mask_in[n % 2], 16 * (n // 2 + 1))
                    nc.scalar.activation(mask[:, n % 2], mask[:, n % 2], ACT.Abs,
                                         accum_out=mask_sums[:, n:n + 1]).then_inc(mask_seen, 1)

                act.wait_ge(mlp_in, 16 * 4)
                act.wait_ge(bias_step, 1)
                for kind, c, step in ORDER:
                    if kind == "O":
                        act.wait_ge(norm_step, c * NSTEPS + 2 * CT + 1)
                        nc.scalar.activation(rms[:, c * CT:(c + 1) * CT], rms[:, c * CT:(c + 1) * CT], ACT.Sqrt).then_inc(root, 1)
                    if kind == "U":
                        f, n = step, c * NF + step
                        if f < NF:
                            act.wait_ge(up_full, n + 1)
                            if n >= NUP:
                                act.wait_ge(gelu_step, gelu_at("last", n - NUP))
                            nc.scalar.activation(up[:, n % NUP], up_ps[:, n % 2], ACT.Identity,
                                                 bias=b_1[:, f:f + 1]).then_inc(up_read, 1)
                            nc.scalar.activation(cubic[:, n % NUP], up_ps[:, n % 2], ACT.Square,
                                                 bias=b_1[:, f:f + 1]).then_inc(up_read, 1)
                        if f:
                            act.wait_ge(gelu_step, gelu_at("inner", n - 1))
                            nc.scalar.activation(cubic[:, (n - 1) % NUP], cubic[:, (n - 1) % NUP], ACT.Tanh,
                                                 scale=GELU_A).then_inc(tanh_done, 1)
                        if f % 2 == 1:
                            see_mask(n // 2)
                    if kind == "Q":
                        for o in range(HALVES):
                            n = c * HALVES + o
                            act.wait_ge(q_full, n + 1)
                            if n >= 1:
                                act.wait_ge(q_step, 3 * n)
                            if c >= 2 and o == 0:
                                act.wait_ge(q_stored[c % 2], 16 * HALVES * (c // 2))
                            nc.scalar.activation(qf[:], q_ps[:, :], ACT.Identity, bias=b_qs[:, o:o + 1],
                                                 scale=SCALE).then_inc(q_read, 1)
                            nc.scalar.activation(q_pc[:, c % 2, o, 0], q_ps[:, :], ACT.Identity, bias=b_qs[:, o:o + 1],
                                                 scale=SCALE).then_inc(q_read, 1)

            @block.vector
            def _(dve):
                dve.wait_ge(proj_in, 16 * 4)
                dve.tensor_scalar(b_qs[:], b_q[:], SCALE, None, ALU.mult).then_inc(bias_step, 1)

                def norm(c):
                    a, base = slice(c * CT, (c + 1) * CT), c * NSTEPS
                    for k in range(CT):
                        T = c * CT + k
                        dve.wait_ge(proj_full, T + 1)
                        dve.wait_ge(x_step, T + 1)
                        dve.wait_ge(turn_full, (turn_no["T", c] + 1) * CT)
                        dve.tensor_tensor(attn[:, T], proj_ps[:, T % 2, 0:H], x_o[:, T], ALU.add).then_inc(proj_read, 1)
                        dve.wait_ge(proj_read, T + 1)
                        if T:
                            dve.wait_ge(norm_step, base + 2 * k if k else base)
                        dve.tensor_tensor_reduce(square[:], attn[:, T], attn[:, T], 1.0, 0.0, ALU.mult, ALU.add,
                                                 sumsq[:, T:T + 1]).then_inc(norm_step, 2)
                    dve.wait_ge(norm_step, base + 2 * CT)
                    dve.tensor_scalar(rms[:, a], sumsq[:, a], 1.0 / H, EPS, ALU.mult, ALU.add).then_inc(norm_step, 1)
                    dve.wait_ge(root, c + 1)
                    dve.reciprocal(sumsq[:, a], rms[:, a]).then_inc(norm_step, 1)
                    dve.wait_ge(norm_step, base + 2 * CT + 2)
                    for k in range(CT):
                        T = c * CT + k
                        dve.scalar_tensor_tensor(out=attn[:, T], in0=attn[:, T], scalar=sumsq[:, T:T + 1], in1=w_n[:],
                                                 op0=ALU.mult, op1=ALU.mult).then_inc(norm_step, 1)

                for kind, c, step in ORDER:
                    if kind in "TYX":
                        for k in range(CT):
                            n = turn_no[kind, c] * CT + k
                            dve.wait_ge(turn_full, n + 1)
                            dve.tensor_copy(turned[kind][:, c % 2, :, k * P:(k + 1) * P],
                                            turn_ps[:, n % 2, 0:H].rearrange("p (i q) -> p i q", i=HALVES)).then_inc(turn_read, 1)
                    if kind == "O":
                        norm(c)
                    if kind == "U":
                        f, n = step, c * NF + step
                        if f < NF:
                            buf = n % NUP
                            dve.wait_ge(up_read, 2 * (n + 1))
                            dve.tensor_scalar(cubic[:, buf], cubic[:, buf], GELU_B, 1.0, ALU.mult, ALU.add).then_inc(gelu_step, 1)
                            dve.wait_ge(gelu_step, gelu_at("inner", n) - 1)
                            dve.tensor_tensor(cubic[:, buf], cubic[:, buf], up[:, buf], ALU.mult).then_inc(gelu_step, 1)
                        if f:
                            m = n - 1
                            dve.wait_ge(tanh_done, m + 1)
                            dve.scalar_tensor_tensor(out=hidden[:, c % 2, f - 1], in0=cubic[:, m % NUP], scalar=1.0,
                                                     in1=up[:, m % NUP], op0=ALU.add, op1=ALU.mult).then_inc(gelu_step, 1)
                    if kind == "D":
                        T = c * CT + step
                        dve.wait_ge(down_full, T + 1)
                        dve.wait_ge(x_step, NT + T + 1)
                        dve.scalar_tensor_tensor(out=x_1[:, T], in0=down_ps[:, 0:H], scalar=0.5, in1=x_2[:, T],
                                                 op0=ALU.mult, op1=ALU.add).then_inc(down_read, 1)
                    if kind == "Q":
                        for o in range(HALVES):
                            n = c * HALVES + o
                            pc = lambda i: q_pc[:, c % 2, o, i]
                            dve.wait_ge(q_read, 2 * (n + 1))
                            dve.tensor_tensor(qf[:], qf[:], pc(0), ALU.subtract).then_inc(q_step, 1)
                            dve.wait_ge(q_step, 3 * n + 1)
                            dve.tensor_copy(pc(1), qf[:]).then_inc(q_step, 1)
                            dve.wait_ge(q_step, 3 * n + 2)
                            dve.tensor_tensor(pc(2), qf[:], pc(1), ALU.subtract).then_inc(q_step, 1)
                dve.memset(ones[:], 1.0).then_inc(flag_step, 1)
                dve.wait_ge(mask_seen, NT)
                dve.tensor_reduce(mask_any[:, 0:1], mask_sums[:], AX.X, ALU.add).then_inc(flag_step, 1)
                dve.wait_ge(flag_step, 2)
                dve.tensor_scalar(mask_any[:, 1:2], mask_any[:, 0:1], 0.0, None, ALU.not_equal).then_inc(flag_step, 1)
                dve.wait_ge(flag_sum, 1)
                dve.tensor_copy(flag[:], q_ps[0:1, 0:1]).then_inc(flag_done, 1)


def finish(nc, t, scratch, out):
    with ExitStack() as ctx:
        sb = lambda name, shape, dt: ctx.enter_context(nc.sbuf_tensor("fin_" + name, shape, dt))
        sem = lambda name: ctx.enter_context(nc.semaphore("fin_" + name))
        psum = ctx.enter_context(nc.psum_tensor("fin_psum", [P, 8, 512], F32))
        w_o = sb("w_o", [P, HALVES, H], F32)
        b_o, gamma, beta = sb("b_o", [P, H], F32), sb("gamma", [P, H], F32), sb("beta", [P, H], F32)
        ident = sb("ident", [P, P], F32)
        attn = sb("attn", [P, NT, H], F32)
        x_1 = sb("x_1", [P, NT, H], F32)
        y = sb("y", [P, NT, H], F32)
        attn_T = sb("attn_T", [P, 4, HALVES, P], F32)
        stats = sb("stats", [P, NT, 6], F32)
        mean_var = sb("mean_var", [P, NT, 2], F32)
        std = sb("std", [P, NT], F32)
        attn_in = [sem(f"attn_in{c}") for c in range(NCH)]
        x_in = [sem(f"x_in{c}") for c in range(NCH)]
        proj_in, affine_in, ident_done = sem("proj_in"), sem("affine_in"), sem("ident_done")
        x_step, turn_full, turn_read = sem("x_step"), sem("turn_full"), sem("turn_read")
        proj_full, proj_read, stat_step, eps_added = sem("proj_full"), sem("proj_read"), sem("stat_step"), sem("eps_added")
        root, inverted, normed = sem("root"), sem("inverted"), sem("normed")
        scaled, shifted, stored = sem("scaled"), sem("shifted"), sem("stored")

        with nc.Block() as block:
            @block.sync
            def _(sp):
                row = lambda name: t[name].rearrange("(a n) -> a n", a=1).to_broadcast([P, H])

                def chunk(c):
                    tiles, b0, b1 = slice(c * CT, (c + 1) * CT), c * CT // QB, (c + 1) * CT // QB
                    for dst, name, came in ((attn, "attn1", attn_in), (x_1, "x1", x_in)):
                        sp.dma_start(dst[:, tiles].rearrange("p (b a) h -> p b (a h)", a=QB),
                                     scratch[name][b0:b1].rearrange("b p a h -> p b (a h)")).then_inc(came[c], 16)

                chunk(0)
                sp.dma_start(w_o[:], t["ow1"].rearrange("(i p) n -> p i n", p=P)).then_inc(proj_in, 16)
                sp.dma_start(b_o[:], row("ob1")).then_inc(proj_in, 16)
                chunk(1)
                sp.dma_start(gamma[:], row("gamma")).then_inc(affine_in, 16)
                sp.dma_start(beta[:], row("beta")).then_inc(affine_in, 16)
                for c in range(2, NCH):
                    chunk(c)
                for b in range(B):
                    sp.wait_ge(shifted, QB * (b + 1))
                    sp.dma_start(out[b].rearrange("(a p) h -> p a h", p=P), y[:, b * QB:(b + 1) * QB]).then_inc(stored, 16)
                sp.wait_ge(stored, 16 * B)

            @block.gpsimd
            def _(pool):
                identity(pool, ident, ident_done)
                pool.wait_ge(proj_in, 32)

                def residual(c):
                    pool.wait_ge(x_in[c], 16)
                    for T in range(c * CT, (c + 1) * CT):
                        pool.tensor_tensor(x_1[:, T], x_1[:, T], b_o[:], ALU.add).then_inc(x_step, 1)

                residual(0)
                for c in range(NCH):
                    if c + 1 < NCH:
                        residual(c + 1)
                    for T in range(c * CT, (c + 1) * CT):
                        if T == 0:
                            pool.wait_ge(affine_in, 32)
                        pool.wait_ge(normed, T + 1)
                        pool.tensor_tensor(y[:, T], y[:, T], gamma[:], ALU.mult).then_inc(scaled, 1)

            @block.tensor
            def _(pe):
                pe.wait_ge(ident_done, 2)
                for T in range(NT + 1):
                    if T < NT:
                        if T % CT == 0:
                            pe.wait_ge(attn_in[T // CT], 16)
                        if T >= 4:
                            pe.wait_ge(turn_read, T - 3)
                        for i in range(HALVES):
                            mm = nc.tensor.transpose(psum[:, T % 4, i * P:(i + 1) * P], attn[:, T, i * P:(i + 1) * P], ident[:])
                        mm.then_inc(turn_full, 1)
                    if T:
                        n = T - 1
                        pe.wait_ge(turn_read, n + 1)
                        if n == 0:
                            pe.wait_ge(proj_in, 32)
                        if n >= 4:
                            pe.wait_ge(proj_read, n - 3)
                        for i in range(HALVES):
                            mm = nc.tensor.matmul(psum[:, 4 + n % 4, 0:H], attn_T[:, n % 4, i, :], w_o[:, i, :],
                                                  start=(i == 0), stop=(i == HALVES - 1))
                        mm.then_inc(proj_full, 1)

            @block.scalar
            def _(act):
                def roots(c):
                    a = slice(c * CT, (c + 1) * CT)
                    act.wait_ge(eps_added, c + 1)
                    nc.scalar.activation(std[:, a], std[:, a], ACT.Sqrt).then_inc(root, 1)

                for T in range(NT):
                    act.wait_ge(turn_full, T + 1)
                    if T >= 4:
                        act.wait_ge(proj_full, T - 3)
                    nc.scalar.copy(attn_T[:, T % 4].rearrange("p i q -> p (i q)"), psum[:, T % 4, 0:H]).then_inc(turn_read, 1)
                    if T % CT == 1 and T > CT:
                        roots(T // CT - 1)
                roots(NCH - 1)

            @block.vector
            def _(dve):
                def shift(c):
                    if c == 0:
                        dve.wait_ge(affine_in, 32)
                    for T in range(c * CT, (c + 1) * CT):
                        dve.wait_ge(scaled, T + 1)
                        dve.tensor_tensor(y[:, T], y[:, T], beta[:], ALU.add).then_inc(shifted, 1)

                for c in range(NCH):
                    a = slice(c * CT, (c + 1) * CT)
                    for T in range(c * CT, (c + 1) * CT):
                        dve.wait_ge(proj_full, T + 1)
                        dve.wait_ge(x_step, T + 1)
                        dve.tensor_tensor(y[:, T], psum[:, 4 + T % 4, 0:H], x_1[:, T], ALU.add).then_inc(proj_read, 1)
                        dve.wait_ge(proj_read, T + 1)
                        dve.bn_stats(stats[:, T], y[:, T]).then_inc(stat_step, 1)
                        dve.wait_ge(stat_step, 2 * T + 1)
                        dve.bn_aggr(mean_var[:, T], stats[:, T]).then_inc(stat_step, 1)
                    dve.wait_ge(stat_step, 2 * (c + 1) * CT)
                    dve.tensor_scalar(std[:, a].unsqueeze(2), mean_var[:, a, 1:2], EPS, None, ALU.add).then_inc(eps_added, 1)
                    if c:
                        shift(c - 1)
                    dve.wait_ge(root, c + 1)
                    dve.reciprocal(std[:, a], std[:, a]).then_inc(inverted, 1)
                    dve.wait_ge(inverted, c + 1)
                    for T in range(c * CT, (c + 1) * CT):
                        dve.tensor_scalar(y[:, T], y[:, T], mean_var[:, T, 0:1], std[:, T:T + 1], ALU.subtract, ALU.mult)\
                           .then_inc(normed, 1)
                shift(NCH - 1)


def build(nc, t, out):
    dram = lambda name, shape, dt: nc.dram_tensor(name, shape, dt, kind="Internal").ap()
    scratch = {
        "kp0": dram("kp0", (B, P, HALVES, 3, K0), BF16),
        "qp0": dram("qp0", (B, P, HALVES, 3, SQ), BF16),
        "kp1": dram("kp1", (B, KV1, 3, K1), BF16),
        "qp1": dram("qp1", (HALVES, P, 3, B * SQ), BF16),
        "v0": dram("v0", (B, P, NKB0, H), F32),
        "v1": dram("v1", (B, P, NKB1, KV1), F32),
        "bias0": dram("bias0_rows", (B, K0), BF16),
        "bias1": dram("bias1_row", (1, K1), BF16),
        "attn0": dram("attn0", (B, P, QB, H), F32),
        "attn1": dram("attn1", (B, P, QB, H), F32),
        "x1": dram("x1", (B, P, QB, H), F32),
        "flag0": dram("flag0", (1, 1), I32),
        "flag1": dram("flag1", (1, 1), I32),
    }
    project_inputs(nc, t, scratch)
    attention(nc, t, scratch, 0)
    middle(nc, t, scratch)
    attention(nc, t, scratch, 1)
    finish(nc, t, scratch, out)


def kernel(**inputs):
    import numpy as np
    import concourse.bacc as bacc
    from concourse.bass_utils import run_bass_kernel_spmd

    a = {name: np.asarray(v) for name, v in inputs.items()}
    kw = a["L0_xattn_kv_w"].reshape(H, H, 2)
    kb = a["L0_xattn_kv_b"].reshape(H, 2)
    column = lambda v: v.reshape(-1, P).T
    laid = {
        "x": a["x"], "xT": a["x"].transpose(0, 2, 1), "ctxT": a["ctx_2048"].transpose(0, 2, 1),
        "mask0": a["mask_BxS2_ik0"], "mask1": a["mask_Bx1xSxS2_ff0"][:, 0], "mask1T": a["mask_Bx1xSxS2_ff0"][:, 0].transpose(0, 2, 1),
        "qw0": a["L0_xattn_q_w"], "qb0": column(a["L0_xattn_q_b"]), "kw0": kw[:, :, 0], "vw0": kw[:, :, 1],
        "kb0": column(kb[:, 0]), "vb0": kb[:, 1], "ow0": a["L0_xattn_out_w"], "ob0": a["L0_xattn_out_b"],
        "nw": a["L0_xattn_postnorm_w"], "w1": a["L0_xattn_mlp_w1"], "b1": column(a["L0_xattn_mlp_b1"]),
        "w2": a["L0_xattn_mlp_w2"], "b2": a["L0_xattn_mlp_b2"],
        "qw1": a["L1_xattn_Wq"], "qb1": column(a["L1_xattn_bq"]), "kw1": a["L1_xattn_Wk"], "kb1": a["L1_xattn_bk"][:, None],
        "vw1": a["L1_xattn_Wv"], "vb1": a["L1_xattn_bv"], "ow1": a["L1_xattn_Wo"], "ob1": a["L1_xattn_bo"],
        "gamma": a["L1_xattn_gamma"], "beta": a["L1_xattn_beta"],
    }
    nc = bacc.Bacc("TRN2", target_bir_lowering=False, num_devices=1)
    arrays, t = {}, {}
    for name, v in laid.items():
        arrays[f"in_{name}"] = np.ascontiguousarray(v)
        t[name] = nc.dram_tensor(f"in_{name}", v.shape, mybir.dt.from_np(v.dtype), kind="ExternalInput").ap()
    out = nc.dram_tensor("out_0", (B, SQ, H), F32, kind="ExternalOutput").ap()
    build(nc, t, out)
    r = run_bass_kernel_spmd(nc, [arrays], core_ids=[0])
    return r.results[0]["out_0"]
```
